# Optimizing a Trainium2 kernel written in Bass

```python
import numpy as np
import jax
import jax.numpy as jnp

def _softmax(x, axis=-1):
    return jax.nn.softmax(x, axis=axis)

def _gelu(x):
    return jax.nn.gelu(x, approximate=True)

def _silu(x):
    return jax.nn.silu(x)

def _sigmoid(x):
    return jax.nn.sigmoid(x)

def _layernorm(x, axis=-1, eps=1e-05):
    m = jnp.mean(x, axis=axis, keepdims=True)
    v = jnp.var(x, axis=axis, keepdims=True)
    return (x - m) / jnp.sqrt(v + eps)

def _scatter_add(tgt, idx, src, axis=0):
    return tgt.at[idx].add(src)

def _segment_sum(src, seg, n):
    return jax.ops.segment_sum(src, seg, n)
kernel_name = 'mk_conv_attn_hybrid_d2_conv_nchw512_r2_9337fd'

def setup_inputs(seed: int=0):
    np.random.seed(seed)
    _w = jnp.asarray

    def _rec_inputs():
        import jax
        import jax.numpy as jnp
        _gk = jax.random.key(seed)
        x = 7.22e-05 + 1 * jax.random.normal(jax.random.fold_in(_gk, 1), (4, 256, 32, 32), jnp.float32)
        return x
    x = _rec_inputs()

    def _L0_conv_setup():
        import jax, jax.numpy as jnp
        import numpy as np
        NUM_GROUPS = 32
        EPS = 1e-05

        def _group_norm(x, weight, bias):
            b, c, h, w = x.shape
            xg = x.reshape(b, NUM_GROUPS, c // NUM_GROUPS, h, w)
            mean = jnp.mean(xg, axis=(2, 3, 4), keepdims=True)
            var = jnp.var(xg, axis=(2, 3, 4), keepdims=True)
            xg = (xg - mean) * jax.lax.rsqrt(var + EPS)
            xn = xg.reshape(b, c, h, w)
            return xn * weight[None, :, None, None] + bias[None, :, None, None]
        key = jax.random.key(seed)
        ks = jax.random.split(key, 4)
        C = 256
        x = jax.random.normal(ks[0], (4, C, 32, 32), dtype=jnp.float32)
        gn_weight = jnp.ones((C,), jnp.float32)
        gn_bias = jnp.zeros((C,), jnp.float32)
        qkv_w = jax.random.normal(ks[1], (3 * C, C), dtype=jnp.float32) / np.sqrt(C)
        qkv_b = jnp.zeros((3 * C,), jnp.float32)
        out_w = jax.random.normal(ks[2], (C, C), dtype=jnp.float32) / np.sqrt(C)
        out_b = jnp.zeros((C,), jnp.float32)
        return {'x': x, 'gn_weight': gn_weight, 'gn_bias': gn_bias, 'qkv_w': qkv_w, 'qkv_b': qkv_b, 'out_w': out_w, 'out_b': out_b}
    _L0_conv_all = _L0_conv_setup()
    _L0_conv_in = {k: v for k, v in _L0_conv_all.items() if k in ('gn_weight', 'gn_bias', 'qkv_w', 'qkv_b', 'out_w', 'out_b')}
    del _L0_conv_all

    def _L1_attn_setup():
        import jax, jax.numpy as jnp
        import numpy as np
        D = 256

        def _resmlp(x, W1, W2):
            return x + jax.nn.silu(x @ W1) @ W2
        key = jax.random.key(seed)
        ks = jax.random.split(key, 12)
        s = 1.0 / np.sqrt(D)
        mk = lambda k: jax.random.normal(k, (D, D), dtype=jnp.float32) * s
        return {'x': jax.random.normal(ks[0], (4, 2048, D), dtype=jnp.float32), 'qW1': mk(ks[1]), 'qW2': mk(ks[2]), 'kW1': mk(ks[3]), 'kW2': mk(ks[4]), 'vW1': mk(ks[5]), 'vW2': mk(ks[6]), 'aWq': mk(ks[7]), 'aWk': mk(ks[8]), 'aWv': mk(ks[9]), 'Wout': mk(ks[10])}
    _L1_attn_all = _L1_attn_setup()
    _L1_attn_in = {k: v for k, v in _L1_attn_all.items() if k in ('qW1', 'qW2', 'kW1', 'kW2', 'vW1', 'vW2', 'aWq', 'aWk', 'aWv', 'Wout')}
    del _L1_attn_all

    def _L1_ffn_setup():
        import jax, jax.numpy as jnp
        import numpy as np
        NUM_EXPERTS = 8
        TOP_K = 2
        LN_EPS = 1e-05

        def _layernorm(x, g, b):
            mu = jnp.mean(x, axis=-1, keepdims=True)
            var = jnp.mean(jnp.square(x - mu), axis=-1, keepdims=True)
            return (x - mu) * jax.lax.rsqrt(var + LN_EPS) * g + b
        key = jax.random.key(seed)
        ks = jax.random.split(key, 8)
        B, S, D, F, E = (8, 2048, 256, 1024, NUM_EXPERTS)
        return {'x': jax.random.normal(ks[0], (B, S, D), dtype=jnp.float32), 'gate_w': jax.random.normal(ks[1], (D, E), dtype=jnp.float32) * 0.02, 'w1': jax.random.normal(ks[2], (E, D, F), dtype=jnp.float32) * 0.02, 'b1': jnp.zeros((E, F), dtype=jnp.float32), 'w2': jax.random.normal(ks[3], (E, F, D), dtype=jnp.float32) * 0.02, 'b2': jnp.zeros((E, D), dtype=jnp.float32), 'ln_g': jnp.ones((D,), dtype=jnp.float32), 'ln_b': jnp.zeros((D,), dtype=jnp.float32)}
    _L1_ffn_all = _L1_ffn_setup()
    _L1_ffn_in = {k: v for k, v in _L1_ffn_all.items() if k in ('gate_w', 'w1', 'b1', 'w2', 'b2', 'ln_g', 'ln_b')}
    del _L1_ffn_all
    return {'x': x, 'L0_conv_gn_weight': _L0_conv_in['gn_weight'], 'L0_conv_gn_bias': _L0_conv_in['gn_bias'], 'L0_conv_qkv_w': _L0_conv_in['qkv_w'], 'L0_conv_qkv_b': _L0_conv_in['qkv_b'], 'L0_conv_out_w': _L0_conv_in['out_w'], 'L0_conv_out_b': _L0_conv_in['out_b'], 'L1_attn_qW1': _L1_attn_in['qW1'], 'L1_attn_qW2': _L1_attn_in['qW2'], 'L1_attn_kW1': _L1_attn_in['kW1'], 'L1_attn_kW2': _L1_attn_in['kW2'], 'L1_attn_vW1': _L1_attn_in['vW1'], 'L1_attn_vW2': _L1_attn_in['vW2'], 'L1_attn_aWq': _L1_attn_in['aWq'], 'L1_attn_aWk': _L1_attn_in['aWk'], 'L1_attn_aWv': _L1_attn_in['aWv'], 'L1_attn_Wout': _L1_attn_in['Wout'], 'L1_ffn_gate_w': _L1_ffn_in['gate_w'], 'L1_ffn_w1': _L1_ffn_in['w1'], 'L1_ffn_b1': _L1_ffn_in['b1'], 'L1_ffn_w2': _L1_ffn_in['w2'], 'L1_ffn_b2': _L1_ffn_in['b2'], 'L1_ffn_ln_g': _L1_ffn_in['ln_g'], 'L1_ffn_ln_b': _L1_ffn_in['ln_b']}

def reference(x, L0_conv_gn_weight, L0_conv_gn_bias, L0_conv_qkv_w, L0_conv_qkv_b, L0_conv_out_w, L0_conv_out_b, L1_attn_qW1, L1_attn_qW2, L1_attn_kW1, L1_attn_kW2, L1_attn_vW1, L1_attn_vW2, L1_attn_aWq, L1_attn_aWk, L1_attn_aWv, L1_attn_Wout, L1_ffn_gate_w, L1_ffn_w1, L1_ffn_b1, L1_ffn_w2, L1_ffn_b2, L1_ffn_ln_g, L1_ffn_ln_b):
    import jax
    import jax.numpy as jnp

    def _L0_conv_ref(x, gn_weight, gn_bias, qkv_w, qkv_b, out_w, out_b):
        import jax, jax.numpy as jnp
        import numpy as np
        NUM_GROUPS = 32
        EPS = 1e-05

        def _group_norm(x, weight, bias):
            b, c, h, w = x.shape
            xg = x.reshape(b, NUM_GROUPS, c // NUM_GROUPS, h, w)
            mean = jnp.mean(xg, axis=(2, 3, 4), keepdims=True)
            var = jnp.var(xg, axis=(2, 3, 4), keepdims=True)
            xg = (xg - mean) * jax.lax.rsqrt(var + EPS)
            xn = xg.reshape(b, c, h, w)
            return xn * weight[None, :, None, None] + bias[None, :, None, None]
        b, c, h, w = x.shape
        xn = _group_norm(x, gn_weight, gn_bias)
        qkv = jnp.einsum('bchw,oc->bohw', xn, qkv_w) + qkv_b[None, :, None, None]
        q, k, v = jnp.split(qkv, 3, axis=1)
        q = q.transpose(0, 2, 3, 1).reshape(b, h * w, c)
        k = k.reshape(b, c, h * w)
        v = v.transpose(0, 2, 3, 1).reshape(b, h * w, c)
        scores = jnp.einsum('bic,bcj->bij', q, k) * c ** (-0.5)
        attn = jax.nn.softmax(scores, axis=-1)
        out = jnp.einsum('bij,bjc->bic', attn, v)
        out = out.reshape(b, h, w, c).transpose(0, 3, 1, 2)
        out = jnp.einsum('bchw,oc->bohw', out, out_w) + out_b[None, :, None, None]
        return out + xn

    def _L1_attn_ref(x, qW1, qW2, kW1, kW2, vW1, vW2, aWq, aWk, aWv, Wout):
        import jax, jax.numpy as jnp
        import numpy as np
        D = 256

        def _resmlp(x, W1, W2):
            return x + jax.nn.silu(x @ W1) @ W2
        q = _resmlp(x, qW1, qW2) @ aWq
        k = _resmlp(x, kW1, kW2) @ aWk
        v = _resmlp(x, vW1, vW2) @ aWv
        attn = jnp.einsum('bqd,bkd->bqk', q, k)
        attn = jax.nn.softmax(attn, axis=1)
        out = jnp.einsum('bqk,bkd->bqd', attn, v)
        return out @ Wout

    def _L1_ffn_ref(x, gate_w, w1, b1, w2, b2, ln_g, ln_b):
        import jax, jax.numpy as jnp
        import numpy as np
        NUM_EXPERTS = 8
        TOP_K = 2
        LN_EPS = 1e-05

        def _layernorm(x, g, b):
            mu = jnp.mean(x, axis=-1, keepdims=True)
            var = jnp.mean(jnp.square(x - mu), axis=-1, keepdims=True)
            return (x - mu) * jax.lax.rsqrt(var + LN_EPS) * g + b
        B, S, D = x.shape
        E = gate_w.shape[1]
        x_norm = _layernorm(x, ln_g, ln_b)
        xf = x_norm.reshape(B * S, D)
        logits = xf @ gate_w
        probs = jax.nn.softmax(logits, axis=-1)
        dispatch_w, expert_idx = jax.lax.top_k(probs, TOP_K)
        combine = jnp.sum(jax.nn.one_hot(expert_idx, E, dtype=xf.dtype) * dispatch_w[..., None], axis=1)
        out = jnp.zeros_like(xf)
        for e in range(E):
            h = jax.nn.gelu(xf @ w1[e] + b1[e], approximate=False)
            y = h @ w2[e] + b2[e]
            out = out + combine[:, e:e + 1] * y
        return x + out.reshape(B, S, D)

    def _gn(v, G=32, eps=1e-05):
        B_, C_, H_, W_ = v.shape
        g = v.reshape(B_, G, C_ // G, H_, W_)
        m = jnp.mean(g, axis=(2, 3, 4), keepdims=True)
        s = jnp.var(g, axis=(2, 3, 4), keepdims=True)
        return ((g - m) / jnp.sqrt(s + eps)).reshape(v.shape)

    def _ln_c(v, eps=1e-06):
        m = jnp.mean(v, axis=1, keepdims=True)
        s = jnp.var(v, axis=1, keepdims=True)
        return (v - m) / jnp.sqrt(s + eps)

    def _ln_t(v, eps=1e-05):
        m = jnp.mean(v, axis=-1, keepdims=True)
        s = jnp.var(v, axis=-1, keepdims=True)
        return (v - m) / jnp.sqrt(s + eps)

    def _to_tokens(v):
        B_, C_, H_, W_ = v.shape
        return v.reshape(B_, C_, H_ * W_).transpose(0, 2, 1)

    def _from_tokens(t, like):
        B_, C_, H_, W_ = like.shape
        return t.transpose(0, 2, 1).reshape(B_, C_, H_, W_)
    x = _L0_conv_ref(x, L0_conv_gn_weight, L0_conv_gn_bias, L0_conv_qkv_w, L0_conv_qkv_b, L0_conv_out_w, L0_conv_out_b)
    t = _to_tokens(x)
    t = t + _L1_attn_ref(_ln_t(t), L1_attn_qW1, L1_attn_qW2, L1_attn_kW1, L1_attn_kW2, L1_attn_vW1, L1_attn_vW2, L1_attn_aWq, L1_attn_aWk, L1_attn_aWv, L1_attn_Wout)
    t = t + _L1_ffn_ref(_ln_t(t), L1_ffn_gate_w, L1_ffn_w1, L1_ffn_b1, L1_ffn_w2, L1_ffn_b2, L1_ffn_ln_g, L1_ffn_ln_b)
    x = _from_tokens(t, x)
    return x

_drawn_inputs = setup_inputs


def setup_inputs(seed=0):
    import zlib

    import numpy as np

    out = dict(_drawn_inputs(seed))
    spreads = {'L0_conv_gn_weight': (1.0, 0.2),
     'L0_conv_gn_bias': (0.0, 0.1),
     'L0_conv_qkv_b': (0.0, 0.1),
     'L0_conv_out_b': (0.0, 0.1),
     'L1_ffn_b1': (0.0, 0.8),
     'L1_ffn_b2': (0.0, 0.787),
     'L1_ffn_ln_g': (1.0, 0.6),
     'L1_ffn_ln_b': (0.0, 0.8)}
    factors = {'L1_ffn_gate_w': 4.202, 'L1_ffn_w1': 5.065, 'L1_ffn_w2': 4.727}
    for name, (base, spread) in spreads.items():
        noise = np.random.default_rng([zlib.crc32(name.encode()), seed]).standard_normal(out[name].shape)
        drawn = base * np.exp(spread * noise) if base else spread * noise
        out[name] = jnp.asarray(drawn.astype(out[name].dtype))
    for name, factor in factors.items():
        out[name] = (out[name] * factor).astype(out[name].dtype)
    return out
```

```python
from contextlib import ExitStack

import concourse.bass as bass
from concourse import mybir

P = 128
ALU = mybir.AluOpType
ACT = mybir.ActivationFunctionType
AXX = mybir.AxisListType.X
F32 = mybir.dt.float32
F32R = mybir.dt.float32r
I32 = mybir.dt.int32

PASSES = ((0, 0), (0, 1), (1, 0))

WQ, WK, Q1, K1, V1, AQ, AK, VO, QA, KA, VA, VB = range(12)
DIRECT = 7


def at(turn, per_turn, n):
    return turn * per_turn + n


def hybrid_block_kernel(nc, x, qT, kT, v_w, oT, qk_b, v_b, out_b, gn, W1, W2T, a_qk, a_vT, Wout,
                        gate_w, w1, b1, w2, b2, ln_g, ln_b, out):
    B, C, T = x.shape
    KC = C // P
    NT = T // P
    HALF = 512
    NH = T // HALF
    TOK = B * T
    TILES = TOK // P
    E = gate_w.shape[1]
    FF = w1.shape[2]
    FC = FF // P
    GROUP = C // 32
    STEP = 256
    SUB = STEP // P
    STEPS = TOK * 2 // STEP + E
    COLS = STEPS * SUB
    GN_EPS = LN_EPS = 1e-5
    SKIP = 2 * TOK
    assert KC == 2 and STEPS % 2 == 0 and NT == 8 and NH == 2 and TILES * E == 256

    x_d = x.rearrange("b (k p) t -> b p k t", p=P)
    out_d = out.rearrange("b (k p) t -> b p k t", p=P)
    acc_d = nc.dram_tensor("acc_rows", (TOK, C), F32, kind="Internal").ap()
    xf_d = nc.dram_tensor("xf_rows", (TOK, C), F32, kind="Internal").ap()
    acc_t = acc_d.rearrange("(t p) c -> p t c", p=P)
    xf_t = xf_d.rearrange("(t p) c -> p t c", p=P)
    w1_d = w1.rearrange("e (k p) f -> e p k f", p=P)
    w2_d = w2.rearrange("e (f p) d -> e p f d", p=P)

    ctx = ExitStack()
    with ctx:
        def psum(name, cols):
            return ctx.enter_context(nc.psum_tensor(name, [P, cols], F32))

        def sem(name):
            return ctx.enter_context(nc.semaphore(name))

        def sb(name, shape, dt=F32, scope=ctx):
            return scope.enter_context(nc.sbuf_tensor(name, shape, dt))

        ps = psum("ps", 8 * 512)

        def bank(n, cols=512, count=1):
            return ps[:, n * 512:(n - 1 + count) * 512 + cols]

        ident = sb("ident", [P, P])
        before = sb("before", [P, P])
        ones = sb("ones", [P, P])
        same_group = sb("same_group", [P, P])
        iota = sb("iota", [P, P])
        iota_i = sb("iota_i", [P, P], I32)
        minus_half = sb("minus_half", [P, 8])
        logits = sb("logits", [P, TILES, E])

        batch_scope = ExitStack()

        def bs(name, shape, dt=F32):
            return sb(name, shape, dt, batch_scope)

        wh = bs("wh", [P, 12, KC, C], F32R)
        wl = bs("wl", [P, 12, KC, C], F32R)
        qk_bias = bs("qk_bias", [P, 4])
        gn_aff = bs("gn_aff", [P, 4])
        o_row = bs("o_row", [P, C])
        g_row = bs("g_row", [P, C])
        b_row = bs("b_row", [P, C])
        gate_sb = bs("gate_sb", [P, KC, E])
        xn = bs("xn", [P, KC, T])
        xs = [bs(f"xs{i}", [P, KC, T], F32R) for i in range(2)]
        qs = [bs(f"qs{i}", [P, KC, T], F32R) for i in range(2)]
        ks = [bs(f"ks{i}", [P, KC, T], F32R) for i in range(2)]
        tok = bs("tok", [P, NT, C])
        prob = bs("prob", [P, 2, T])
        pr = [bs(f"pr{i}", [P, 2, T], F32R) for i in range(2)]
        u32 = bs("u32", [P, 2, HALF])
        x_row = bs("x_row", [P, 2, C])
        gn_bn = bs("gn_bn", [P, KC, 2, 6])
        gn_mv = bs("gn_mv", [P, KC, 2])
        gn_avg = bs("gn_avg", [P, KC, 2])
        gn_d = bs("gn_d", [P, KC])
        gn_d2 = bs("gn_d2", [P, KC])
        gn_r = bs("gn_r", [P, KC])
        gn_var = bs("gn_var", [P, KC])
        gn_s = bs("gn_s", [P, KC])
        gn_t = bs("gn_t", [P, KC])
        neg_max = bs("neg_max", [P, NT])
        row_sum = bs("row_sum", [P, NT])
        row_inv = bs("row_inv", [P, NT])
        ln_bn = bs("ln_bn", [P, NT, 6])
        ln_mv = bs("ln_mv", [P, NT, 2])
        ln_eps = bs("ln_eps", [P, NT])
        ln_r = bs("ln_r", [P, NT])
        spare = bs("spare", [P, 1])
        here = ExitStack()
        raw = sb("raw", [P, 14, KC * C], F32, here)
        raw_vo = sb("raw_vo", [P, KC * C], F32, here)
        vb_wide = sb("vb_wide", [P, KC, P], F32, here)
        vb_col = sb("vb_col", [P, KC], F32, here)
        here.close()
        us = [[sb(f"us{n}{i}", [P, KC, T], F32R, here) for i in range(2)] for n in range(2)]
        here.close()
        x2 = sb("x2", [P, NT, C], F32, here)
        xf = sb("xf", [P, NT, C], F32, here)
        xfT = sb("xfT", [P, KC, T], F32, here)
        tn = sb("tn", [P, NT, C], F32, here)
        here.close()
        hold_r1 = sb("hold_r1", [P, 8192], F32, batch_scope)
        vs = [sb(f"vs{i}", [P, NT, C], F32R, here) for i in range(2)]
        here.close()
        v32 = sb("v32", [P, NT, C], F32, here)
        vk = [sb(f"vk{i}", [P, 2, C], F32R, here) for i in range(2)]
        here.close()
        hold_r2 = sb("hold_r2", [P, 4096], F32, batch_scope)
        batch_scope.close()

        route_scope = ExitStack()

        def rs(name, shape, dt=F32):
            return sb(name, shape, dt, route_scope)

        expert_of = ctx.enter_context(nc.sbuf_tensor("expert_of", [P, STEPS], I32))
        fresh = ctx.enter_context(nc.sbuf_tensor("fresh", [P, STEPS], I32))
        gather_at = sb("gather_at", [P, COLS], I32)
        scatter_at = sb("scatter_at", [P, COLS], I32)
        slot_w = sb("slot_w", [P, COLS])
        top8 = rs("top8", [P, TILES, 8])
        top_i = rs("top_i", [P, TILES, 8], mybir.dt.uint32)
        top_f = rs("top_f", [P, TILES, 8])
        exps = rs("exps", [P, TILES, E])
        zsum = rs("zsum", [P, TILES])
        zinv = rs("zinv", [P, TILES])
        is_top = [rs(f"is_top{k}", [P, TILES, E]) for k in range(2)]
        either = rs("either", [P, TILES, E])
        scratch = rs("scratch", [P, TILES, E])
        top_w = [rs(f"top_w{k}", [P, TILES]) for k in range(2)]
        prefix = [rs(f"prefix{i}", [P, TILES, E]) for i in range(2)]
        slot_all = rs("slot_all", [P, TILES, E])
        cnt_f = rs("cnt_f", [P, E])
        cnt_i = rs("cnt_i", [P, E], I32)
        cnt_s = rs("cnt_s", [P, E], I32)
        need = rs("need", [P, E])
        ends_t = [rs(f"ends{i}", [P, E]) for i in range(2)]
        base = rs("base", [P, E])
        past = rs("past", [P, STEPS, E])
        expert_f = rs("expert_f", [P, STEPS])
        slot_f = [rs(f"slot_f{k}", [P, TILES]) for k in range(2)]
        slot_i = [rs(f"slot_i{k}", [P, TILES], I32) for k in range(2)]
        lo_i = [rs(f"lo_i{k}", [P, TILES], I32) for k in range(2)]
        hi_i = [rs(f"hi_i{k}", [P, TILES], I32) for k in range(2)]
        lo_f = [rs(f"lo_f{k}", [P, TILES]) for k in range(2)]
        hi_f = [rs(f"hi_f{k}", [P, TILES]) for k in range(2)]
        number_i = rs("number_i", [P, TILES], I32)
        number = rs("number", [P, TILES])
        pick_lo = rs("pick_lo", [P, 4, P])
        pick_hi = rs("pick_hi", [P, 4, 2, COLS])
        at_f = rs("at_f", [P, COLS])
        at_g = rs("at_g", [P, COLS])
        at_s = rs("at_s", [P, COLS])
        at_m = rs("at_m", [P, COLS])
        route_scope.close()

        ex_scope = ExitStack()

        def es(name, shape, dt=F32):
            return sb(name, shape, dt, ex_scope)

        w1r = es("w1r", [P, 2, KC * FF])
        w2r = es("w2r", [P, 2, FC * C])
        b1t = es("b1t", [P, 2, FC])
        b2t = es("b2t", [P, 2, C])
        w1s = [[es(f"w1s{n}{i}", [P, KC, FF], F32R) for i in range(2)] for n in range(2)]
        w2s = [[es(f"w2s{n}{i}", [P, FC, C], F32R) for i in range(2)] for n in range(2)]
        xg = es("xg", [P, 2, SUB, C])
        xt = [[es(f"xt{n}{i}", [P, KC, STEP], F32R) for i in range(2)] for n in range(2)]
        h32 = es("h32", [P, 4, STEP])
        hs = [es(f"hs{i}", [P, FC, STEP], F32R) for i in range(2)]
        y_b = es("y_b", [P, SUB, C])
        y_w = es("y_w", [P, 2, SUB, C])
        now_g = es("now_g", [P, 2, SUB], I32)
        now_s = es("now_s", [P, 2, SUB], I32)
        ex_scope.close()
        rows = sb("rows", [P, 2, 4, C], F32, ex_scope)
        cols_out = sb("cols_out", [P, 2, KC, HALF], F32, ex_scope)
        ex_scope.close()

        S = {}

        def signal(name):
            S[name] = sem(name)
            return S[name]

        pool_held = signal("pool_held")
        sp_held = signal("sp_held")
        c_made = signal("c_made")
        w_in = signal("w_in")
        w_fold = signal("w_fold")
        w_hi = signal("w_hi")
        w_lo = signal("w_lo")
        vo_ready = signal("vo_ready")
        vb_ready = signal("vb_ready")
        x_in = signal("x_in")
        gn_stat = signal("gn_stat")
        gn_mm = signal("gn_mm")
        pow_in = signal("pow_in")
        pow_out = signal("pow_out")
        xn_done = signal("xn_done")
        xn_hi = signal("xn_hi")
        xn_lo = signal("xn_lo")
        pj_mm = signal("pj_mm")
        pj_hi = signal("pj_hi")
        pj_lo = signal("pj_lo")
        s_mm = signal("s_mm")
        s_max = signal("s_max")
        p_exp = signal("p_exp")
        pt_mm = signal("pt_mm")
        pt_hi = signal("pt_hi")
        pt_lo = signal("pt_lo")
        av_mm = signal("av_mm")
        t_done = signal("t_done")
        tn_tok = signal("tn_tok")
        tn_mm = signal("tn_mm")
        tn_hi = signal("tn_hi")
        tn_lo = signal("tn_lo")
        r_mm = signal("r_mm")
        r_act = signal("r_act")
        r_dve = signal("r_dve")
        s2_mm = signal("s2_mm")
        s2_max = signal("s2_max")
        p2_exp = signal("p2_exp")
        p2_hi = signal("p2_hi")
        p2_lo = signal("p2_lo")
        v2_done = signal("v2_done")
        av2_mm = signal("av2_mm")
        r_ready = signal("r_ready")
        xf_ready = signal("xf_ready")
        stored = signal("stored")
        xf_mm = signal("xf_mm")
        xf_col = signal("xf_col")
        g_mm = signal("g_mm")
        own = signal("own")
        pe_end = signal("pe_end")
        act_end = signal("act_end")
        dve_end = signal("dve_end")
        pool_end = signal("pool_end")
        sp_end = signal("sp_end")
        top_done = signal("top_done")
        exp_done = signal("exp_done")
        rank_mm = signal("rank_mm")
        pick_done = signal("pick_done")
        pick_mm = signal("pick_mm")
        num_done = signal("num_done")
        tables = signal("tables")
        own_r = signal("own_r")
        w1_in = [signal(f"w1_in{n}") for n in range(2)]
        w2_in = [signal(f"w2_in{n}") for n in range(2)]
        b_in = [signal(f"b_in{n}") for n in range(2)]
        ws_act = signal("ws_act")
        ws_dve = signal("ws_dve")
        ws_pool = signal("ws_pool")
        g_in = [signal(f"g_in{n}") for n in range(2)]
        idx_g = signal("idx_g")
        idx_s = signal("idx_s")
        xt_mm = signal("xt_mm")
        xt_hi = signal("xt_hi")
        xt_lo = signal("xt_lo")
        h_mm = signal("h_mm")
        h_act = signal("h_act")
        h_hi = signal("h_hi")
        h_lo = signal("h_lo")
        y_mm = signal("y_mm")
        y_dve = signal("y_dve")
        y_act = signal("y_act")
        added = signal("added")
        y_free = signal("y_free")
        r_in = [signal(f"r_in{n}") for n in range(2)]
        o_mm = signal("o_mm")
        o_act = signal("o_act")
        o_dve = signal("o_dve")
        o_out = [signal(f"o_out{n}") for n in range(2)]

        R = [("u", 0, 0, 0), ("u", 0, 0, 1), ("u", 1, 0, 0), ("u", 1, 0, 1),
             ("u", 0, 1, 0), ("u", 0, 1, 1), ("u", 1, 1, 0), ("u", 1, 1, 1)]
        R += [("p", 0, n, m) for n in range(NH) for m in range(KC)]
        R += [("u", 2, n, m) for n in range(NH) for m in range(KC)]
        R += [("p", 1, n, m) for n in range(NH) for m in range(KC)]
        R += [("v", 2, j, 0) for j in range(NT // 2)]
        RG = len(R)
        R_DVE = [sum(k != "v" for k, *_ in R[:g + 1]) for g in range(RG)]
        RD = R_DVE[-1]
        R_BANKS = (4, 5, 6, 7)

        block = ctx.enter_context(nc.Block())

        POWS = 1 + NT + 2
        PJ = 12

        def ends(eng, b, semaphores):
            for s in semaphores:
                eng.wait_ge(s, at(b, 1, 1))

        RAW_IN = 14 * 16
        ROW_IN = 9 * 16

        @block.sync
        def _(sp):
            for n, w in enumerate([qT, kT, W1[0], W1[1], W1[2], a_qk[0], a_qk[1],
                                   v_w, oT, W2T[0], W2T[1], W2T[2], a_vT, Wout]):
                sp.dma_start(raw[:, n, :].rearrange("p (k c) -> p k c", k=KC),
                             w.rearrange("(k p) c -> p k c", p=P)).then_inc(w_in, 16)
                if n == 1:
                    sp.dma_start(xn[:, :, :], x_d[0]).then_inc(x_in, 16)
            sp.dma_start(qk_bias[:, :], qk_b).then_inc(w_in, 16)
            sp.dma_start(gn_aff[:, :], gn).then_inc(w_in, 16)
            sp.dma_start(vb_col[:, :], v_b).then_inc(w_in, 16)
            with nc.allow_non_contiguous_dma(reason="rows read by every partition"):
                sp.dma_start(o_row[:, :], out_b.to_broadcast((P, C))).then_inc(w_in, 16)
                sp.dma_start(g_row[:, :], ln_g.to_broadcast((P, C))).then_inc(w_in, 16)
                sp.dma_start(b_row[:, :], ln_b.to_broadcast((P, C))).then_inc(w_in, 16)
            for k in range(KC):
                sp.dma_start(gate_sb[:, k, :], gate_w[k * P:(k + 1) * P, :]).then_inc(w_in, 16)
            sp.sem_inc(sp_end, 1)

            def image(b, last):
                sp.wait_ge(r_ready, at(b, 1, 1))
                sp.sem_inc(sp_held, 1)
                sp.dma_start(acc_t[:, bass.ds(b * NT, NT), :], tok[:, :, :]).then_inc(stored, 16)
                sp.wait_ge(xf_ready, at(b, 1, 1))
                sp.sem_inc(sp_held, 1)
                sp.dma_start(xf_t[:, bass.ds(b * NT, NT), :], xf[:, :, :]).then_inc(stored, 16)
                if not last:
                    sp.dma_start(xn[:, :, :], x_d[b + 1] if isinstance(b, int) else
                                 x_d[bass.ds(b + 1, 1)].rearrange("b p k t -> (b p) k t")
                                 ).then_inc(x_in, 16)
                sp.wait_ge(stored, at(b, 32, 32))
                sp.sem_inc(sp_end, 1)

            with sp.Fori(0, B - 1) as b:
                image(b, False)
            image(B - 1, True)

            sp.wait_ge(tables, 4)
            ends(sp, B, (pe_end, act_end, dve_end, pool_end))

            def expert_load(s, n, u, first):
                if not first:
                    sp.wait_ge(ws_act, at(s, 8, -8))
                    sp.sem_inc(sp_held, 1)
                    sp.wait_ge(ws_dve, at(s, 4, -4))
                    sp.sem_inc(sp_held, 1)
                    sp.wait_ge(ws_pool, at(s, 4, -4))
                    sp.sem_inc(sp_held, 1)
                e = sp.value_load(expert_of[0:1, bass.ds(s, 1)], min_val=0, max_val=E - 1)

                def weights():
                    sp.dma_start(w1r[:, n, :].rearrange("p (k f) -> p k f", k=KC),
                                 w1_d[bass.ds(e, 1)].rearrange("e p k f -> (e p) k f")).then_inc(w1_in[n], 16)
                    sp.dma_start(w2r[:, n, :].rearrange("p (f c) -> p f c", f=FC),
                                 w2_d[bass.ds(e, 1)].rearrange("e p f c -> (e p) f c")).then_inc(w2_in[n], 16)

                if first:
                    weights()
                else:
                    with sp.If(sp.value_load(fresh[0:1, bass.ds(s, 1)], min_val=0, max_val=1) == 1):
                        weights()
                    with sp.Else():
                        sp.wait_ge(w1_in[n], at(u, 16, 0))
                        sp.sem_inc(w1_in[n], 16)
                        sp.wait_ge(w2_in[n], at(u, 16, 0))
                        sp.sem_inc(w2_in[n], 16)
                if not first:
                    sp.wait_ge(h_act, at(s, FC, -FC))
                    sp.sem_inc(sp_held, 1)
                    sp.wait_ge(y_dve, at(s, 1, -1))
                    sp.sem_inc(sp_held, 1)
                sp.dma_start(b1t[:, n, :], b1[bass.ds(e, 1)].rearrange("e p f -> (e p) f")
                             ).then_inc(b_in[n], 16)
                sp.dma_start(b2t[:, n, :], b2[bass.ds(e, 1), :].to_broadcast((P, C))).then_inc(b_in[n], 16)

            expert_load(0, 0, 0, True)
            expert_load(1, 1, 0, True)
            with sp.Fori(1, STEPS // 2) as i:
                for n in range(2):
                    expert_load(i * 2 + n, n, i, False)

            sp.wait_ge(added, STEPS * SUB * 16)
            ends(sp, B + 1, (pe_end, act_end, dve_end))
            G = TILES // 4
            for g in range(2):
                sp.dma_start(rows[:, g % 2, :, :], acc_t[:, 4 * g:4 * g + 4, :]).then_inc(r_in[g % 2], 16)

            def piece(g, n, more):
                sp.wait_ge(o_act, at(g, 1, 1))
                sp.wait_ge(o_dve, at(g, 1, 1))
                b = g // NH
                sp.dma_start(out_d[b, :, :, n * HALF:(n + 1) * HALF],
                             cols_out[:, n, :, :]).then_inc(o_out[n], 16)
                if more:
                    sp.dma_start(rows[:, n, :, :], acc_t[:, bass.ds((g + 2) * 4, 4), :]).then_inc(r_in[n], 16)

            for g in range(G):
                piece(g, g % 2, g + 2 < G)
            for n in range(2):
                sp.wait_ge(o_out[n], G // 2 * 16)

        @block.gpsimd
        def _(pool):
            g = nc.gpsimd
            made = [0]

            def make(ins):
                made[0] += 1
                ins.then_inc(c_made, 1)

            make(g.memset(ident[:, :], 0.0))
            make(g.memset(ones[:, :], 1.0))
            make(g.memset(same_group[:, :], 1.0 / GROUP))
            make(g.memset(minus_half[:, :], -0.5))
            make(g.iota(iota_i[:, :], pattern=[[1, P]], base=0, channel_multiplier=0))
            pool.wait_ge(c_made, made[0])
            make(g.affine_select(out=ident[:, :], in_=ident[:, :], compare_op=ALU.not_equal, fill=1.0,
                                 base=0, pattern=[[-1, P]], channel_multiplier=1))
            make(g.affine_select(out=before[:, :], in_=ones[:, :], compare_op=ALU.is_gt, fill=0.0,
                                 base=0, pattern=[[1, P]], channel_multiplier=-1))
            wide = same_group[:, :].rearrange("p (g c) -> p g c", c=GROUP)
            make(g.affine_select(out=wide, in_=wide, compare_op=ALU.is_ge, fill=0.0,
                                 base=0, pattern=[[-GROUP, P // GROUP], [0, GROUP]], channel_multiplier=1))
            pool.wait_ge(c_made, made[0])
            make(g.affine_select(out=wide, in_=wide, compare_op=ALU.is_ge, fill=0.0, base=GROUP - 1,
                                 pattern=[[GROUP, P // GROUP], [0, GROUP]], channel_multiplier=-1))
            make(g.tensor_copy(iota[:, :], iota_i[:, :]))
            pool.sem_inc(pool_end, 1)
            assert made[0] == CONSTANTS

            def rsqrt(b, n, dst, src):
                pool.wait_ge(pow_in, at(b, POWS, n + 1))
                g.tensor_tensor(dst, src, minus_half[:, 0:src.shape[1]], ALU.pow).then_inc(pow_out, 1)

            with pool.Fori(0, B) as b:
                rsqrt(b, 0, gn_r[:, :], gn_var[:, :])
                for i in range(NT):
                    rsqrt(b, 1 + i, ln_r[:, i:i + 1], ln_eps[:, i:i + 1])
                for i in range(2):
                    rsqrt(b, 1 + NT + i, ln_r[:, :], ln_eps[:, :])
                pool.sem_inc(pool_end, 1)

            ends(pool, B, (pe_end, act_end, dve_end, sp_end))
            g.iota(number_i[:, :], pattern=[[P, TILES]], base=1, channel_multiplier=1).then_inc(num_done, 1)
            pool.wait_ge(num_done, 1)
            g.tensor_copy(number[:, :], number_i[:, :]).then_inc(num_done, 1)
            pool.wait_ge(tables, 4)

            def gather(s, n, first):
                if not first:
                    pool.wait_ge(xt_mm, at(s, 1, -1))
                    pool.sem_inc(pool_held, 1)
                g.tensor_copy(now_g[:, n, :], gather_at[:, bass.ds(s * SUB, SUB)]).then_inc(idx_g, 1)
                pool.wait_ge(idx_g, at(s, 1, 1))
                pool.sem_inc(pool_held, 1)
                for h in range(SUB):
                    g.indirect_dma_start(out=xg[:, n, h, :], out_offset=None, in_=xf_d,
                                         in_offset=bass.IndirectOffsetOnAxis(ap=now_g[:, n, h:h + 1], axis=0),
                                         bounds_check=TOK - 1, oob_is_err=True).then_inc(g_in[n], 16)

            def scatter(s, n, first):
                g.tensor_copy(now_s[:, n, :], scatter_at[:, bass.ds(s * SUB, SUB)]).then_inc(idx_s, 1)
                pool.wait_ge(idx_s, at(s, 1, 1))
                pool.wait_ge(y_act, at(s, 1, 1))
                if not first:
                    pool.wait_ge(added, at(s, SUB * 16, 0))
                pool.sem_inc(y_free, 1)
                for h in range(SUB):
                    g.indirect_dma_start(out=acc_d, out_offset=bass.IndirectOffsetOnAxis(
                        ap=now_s[:, n, h:h + 1], axis=0), in_=y_w[:, n, h, :], in_offset=None,
                        bounds_check=TOK - 1, oob_is_err=False, compute_op=ALU.add).then_inc(added, 16)

            def lo_pieces(s, n, u):
                if isinstance(s, int) and s < 2:
                    split_w2(s, n, u)
                    return
                with pool.If(pool.value_load(fresh[0:1, bass.ds(s, 1)], min_val=0, max_val=1) == 1):
                    split_w2(s, n, u)
                with pool.Else():
                    pool.wait_ge(ws_pool, at(s, 4, 0))
                    pool.sem_inc(ws_pool, 4)

            def split_w2(s, n, u):
                pool.wait_ge(w2_in[n], at(u, 16, 16))
                if not (isinstance(s, int) and s < 2):
                    pool.wait_ge(y_mm, at(s, FC, -FC))
                for f in range(4, 8):
                    pool.wait_ge(ws_act, at(s, 8, f + 1))
                    c = slice((2 * (f - 4)) * C, (2 * (f - 4) + 2) * C)
                    g.tensor_tensor(w2s[n][1][:, :, :].rearrange("p f c -> p (f c)")[:, c], w2r[:, n, c],
                                    w2s[n][0][:, :, :].rearrange("p f c -> p (f c)")[:, c].bitcast(F32),
                                    ALU.subtract).then_inc(ws_pool, 1)

            gather(0, 0, True)
            gather(1, 1, True)
            lo_pieces(0, 0, 0)

            def steps(i, first, last):
                for n in range(2):
                    s = i * 2 + n
                    if not last:
                        gather(s + 2, n, False)
                    if not (first and n == 0):
                        scatter(s - 1, 1 - n, first)
                    if not (last and n == 1):
                        lo_pieces(s + 1, 1 - n, (i if n == 0 else i + 1))

            steps(0, True, False)
            with pool.Fori(1, STEPS // 2 - 1) as i:
                steps(i, False, False)
            steps(STEPS // 2 - 1, False, True)
            scatter(STEPS - 1, 1, False)

        @block.scalar
        def _(act):
            a = nc.scalar
            act.wait_ge(w_in, RAW_IN + ROW_IN - 16)
            flat_h = wh[:, :, :, :].rearrange("p w k c -> p w (k c)")
            a.mul(raw[:, 0, :], raw[:, 0, :], C ** -0.5).then_inc(w_hi, 1)
            a.mul(qk_bias[:, 0:KC], qk_bias[:, 0:KC], C ** -0.5).then_inc(w_hi, 1)
            act.wait_ge(w_hi, 1)
            a.copy(flat_h[:, 0:DIRECT, :], raw[:, 0:DIRECT, :]).then_inc(w_hi, 1)
            for n, w in enumerate((VO, QA, KA, VA)):
                act.wait_ge(w_fold, n + 1)
                if w == VA:
                    a.copy(raw_vo[:, :], bank(n)).then_inc(vo_ready, 1)
                a.copy(flat_h[:, w, :], bank(n)).then_inc(w_hi, 1)
            act.wait_ge(w_fold, 5)
            a.copy(flat_h[:, VB, :], bank(4)).then_inc(w_hi, 1)
            act.sem_inc(act_end, 1)

            def image(b):
                def w(s, per, n):
                    act.wait_ge(s, at(b, per, n))

                ends(act, b, (pe_end, dve_end, sp_end))
                for k in range(KC):
                    w(xn_done, KC, k + 1)
                    a.copy(xs[0][:, k, :], xn[:, k, :]).then_inc(xn_hi, 1)
                for gi in range(PJ):
                    w(pj_mm, PJ, gi + 1)
                    if gi < 8:
                        q, n, m = gi // 4, gi % 4 // 2, gi % 2
                        dst = (qs, ks)[q][0][:, m, n * HALF:(n + 1) * HALF]
                        a.activation(dst, bank(gi % 4), ACT.Identity,
                                     bias=qk_bias[:, 2 * q + m:2 * q + m + 1]).then_inc(pj_hi, 1)
                    else:
                        j = gi - 8
                        a.copy(vs[0][:, 2 * j:2 * j + 2, :].rearrange("p j c -> p (j c)"),
                               bank(gi % 4)).then_inc(pj_hi, 1)

                def exp1(i):
                    w(s_max, NT, i + 1)
                    if i >= 2:
                        w(pt_mm, NT, i - 1)
                    a.activation(prob[:, i % 2, :], bank(2 * (i % 2), count=2), ACT.Exp,
                                 bias=neg_max[:, i:i + 1], accum_out=row_sum[:, i:i + 1]).then_inc(p_exp, 1)

                def hi1(i):
                    w(pt_mm, NT, i + 1)
                    if i >= 1:
                        w(av_mm, NT, i)
                    a.copy(pr[0][:, 0, :], bank(4, count=2)).then_inc(pt_hi, 1)

                def hi_tn(h):
                    w(tn_mm, 2, h + 1)
                    a.copy(xs[0][:, :, h * HALF:(h + 1) * HALF],
                           bank(2 * h, count=2).rearrange("p (k t) -> p k t", k=KC)).then_inc(tn_hi, 1)

                exp1(0)
                exp1(1)
                for i in range(NT):
                    hi1(i)
                    if i + 2 < NT:
                        exp1(i + 2)
                    if i == 6:
                        hi_tn(0)

                n_u = 0
                for gi, (kind, o, n, m) in enumerate(R):
                    if gi == 2:
                        hi_tn(1)
                    w(r_mm, RG, gi + 1)
                    src = bank(R_BANKS[gi % 4])
                    if kind == "u":
                        if n_u >= 2:
                            prior = [j for j in range(gi) if R[j][0] == "u"][-2]
                            w(r_dve, RD, R_DVE[prior])
                        a.activation(u32[:, n_u % 2, :], src, ACT.Silu).then_inc(r_act, 1)
                        n_u += 1
                    elif kind == "p":
                        a.copy((qs, ks)[o][0][:, m, n * HALF:(n + 1) * HALF], src).then_inc(r_act, 1)
                    else:
                        a.copy(v32[:, 2 * n:2 * n + 2, :].rearrange("p j c -> p (j c)"), src).then_inc(r_act, 1)

                def exp2(i):
                    w(s2_max, NT, i + 1)
                    if i >= 2:
                        w(p2_lo, NT, i - 1)
                    a.activation(prob[:, i % 2, :], bank(2 * (i % 2), count=2), ACT.Exp,
                                 bias=neg_max[:, i:i + 1], accum_out=row_sum[:, i:i + 1]).then_inc(p2_exp, 1)

                def hi2(i):
                    w(p2_exp, NT, i + 1)
                    if i >= 2:
                        w(av2_mm, NT, i - 1)
                    a.copy(pr[0][:, i % 2, :], prob[:, i % 2, :]).then_inc(p2_hi, 1)

                for i in range(NT):
                    exp2(i)
                    hi2(i)
                for h in range(2):
                    w(xf_mm, 2, h + 1)
                    a.copy(xfT[:, :, h * HALF:(h + 1) * HALF],
                           bank(2 * h, count=2).rearrange("p (k t) -> p k t", k=KC)).then_inc(xf_col, 1)
                act.sem_inc(act_end, 1)

            with act.Fori(0, B) as b:
                image(b)

            act.wait_ge(top_done, 2)
            a.activation(exps[:, :, :], scratch[:, :, :], ACT.Exp).then_inc(exp_done, 1)

            act.wait_ge(tables, 4)

            def w_piece(s, n, u, f):
                first = isinstance(s, int) and s < 2
                if f < 4:
                    if f == 0:
                        act.wait_ge(w1_in[n], at(u, 16, 16))
                        if not first:
                            act.wait_ge(h_mm, at(s, FC, -FC))
                    dst = w1s[n][0][:, :, :].rearrange("p k f -> p (k f)")
                    src = w1r
                else:
                    if f == 4:
                        act.wait_ge(w2_in[n], at(u, 16, 16))
                        if not first:
                            act.wait_ge(y_mm, at(s, FC, -FC))
                    dst = w2s[n][0][:, :, :].rearrange("p f c -> p (f c)")
                    src = w2r
                c = slice((f % 4) * 512, (f % 4 + 1) * 512)
                a.copy(dst[:, c], src[:, n, c]).then_inc(ws_act, 1)

            def x_hi(s, n):
                act.wait_ge(xt_mm, at(s, 1, 1))
                a.copy(xt[n][0][:, :, :].rearrange("p k t -> p (k t)"), bank(6)).then_inc(xt_hi, 1)

            for f in range(8):
                w_piece(0, 0, 0, f)
            x_hi(0, 0)

            def steps(i, first, last):
                for n in range(2):
                    s = i * 2 + n
                    act.wait_ge(b_in[n], at(i, 32, 32))
                    if last and n == 1:
                        chunks(i, n, first, last, False)
                    elif first and n == 0:
                        chunks(i, n, first, last, True)
                    else:
                        with act.If(act.value_load(fresh[0:1, bass.ds(s + 1, 1)], min_val=0, max_val=1) == 1):
                            chunks(i, n, first, last, True)
                        with act.Else():
                            act.wait_ge(ws_act, at(s, 8, 8))
                            act.sem_inc(ws_act, 8)
                            chunks(i, n, first, last, False)

            def chunks(i, n, first, last, split):
                if True:
                    s = i * 2 + n
                    for f in range(FC):
                        gi = n * FC + f
                        act.wait_ge(h_mm, at(i, 2 * FC, gi + 1))
                        if not (first and gi < 4):
                            act.wait_ge(h_lo, at(i, 2 * FC, gi - 3))
                        a.activation(h32[:, gi % 4, :], bank(gi % 4, STEP), ACT.Gelu,
                                     bias=b1t[:, n, f:f + 1]).then_inc(h_act, 1)
                        if split:
                            w_piece(s + 1, 1 - n, (i if n == 0 else i + 1), f)
                        if f == 4 and not (last and n == 1):
                            x_hi(s + 1, 1 - n)
                        if f == 3 and not (first and n == 0):
                            y_scale(s - 1, 1 - n, first)

            def y_scale(s, n, first):
                act.wait_ge(y_dve, at(s, 1, 1))
                if not first:
                    act.wait_ge(y_free, at(s, 1, 0))
                for h in range(SUB):
                    ins = a.activation(y_w[:, n, h, :], y_b[:, h, :], ACT.Copy,
                                       scale=slot_w[:, bass.ds(s * SUB + h, 1)])
                ins.then_inc(y_act, 1)

            steps(0, True, False)
            with act.Fori(1, STEPS // 2 - 1) as i:
                steps(i, False, False)
            steps(STEPS // 2 - 1, False, True)
            y_scale(STEPS - 1, 1, False)
            act.sem_inc(act_end, 1)

            for gi in range(TILES // 4):
                act.wait_ge(o_mm, gi + 1)
                if gi >= 2:
                    act.wait_ge(o_out[gi % 2], gi // 2 * 16)
                a.copy(cols_out[:, gi % 2, 0, :], bank(2 * (gi % 2))).then_inc(o_act, 1)

        def route(dve, v):
            done = [0]

            def step(ins):
                done[0] += 1
                ins.then_inc(own_r, 1)

            def settle():
                dve.wait_ge(own_r, done[0])

            def wide(a):
                return a.unsqueeze(2).to_broadcast((P, TILES, E))

            for t in range(TILES):
                step(v.max(top8[:, t, :], logits[:, t, :]))
            settle()
            v.tensor_tensor(scratch[:, :, :], logits[:, :, :], wide(top8[:, :, 0]), ALU.subtract).then_inc(top_done, 1)
            for t in range(TILES):
                step(v.max_index(top_i[:, t, :], top8[:, t, :], logits[:, t, :]))
            settle()
            v.tensor_copy(top_f[:, :, :], top_i[:, :, :]).then_inc(top_done, 1)
            dve.wait_ge(top_done, 2)
            experts = iota[:, 0:E].unsqueeze(1).to_broadcast((P, TILES, E))
            for k in range(2):
                step(v.tensor_tensor(is_top[k][:, :, :], wide(top_f[:, :, k]), experts, ALU.is_equal))
            settle()
            v.tensor_tensor(either[:, :, :], is_top[0][:, :, :], is_top[1][:, :, :], ALU.add).then_inc(top_done, 1)
            dve.wait_ge(exp_done, 1)
            step(v.tensor_reduce(zsum[:, :], exps[:, :, :], AXX, ALU.add))
            settle()
            step(v.reciprocal(zinv[:, :], zsum[:, :]))
            for k in range(2):
                settle()
                step(v.tensor_tensor(scratch[:, :, :], exps[:, :, :], is_top[k][:, :, :], ALU.mult))
                settle()
                step(v.tensor_reduce(top_w[k][:, :], scratch[:, :, :], AXX, ALU.add))
                settle()
                step(v.tensor_tensor(top_w[k][:, :], top_w[k][:, :], zinv[:, :], ALU.mult))
            dve.wait_ge(rank_mm, 1)
            tile_n = bank(1, TILES * E).rearrange("p (t e) -> p t e", e=E)
            step(v.memset(prefix[0][:, 0:1, :], 0.0))
            step(v.tensor_copy(prefix[0][:, 1:TILES, :], tile_n[:, 0:TILES - 1, :]))
            src, d = 0, 1
            while d < TILES:
                settle()
                step(v.tensor_copy(prefix[1 - src][:, 0:d, :], prefix[src][:, 0:d, :]))
                step(v.tensor_tensor(prefix[1 - src][:, d:, :], prefix[src][:, d:, :],
                                     prefix[src][:, :TILES - d, :], ALU.add))
                src, d = 1 - src, 2 * d
            settle()
            step(v.tensor_tensor(cnt_f[:, :], prefix[src][:, TILES - 1, :], tile_n[:, TILES - 1, :], ALU.add))
            settle()
            step(v.tensor_scalar(cnt_i[:, :], cnt_f[:, :], float(STEP - 1), None, ALU.add))
            settle()
            shift = STEP.bit_length() - 1
            step(v.tensor_single_scalar(cnt_s[:, :], cnt_i[:, :], shift, ALU.logical_shift_right))
            settle()
            step(v.tensor_copy(need[:, :], cnt_s[:, :]))
            settle()
            step(v.tensor_copy(ends_t[0][:, :], need[:, :]))
            es_, d = 0, 1
            while d < E:
                settle()
                step(v.tensor_copy(ends_t[1 - es_][:, 0:d], ends_t[es_][:, 0:d]))
                step(v.tensor_tensor(ends_t[1 - es_][:, d:], ends_t[es_][:, d:], ends_t[es_][:, :E - d], ALU.add))
                es_, d = 1 - es_, 2 * d
            settle()
            step(v.tensor_tensor(base[:, :], ends_t[es_][:, :], need[:, :], ALU.subtract))
            settle()
            step(v.tensor_scalar(base[:, :], base[:, :], float(STEP), None, ALU.mult))
            step(v.tensor_tensor(past[:, :, :], iota[:, 0:STEPS].unsqueeze(2).to_broadcast((P, STEPS, E)),
                                 ends_t[es_][:, :].unsqueeze(1).to_broadcast((P, STEPS, E)), ALU.is_ge))
            settle()
            step(v.tensor_reduce(expert_f[:, :], past[:, :, :], AXX, ALU.add))
            settle()
            v.tensor_scalar(expert_of[:, :], expert_f[:, :], float(E - 1), None, ALU.min).then_inc(tables, 1)
            dve.wait_ge(tables, 1)
            v.tensor_tensor(fresh[:, 2:STEPS], expert_of[:, 2:STEPS], expert_of[:, 0:STEPS - 2],
                            ALU.not_equal).then_inc(tables, 1)
            rank = bank(0, TILES * E).rearrange("p (t e) -> p t e", e=E)
            step(v.tensor_tensor(slot_all[:, :, :], rank, prefix[src][:, :, :], ALU.add))
            settle()
            step(v.tensor_tensor(slot_all[:, :, :], slot_all[:, :, :],
                                 base[:, :].unsqueeze(1).to_broadcast((P, TILES, E)), ALU.add))
            for k in range(2):
                settle()
                step(v.tensor_tensor(scratch[:, :, :], slot_all[:, :, :], is_top[k][:, :, :], ALU.mult))
                settle()
                step(v.tensor_reduce(slot_f[k][:, :], scratch[:, :, :], AXX, ALU.add))
                settle()
                step(v.tensor_copy(slot_i[k][:, :], slot_f[k][:, :]))
                settle()
                step(v.tensor_single_scalar(lo_i[k][:, :], slot_i[k][:, :], P - 1, ALU.bitwise_and))
                step(v.tensor_single_scalar(hi_i[k][:, :], slot_i[k][:, :], 7, ALU.logical_shift_right))
                settle()
                step(v.tensor_copy(lo_f[k][:, :], lo_i[k][:, :]))
                step(v.tensor_copy(hi_f[k][:, :], hi_i[k][:, :]))
            settle()
            dve.wait_ge(num_done, 2)
            for j in range(2 * TILES):
                t, k = j // 2, j % 2
                if j >= 4:
                    dve.wait_ge(pick_mm, j - 3)
                v.tensor_scalar(pick_lo[:, j % 4, :], iota[:, :], lo_f[k][:, t:t + 1], None, ALU.is_equal)
                v.tensor_scalar(pick_hi[:, j % 4, 0, :], iota[:, 0:COLS], hi_f[k][:, t:t + 1],
                                number[:, t:t + 1], ALU.is_equal, ALU.mult)
                v.tensor_scalar(pick_hi[:, j % 4, 1, :], iota[:, 0:COLS], hi_f[k][:, t:t + 1],
                                top_w[k][:, t:t + 1], ALU.is_equal, ALU.mult).then_inc(pick_done, 1)
            dve.wait_ge(pick_mm, 2 * TILES)
            v.tensor_copy(slot_w[:, :], bank(2)[:, COLS:2 * COLS]).then_inc(tables, 1)
            step(v.tensor_scalar(at_f[:, :], bank(2)[:, 0:COLS], -1.0, None, ALU.add))
            settle()
            step(v.tensor_scalar(gather_at[:, :], at_f[:, :], 0.0, None, ALU.max))
            step(v.tensor_scalar(at_m[:, :], at_f[:, :], 0.0, float(SKIP), ALU.is_lt, ALU.mult))
            settle()
            v.tensor_tensor(scatter_at[:, :], at_f[:, :], at_m[:, :], ALU.add).then_inc(tables, 1)

        @block.vector
        def _(dve):
            v = nc.vector
            count = [0]
            turn = [None]

            def step(ins):
                count[0] += 1
                ins.then_inc(own, 1)

            def settle():
                dve.wait_ge(own, count[0] if turn[0] is None else at(turn[0], OWN_B, OWN_P + count[0]))

            def settle_aggr():
                settle()
                v.memset(spare[:, :], 0.0)

            flat_h = wh[:, :, :, :].rearrange("p w k c -> p w (k c)")
            flat_l = wl[:, :, :, :].rearrange("p w k c -> p w (k c)")
            dve.wait_ge(w_in, RAW_IN + ROW_IN - 16)
            dve.wait_ge(c_made, CONSTANTS)
            for k in range(KC):
                v.tensor_scalar(vb_wide[:, k, :], ones[:, :], vb_col[:, k:k + 1], None,
                                ALU.mult).then_inc(vb_ready, 1)
            dve.wait_ge(w_hi, 3)
            v.tensor_tensor(flat_l[:, 0:DIRECT, :], raw[:, 0:DIRECT, :],
                            flat_h[:, 0:DIRECT, :].bitcast(F32), ALU.subtract).then_inc(w_lo, 1)
            for n, w in enumerate((VO, QA, KA, VA, VB)):
                dve.wait_ge(w_hi, 4 + n)
                v.tensor_tensor(flat_l[:, w, :], bank(n), flat_h[:, w, :].bitcast(F32),
                                ALU.subtract).then_inc(w_lo, 1)
            dve.wait_ge(w_fold, 6)
            step(v.tensor_tensor(o_row[:, :], bank(5, C), o_row[:, :], ALU.add))
            settle()
            assert count[0] == OWN_P
            dve.sem_inc(dve_end, 1)
            count[0] = 0

            def image(b):
                turn[0] = b

                def w(s, per, n):
                    dve.wait_ge(s, at(b, per, n))

                w(x_in, 16, 16)
                for k in range(KC):
                    for h in range(2):
                        step(v.bn_stats(gn_bn[:, k, h, :], xn[:, k, h * HALF:(h + 1) * HALF]))
                settle_aggr()
                for k in range(KC):
                    ins = v.bn_aggr(gn_mv[:, k, :], gn_bn[:, k, :, :].rearrange("p h s -> p (h s)"))
                ins.then_inc(gn_stat, 1)
                w(gn_mm, 2, 1)
                G0 = bank(7)[:, 0:2 * KC].rearrange("p (k s) -> p k s", k=KC)
                step(v.tensor_copy(gn_avg[:, :, :], G0))
                settle()
                step(v.tensor_tensor(gn_d[:, :], gn_mv[:, :, 0], gn_avg[:, :, 0], ALU.subtract))
                settle()
                v.tensor_tensor(gn_d2[:, :], gn_d[:, :], gn_d[:, :], ALU.mult).then_inc(gn_stat, 1)
                w(gn_mm, 2, 2)
                v.scalar_tensor_tensor(gn_var[:, :], bank(7)[:, 8:8 + KC], GN_EPS, gn_avg[:, :, 1],
                                       ALU.add, ALU.add).then_inc(pow_in, 1)
                w(pow_out, POWS, 1)
                step(v.tensor_tensor(gn_s[:, :], gn_r[:, :], gn_aff[:, 0:KC], ALU.mult))
                settle()
                step(v.tensor_tensor(gn_t[:, :], gn_avg[:, :, 0], gn_s[:, :], ALU.mult))
                settle()
                step(v.tensor_tensor(gn_t[:, :], gn_aff[:, KC:2 * KC], gn_t[:, :], ALU.subtract))
                settle()
                ends(dve, b, (pe_end, act_end, sp_end))
                for k in range(KC):
                    v.tensor_scalar(xn[:, k, :], xn[:, k, :], gn_s[:, k:k + 1], gn_t[:, k:k + 1],
                                    ALU.mult, ALU.add).then_inc(xn_done, 1)
                for k in range(KC):
                    w(xn_hi, KC, k + 1)
                    v.tensor_tensor(xs[1][:, k, :], xn[:, k, :], xs[0][:, k, :].bitcast(F32),
                                    ALU.subtract).then_inc(xn_lo, 1)
                for gi in range(PJ):
                    w(pj_hi, PJ, gi + 1)
                    if gi < 8:
                        q, n, m = gi // 4, gi % 4 // 2, gi % 2
                        c = slice(n * HALF, (n + 1) * HALF)
                        v.scalar_tensor_tensor((qs, ks)[q][1][:, m, c], bank(gi % 4),
                                               qk_bias[:, 2 * q + m:2 * q + m + 1],
                                               (qs, ks)[q][0][:, m, c].bitcast(F32),
                                               ALU.add, ALU.subtract).then_inc(pj_lo, 1)
                    else:
                        j = gi - 8
                        v.tensor_tensor(vs[1][:, 2 * j:2 * j + 2, :].rearrange("p j c -> p (j c)"),
                                        bank(gi % 4),
                                        vs[0][:, 2 * j:2 * j + 2, :].rearrange("p j c -> p (j c)").bitcast(F32),
                                        ALU.subtract).then_inc(pj_lo, 1)

                def max1(i):
                    w(s_mm, NT, i + 1)
                    v.tensor_reduce(neg_max[:, i:i + 1], bank(2 * (i % 2), count=2), AXX, ALU.max,
                                    negate=True).then_inc(s_max, 1)

                def lo1(i):
                    w(pt_mm, NT, i + 1)
                    step(v.tensor_tensor(x_row[:, i % 2, :], bank(6 + i % 2)[:, C:2 * C], o_row[:, :], ALU.add))
                    step(v.reciprocal(row_inv[:, i:i + 1], row_sum[:, i:i + 1]))
                    w(pt_hi, NT, i + 1)
                    v.tensor_tensor(pr[1][:, 0, :], bank(4, count=2), pr[0][:, 0, :].bitcast(F32),
                                    ALU.subtract).then_inc(pt_lo, 1)

                def out1(i):
                    w(av_mm, NT, i + 1)
                    settle()
                    v.scalar_tensor_tensor(tok[:, i, :], bank(6 + i % 2)[:, 0:C], row_inv[:, i:i + 1],
                                           x_row[:, i % 2, :], ALU.mult, ALU.add).then_inc(t_done, 1)
                    w(t_done, NT, i + 1)
                    step(v.bn_stats(ln_bn[:, i, :], tok[:, i, :]))
                    settle_aggr()
                    step(v.bn_aggr(ln_mv[:, i, :], ln_bn[:, i, :]))
                    settle()
                    v.tensor_scalar(ln_eps[:, i:i + 1], ln_mv[:, i, 1:2], LN_EPS, None,
                                    ALU.add).then_inc(pow_in, 1)

                def norm1(i):
                    w(pow_out, POWS, i + 2)
                    v.tensor_scalar(tn[:, i, :], tok[:, i, :], ln_mv[:, i, 0:1], ln_r[:, i:i + 1],
                                    ALU.subtract, ALU.mult).then_inc(tn_tok, 1)

                def lo_tn(h):
                    w(tn_hi, 2, h + 1)
                    c = slice(h * HALF, (h + 1) * HALF)
                    v.tensor_tensor(xs[1][:, :, c], bank(2 * h, count=2).rearrange("p (k t) -> p k t", k=KC),
                                    xs[0][:, :, c].bitcast(F32), ALU.subtract).then_inc(tn_lo, 1)

                max1(0)
                max1(1)
                for i in range(NT):
                    if i >= 1:
                        norm1(i - 1) if i >= 2 else None
                    lo1(i)
                    if i == 6:
                        lo_tn(0)
                    if i + 2 < NT:
                        max1(i + 2)
                    out1(i)
                    if i == 0:
                        norm1(0)
                norm1(NT - 1)

                n_u = 0
                for gi, (kind, o, n, m) in enumerate(R):
                    if gi == 2:
                        lo_tn(1)
                    if kind == "v":
                        continue
                    w(r_act, RG, gi + 1)
                    c = slice(n * HALF, (n + 1) * HALF)
                    if kind == "u":
                        dst = us[o % 2]
                        step(v.tensor_copy(dst[0][:, m, c], u32[:, n_u % 2, :]))
                        settle()
                        v.tensor_tensor(dst[1][:, m, c], u32[:, n_u % 2, :], dst[0][:, m, c].bitcast(F32),
                                        ALU.subtract).then_inc(r_dve, 1)
                        n_u += 1
                    else:
                        v.tensor_tensor((qs, ks)[o][1][:, m, c], bank(R_BANKS[gi % 4]),
                                        (qs, ks)[o][0][:, m, c].bitcast(F32), ALU.subtract).then_inc(r_dve, 1)

                def max2(i):
                    w(s2_mm, NT, i + 1)
                    v.tensor_reduce(neg_max[:, i:i + 1], bank(2 * (i % 2), count=2), AXX, ALU.max,
                                    negate=True).then_inc(s2_max, 1)

                def lo2(i):
                    w(p2_hi, NT, i + 1)
                    if i >= 2:
                        w(av2_mm, NT, i - 1)
                    v.tensor_tensor(pr[1][:, i % 2, :], prob[:, i % 2, :], pr[0][:, i % 2, :].bitcast(F32),
                                    ALU.subtract).then_inc(p2_lo, 1)

                def values2(i):
                    w(p2_exp, NT, i + 1)
                    if i >= 2:
                        w(av2_mm, NT, i - 1)
                    step(v.reciprocal(row_inv[:, i:i + 1], row_sum[:, i:i + 1]))
                    settle()
                    step(v.tensor_scalar(vk[0][:, i % 2, :], v32[:, i, :], row_inv[:, i:i + 1], None, ALU.mult))
                    settle()
                    v.scalar_tensor_tensor(vk[1][:, i % 2, :], v32[:, i, :], row_inv[:, i:i + 1],
                                           vk[0][:, i % 2, :].bitcast(F32), ALU.mult,
                                           ALU.subtract).then_inc(v2_done, 1)

                w(r_act, RG, RG)
                max2(0)
                for i in range(NT):
                    values2(i)
                    if i + 1 < NT:
                        max2(i + 1)
                    lo2(i)

                w(av2_mm, NT, NT)
                for m in range(4):
                    step(v.tensor_tensor(tok[:, 2 * m:2 * m + 2, :].rearrange("p j c -> p (j c)"), bank(4 + m),
                                         tok[:, 2 * m:2 * m + 2, :].rearrange("p j c -> p (j c)"), ALU.add))
                settle()

                def layer_norm(dst, src, n):
                    for i in range(NT):
                        step(v.bn_stats(ln_bn[:, i, :], src[:, i, :]))
                    settle_aggr()
                    for i in range(NT):
                        step(v.bn_aggr(ln_mv[:, i, :], ln_bn[:, i, :]))
                    settle()
                    v.tensor_scalar(ln_eps[:, :], ln_mv[:, :, 1], LN_EPS, None, ALU.add).then_inc(pow_in, 1)
                    w(pow_out, POWS, 1 + NT + n + 1)
                    for i in range(NT):
                        step(v.tensor_scalar(dst[:, i, :], src[:, i, :], ln_mv[:, i, 0:1], ln_r[:, i:i + 1],
                                             ALU.subtract, ALU.mult))
                    settle()

                layer_norm(x2, tok, 0)
                v.tensor_tensor(tok[:, :, :], tok[:, :, :], x2[:, :, :], ALU.add).then_inc(r_ready, 1)
                layer_norm(xf, x2, 1)
                step(v.tensor_tensor(xf[:, :, :], xf[:, :, :],
                                     g_row[:, :].unsqueeze(1).to_broadcast((P, NT, C)), ALU.mult))
                settle()
                v.tensor_tensor(xf[:, :, :], xf[:, :, :],
                                b_row[:, :].unsqueeze(1).to_broadcast((P, NT, C)), ALU.add).then_inc(xf_ready, 1)
                w(g_mm, 1, 1)
                step(v.tensor_copy(logits[:, bass.ds(b * NT, NT), :].rearrange("p t e -> p (t e)"),
                                   bank(4)[:, 0:NT * E]))
                settle()
                dve.sem_inc(dve_end, 1)
                assert count[0] == OWN_B, count[0]
                count[0] = 0

            with dve.Fori(0, B) as b:
                image(b)

            ends(dve, B, (pe_end, act_end, sp_end, pool_end))
            turn[0] = None
            route(dve, v)

            def w_piece(s, n, u, f):
                first = isinstance(s, int) and s < 2
                if f == 0:
                    dve.wait_ge(w1_in[n], at(u, 16, 16))
                    if not first:
                        dve.wait_ge(h_mm, at(s, FC, -FC))
                dve.wait_ge(ws_act, at(s, 8, f + 1))
                c = slice(f * 512, (f + 1) * 512)
                v.tensor_tensor(w1s[n][1][:, :, :].rearrange("p k f -> p (k f)")[:, c], w1r[:, n, c],
                                w1s[n][0][:, :, :].rearrange("p k f -> p (k f)")[:, c].bitcast(F32),
                                ALU.subtract).then_inc(ws_dve, 1)

            def x_lo(s, n):
                dve.wait_ge(xt_hi, at(s, 1, 1))
                v.tensor_tensor(xt[n][1][:, :, :].rearrange("p k t -> p (k t)"), bank(6),
                                xt[n][0][:, :, :].rearrange("p k t -> p (k t)").bitcast(F32),
                                ALU.subtract).then_inc(xt_lo, 1)

            def y_bias(s, n, first):
                dve.wait_ge(y_mm, at(s, FC, FC))
                if not first:
                    dve.wait_ge(y_act, at(s, 1, 0))
                ins = v.tensor_tensor(y_b[:, :, :], bank(4 + n).rearrange("p (h c) -> p h c", h=SUB),
                                      b2t[:, n:n + 1, :].to_broadcast((P, SUB, C)), ALU.add)
                ins.then_inc(y_dve, 1)

            for f in range(4):
                w_piece(0, 0, 0, f)
            x_lo(0, 0)

            def steps(i, first, last):
                for n in range(2):
                    s = i * 2 + n
                    if last and n == 1:
                        chunks(i, n, first, last, False)
                    elif first and n == 0:
                        chunks(i, n, first, last, True)
                    else:
                        with dve.If(dve.value_load(fresh[0:1, bass.ds(s + 1, 1)], min_val=0, max_val=1) == 1):
                            chunks(i, n, first, last, True)
                        with dve.Else():
                            dve.wait_ge(ws_dve, at(s, 4, 4))
                            dve.sem_inc(ws_dve, 4)
                            chunks(i, n, first, last, False)

            def chunks(i, n, first, last, split):
                if True:
                    s = i * 2 + n
                    for f in range(FC):
                        gi = n * FC + f
                        dve.wait_ge(h_act, at(i, 2 * FC, gi + 1))
                        if not (first and n == 0):
                            dve.wait_ge(y_mm, at(i, 2 * FC, gi + 1 - FC))
                        v.tensor_copy(hs[0][:, f, :], h32[:, gi % 4, :]).then_inc(h_hi, 1)
                        dve.wait_ge(h_hi, at(i, 2 * FC, gi + 1))
                        v.tensor_tensor(hs[1][:, f, :], h32[:, gi % 4, :], hs[0][:, f, :].bitcast(F32),
                                        ALU.subtract).then_inc(h_lo, 1)
                        if f == 2 and not (first and n == 0):
                            y_bias(s - 1, 1 - n, first)
                        if split and f < 4:
                            w_piece(s + 1, 1 - n, (i if n == 0 else i + 1), f)
                        if f == 4 and not (last and n == 1):
                            x_lo(s + 1, 1 - n)

            steps(0, True, False)
            with dve.Fori(1, STEPS // 2 - 1) as i:
                steps(i, False, False)
            steps(STEPS // 2 - 1, False, True)
            y_bias(STEPS - 1, 1, False)
            dve.sem_inc(dve_end, 1)

            for gi in range(TILES // 4):
                dve.wait_ge(o_mm, gi + 1)
                if gi >= 2:
                    dve.wait_ge(o_out[gi % 2], gi // 2 * 16)
                v.tensor_copy(cols_out[:, gi % 2, 1, :], bank(2 * (gi % 2) + 1)).then_inc(o_dve, 1)

        @block.tensor
        def _(pe):
            t = nc.tensor

            def three(out, left, right, first=True, last=True, **more):
                for n, (l, r) in enumerate(PASSES):
                    ins = t.matmul(out, left[l], right[r], start=first and n == 0, stop=last and n == 2, **more)
                return ins

            def weight(slot, k, m):
                return [w[:, slot, k, m * P:(m + 1) * P] for w in (wh, wl)]

            def weight_row(slot, k):
                return [w[:, slot, k, :] for w in (wh, wl)]

            def fold(n, left, right):
                for m in range(KC):
                    for k in range(KC):
                        ins = t.matmul(bank(n)[:, m * C:(m + 1) * C], left[:, k * C + m * P:k * C + (m + 1) * P],
                                       right[:, k * C:(k + 1) * C], start=(k == 0), stop=(k == KC - 1))
                ins.then_inc(w_fold, 1)

            pe.wait_ge(w_in, RAW_IN + ROW_IN - 16)
            fold(0, raw[:, 7, :], raw[:, 8, :])
            fold(1, raw[:, 9, :], raw[:, 5, :])
            fold(2, raw[:, 10, :], raw[:, 6, :])
            fold(3, raw[:, 12, :], raw[:, 13, :])
            pe.wait_ge(vo_ready, 1)
            fold(4, raw[:, 11, :], raw_vo[:, :])
            pe.wait_ge(vb_ready, KC)
            for k in range(KC):
                ins = t.matmul(bank(5, C), vb_wide[:, k, :], raw[:, 8, k * C:(k + 1) * C],
                               start=(k == 0), stop=(k == KC - 1))
            ins.then_inc(w_fold, 1)
            pe.wait_ge(c_made, CONSTANTS)
            pe.wait_ge(w_lo, 6)
            pe.sem_inc(pe_end, 1)

            def image(b):
                def w(s, per, n):
                    pe.wait_ge(s, at(b, per, n))

                ends(pe, b, (act_end, dve_end))
                w(gn_stat, 2, 1)
                t.matmul(bank(7)[:, 0:2 * KC], same_group[:, :], gn_mv[:, :, :].rearrange("p k s -> p (k s)"),
                         start=True, stop=True).then_inc(gn_mm, 1)
                w(gn_stat, 2, 2)
                t.matmul(bank(7)[:, 8:8 + KC], same_group[:, :], gn_d2[:, :],
                         start=True, stop=True).then_inc(gn_mm, 1)
                w(xn_lo, KC, KC)
                for gi in range(PJ):
                    if gi >= 4:
                        w(pj_lo, PJ, gi - 3)
                    out = bank(gi % 4)
                    if gi < 8:
                        q, n, m = gi // 4, gi % 4 // 2, gi % 2
                        for k in range(KC):
                            ins = three(out, weight(WQ + q, k, m),
                                        [a[:, k, n * HALF:(n + 1) * HALF] for a in xs], k == 0, k == KC - 1)
                    else:
                        for h in range(2):
                            j = 2 * (gi - 8) + h
                            for k in range(KC):
                                ins = three(out[:, h * C:(h + 1) * C], [a[:, k, j * P:(j + 1) * P] for a in xs],
                                            weight_row(VO, k), k == 0, k == KC - 1)
                    ins.then_inc(pj_mm, 1)
                w(pj_lo, PJ, PJ)

                def scores(i, rows_of, cols_of, signal_):
                    for n in range(NH):
                        for k in range(KC):
                            ins = three(bank(2 * (i % 2) + n), [a[:, k, i * P:(i + 1) * P] for a in rows_of],
                                        [a[:, k, n * HALF:(n + 1) * HALF] for a in cols_of], k == 0, k == KC - 1)
                    ins.then_inc(signal_, 1)

                def turn1(i):
                    w(p_exp, NT, i + 1)
                    if i >= 1:
                        w(pt_lo, NT, i)
                    if i >= 2:
                        w(t_done, NT, i - 1)
                    for k in range(KC):
                        t.transpose(bank(6 + i % 2)[:, C + k * P:C + (k + 1) * P], xn[:, k, i * P:(i + 1) * P],
                                    ident[:, :])
                    for j in range(NT):
                        ins = t.transpose(bank(4, count=2)[:, j * P:(j + 1) * P],
                                          prob[:, i % 2, j * P:(j + 1) * P], ident[:, :])
                    ins.then_inc(pt_mm, 1)

                def mix1(i):
                    w(pt_lo, NT, i + 1)
                    for j in range(NT):
                        ins = three(bank(6 + i % 2)[:, 0:C], [a[:, 0, j * P:(j + 1) * P] for a in pr],
                                    [a[:, j, :] for a in vs], j == 0, j == NT - 1)
                    ins.then_inc(av_mm, 1)

                def turn_tn(h):
                    w(tn_tok, NT, 4 * h + 4)
                    for k in range(KC):
                        for j in range(4):
                            ins = t.transpose(bank(2 * h + k)[:, j * P:(j + 1) * P],
                                              tn[:, 4 * h + j, k * P:(k + 1) * P], ident[:, :])
                    ins.then_inc(tn_mm, 1)

                scores(0, qs, ks, s_mm)
                scores(1, qs, ks, s_mm)
                for i in range(NT):
                    turn1(i)
                    if i + 2 < NT:
                        scores(i + 2, qs, ks, s_mm)
                    if i == 6:
                        turn_tn(0)
                    mix1(i)

                for gi, (kind, o, n, m) in enumerate(R):
                    if gi == 2:
                        turn_tn(1)
                    if gi == 0:
                        w(tn_lo, 2, 1)
                    if gi == 2:
                        w(t_done, NT, 7)
                    if gi == 3:
                        w(t_done, NT, 8)
                    if gi == 4:
                        w(tn_lo, 2, 2)
                    if gi >= 4:
                        w(r_act, RG, gi - 3)
                        if R[gi - 4][0] == "p":
                            w(r_dve, RD, R_DVE[gi - 4])
                    if kind != "u" and R[gi - 1][:2] != R[gi][:2]:
                        w(r_dve, RD, R_DVE[max(j for j in range(gi) if R[j][:2] == ("u", o))])
                    out = bank(R_BANKS[gi % 4])
                    if kind == "u":
                        for k in range(KC):
                            ins = three(out, weight(Q1 + o, k, m),
                                        [a[:, k, n * HALF:(n + 1) * HALF] for a in xs], k == 0, k == KC - 1)
                    elif kind == "p":
                        for k in range(KC):
                            three(out, weight(AQ + o, k, m),
                                  [a[:, k, n * HALF:(n + 1) * HALF] for a in xs], k == 0, False)
                        for k in range(KC):
                            ins = three(out, weight(QA + o, k, m),
                                        [a[:, k, n * HALF:(n + 1) * HALF] for a in us[o % 2]], False, k == KC - 1)
                    else:
                        for h in range(2):
                            j = 2 * n + h
                            for k in range(KC):
                                three(out[:, h * C:(h + 1) * C], [a[:, k, j * P:(j + 1) * P] for a in xs],
                                      weight_row(VA, k), k == 0, False)
                            for k in range(KC):
                                ins = three(out[:, h * C:(h + 1) * C], [a[:, k, j * P:(j + 1) * P] for a in us[0]],
                                            weight_row(VB, k), False, k == KC - 1)
                    ins.then_inc(r_mm, 1)

                def mix2(i):
                    w(p2_lo, NT, i + 1)
                    w(v2_done, NT, i + 1)
                    if i == 0:
                        w(r_act, RG, RG)
                        w(r_dve, RD, RD)
                    for j in range(NT):
                        ins = three(bank(4 + j // 2)[:, j % 2 * C:(j % 2 + 1) * C],
                                    [a[:, i % 2, j * P:(j + 1) * P] for a in pr],
                                    [a[:, i % 2, :] for a in vk], i == 0 and j % 2 == 0, i == NT - 1,
                                    skip_group_check=True)
                    ins.then_inc(av2_mm, 1)

                w(r_dve, RD, RD)
                scores(0, ks, qs, s2_mm)
                scores(1, ks, qs, s2_mm)
                for i in range(NT):
                    mix2(i)
                    if i + 2 < NT:
                        w(p2_exp, NT, i + 1)
                        scores(i + 2, ks, qs, s2_mm)

                w(xf_ready, 1, 1)
                for h in range(2):
                    for k in range(KC):
                        for j in range(4):
                            ins = t.transpose(bank(2 * h + k)[:, j * P:(j + 1) * P],
                                              xf[:, 4 * h + j, k * P:(k + 1) * P], ident[:, :])
                    ins.then_inc(xf_mm, 1)
                for j in range(NT):
                    if j % 4 == 0:
                        w(xf_col, 2, j // 4 + 1)
                    for k in range(KC):
                        ins = t.matmul(bank(4)[:, j * E:(j + 1) * E], xfT[:, k, j * P:(j + 1) * P],
                                       gate_sb[:, k, :], start=(k == 0), stop=(k == KC - 1))
                ins.then_inc(g_mm, 1)
                pe.sem_inc(pe_end, 1)

            with pe.Fori(0, B) as b:
                image(b)

            pe.wait_ge(top_done, 3)
            flat = either[:, :, :].rearrange("p t e -> p (t e)")
            t.matmul(bank(0, TILES * E), before[:, :], flat, start=True, stop=True)
            t.matmul(bank(1, TILES * E), ones[:, :], flat, start=True, stop=True).then_inc(rank_mm, 1)
            for j in range(2 * TILES):
                pe.wait_ge(pick_done, j + 1)
                t.matmul(bank(2, 2 * COLS), pick_lo[:, j % 4, :],
                         pick_hi[:, j % 4, :, :].rearrange("p a c -> p (a c)"),
                         start=(j == 0), stop=(j == 2 * TILES - 1)).then_inc(pick_mm, 1)

            pe.wait_ge(tables, 4)

            def x_turn(s, n, u):
                pe.wait_ge(g_in[n], at(u, SUB * 16, SUB * 16))
                if not (isinstance(s, int) and s == 0):
                    pe.wait_ge(xt_lo, at(s, 1, 0))
                for k in range(KC):
                    for h in range(SUB):
                        ins = t.transpose(bank(6)[:, k * STEP + h * P:k * STEP + (h + 1) * P],
                                          xg[:, n, h, k * P:(k + 1) * P], ident[:, :])
                ins.then_inc(xt_mm, 1)

            def first_product(i, s, n, f, new):
                gi = n * FC + f
                if f == 0:
                    pe.wait_ge(xt_lo, at(s, 1, 1))
                    pe.wait_ge(ws_dve, at(s, 4, 4))
                if not (new and gi < 4):
                    pe.wait_ge(h_act, at(i, 2 * FC, gi - 3))
                for k in range(KC):
                    ins = three(bank(gi % 4, STEP), [a[:, k, f * P:(f + 1) * P] for a in w1s[n % 2]],
                                [a[:, k, :] for a in xt[n % 2]], k == 0, k == KC - 1)
                ins.then_inc(h_mm, 1)

            def second_product(i, s, n, f, new):
                gi = n * FC + f
                pe.wait_ge(h_lo, at(i, 2 * FC, gi + 1))
                if f % 2 == 0:
                    pe.wait_ge(ws_act, at(s, 8, 5 + f // 2))
                    pe.wait_ge(ws_pool, at(s, 4, 1 + f // 2))
                if f == 0:
                    if not new:
                        pe.wait_ge(y_dve, at(s, 1, -1))
                for h in range(SUB):
                    ins = three(bank(4 + n)[:, h * C:(h + 1) * C], [a[:, f, h * P:(h + 1) * P] for a in hs],
                                [a[:, f, :] for a in w2s[n]], f == 0 and h == 0, f == FC - 1,
                                skip_group_check=True)
                ins.then_inc(y_mm, 1)

            AHEAD = 2
            x_turn(0, 0, 0)
            for f in range(AHEAD):
                first_product(0, 0, 0, f, True)

            def steps(i, first, last):
                for gi in range(2 * FC):
                    n, f = gi // FC, gi % FC
                    s = i * 2 + n
                    if f == 3 and not (last and n == 1):
                        x_turn(s + 1, 1 - n, (i if n == 0 else i + 1))
                    ahead = gi + AHEAD
                    if not (last and ahead >= 2 * FC):
                        na, fa = ahead // FC, ahead % FC
                        first_product(i, i * 2 + na, na, fa, first)
                    second_product(i, s, n, f, first)

            steps(0, True, False)
            with pe.Fori(1, STEPS // 2 - 1) as i:
                steps(i, False, False)
            steps(STEPS // 2 - 1, False, True)
            pe.sem_inc(pe_end, 1)

            for gi in range(TILES // 4):
                pe.wait_ge(r_in[gi % 2], (gi // 2 + 1) * 16)
                if gi == 0:
                    ends(pe, B + 1, (act_end, dve_end))
                if gi >= 2:
                    pe.wait_ge(o_act, gi - 1)
                    pe.wait_ge(o_dve, gi - 1)
                for k in range(KC):
                    for j in range(4):
                        ins = t.transpose(bank(2 * (gi % 2) + k)[:, j * P:(j + 1) * P],
                                          rows[:, gi % 2, j, k * P:(k + 1) * P], ident[:, :])
                ins.then_inc(o_mm, 1)


CONSTANTS = 10
OWN_P = 1
OWN_B = 123


def kernel(**inputs):
    import numpy as np
    import concourse.bacc as bacc
    from concourse.bass_utils import run_bass_kernel_spmd

    a = {k: np.asarray(v) for k, v in inputs.items()}
    x = a["x"]
    B, C, H, W = x.shape

    def chunks(v):
        return v.reshape(-1, P).T

    qkv_w, qkv_b = a["L0_conv_qkv_w"], a["L0_conv_qkv_b"]
    E, F = a["L1_ffn_b1"].shape
    args = {
        "x": x.reshape(B, C, H * W),
        "qT": qkv_w[0:C].T, "kT": qkv_w[C:2 * C].T, "v_w": qkv_w[2 * C:3 * C], "oT": a["L0_conv_out_w"].T,
        "qk_b": chunks(qkv_b[0:2 * C]), "v_b": chunks(qkv_b[2 * C:3 * C]),
        "out_b": a["L0_conv_out_b"].reshape(1, C),
        "gn": np.concatenate([chunks(a["L0_conv_gn_weight"]), chunks(a["L0_conv_gn_bias"])], axis=1),
        "W1": np.stack([a[f"L1_attn_{n}W1"] for n in "qkv"]),
        "W2T": np.stack([a[f"L1_attn_{n}W2"].T for n in "qkv"]),
        "a_qk": np.stack([a["L1_attn_aWq"], a["L1_attn_aWk"]]),
        "a_vT": a["L1_attn_aWv"].T, "Wout": a["L1_attn_Wout"],
        "gate_w": a["L1_ffn_gate_w"], "w1": a["L1_ffn_w1"],
        "b1": a["L1_ffn_b1"].reshape(E, F // P, P).transpose(0, 2, 1),
        "w2": a["L1_ffn_w2"], "b2": a["L1_ffn_b2"],
        "ln_g": a["L1_ffn_ln_g"].reshape(1, C), "ln_b": a["L1_ffn_ln_b"].reshape(1, C),
    }
    nc = bacc.Bacc("TRN2", target_bir_lowering=False, num_devices=1)
    arrays, aps = {}, {}
    for name, v in args.items():
        v = np.ascontiguousarray(v)
        arrays[f"in_{name}"] = v
        aps[name] = nc.dram_tensor(f"in_{name}", v.shape, mybir.dt.from_np(v.dtype), kind="ExternalInput").ap()
    aps["out"] = nc.dram_tensor("out_tokens", (B, C, H * W), F32, kind="ExternalOutput").ap()
    hybrid_block_kernel(nc, **aps)
    r = run_bass_kernel_spmd(nc, [arrays], core_ids=[0])
    return r.results[0]["out_tokens"].reshape(B, C, H, W)
```

```python
from contextlib import ExitStack

import concourse.bass as bass
from concourse import mybir

P = 128
ALU = mybir.AluOpType
ACT = mybir.ActivationFunctionType
AXX = mybir.AxisListType.X
F32 = mybir.dt.float32
F32R = mybir.dt.float32r
I32 = mybir.dt.int32

PASSES = ((0, 0), (0, 1), (1, 0))

WQ, WK, Q1, K1, V1, AQ, AK, VO, QA, KA, VA, VB = range(12)
DIRECT = 7


def at(turn, per_turn, n):
    return turn * per_turn + n


def hybrid_block_kernel(nc, x, qT, kT, v_w, oT, qk_b, v_b, out_b, gn, W1, W2T, a_qk, a_vT, Wout,
                        gate_w, w1, b1, w2, b2, ln_g, ln_b, out):
    B, C, T = x.shape
    KC = C // P
    NT = T // P
    HALF = 512
    NH = T // HALF
    TOK = B * T
    TILES = TOK // P
    E = gate_w.shape[1]
    FF = w1.shape[2]
    FC = FF // P
    GROUP = C // 32
    STEP = 256
    SUB = STEP // P
    STEPS = TOK * 2 // STEP + E
    COLS = STEPS * SUB
    GN_EPS = LN_EPS = 1e-5
    SKIP = 2 * TOK
    assert KC == 2 and STEPS % 2 == 0 and NT == 8 and NH == 2 and TILES * E == 256

    x_d = x.rearrange("b (k p) t -> b p k t", p=P)
    out_d = out.rearrange("b (k p) t -> b p k t", p=P)
    acc_d = nc.dram_tensor("acc_rows", (TOK, C), F32, kind="Internal").ap()
    xf_d = nc.dram_tensor("xf_rows", (TOK, C), F32, kind="Internal").ap()
    acc_t = acc_d.rearrange("(t p) c -> p t c", p=P)
    xf_t = xf_d.rearrange("(t p) c -> p t c", p=P)
    w1_d = w1.rearrange("e (k p) f -> e p k f", p=P)
    w2_d = w2.rearrange("e (f p) d -> e p f d", p=P)

    ctx = ExitStack()
    with ctx:
        def psum(name, cols):
            return ctx.enter_context(nc.psum_tensor(name, [P, cols], F32))

        def sem(name):
            return ctx.enter_context(nc.semaphore(name))

        def sb(name, shape, dt=F32, scope=ctx):
            return scope.enter_context(nc.sbuf_tensor(name, shape, dt))

        ps = psum("ps", 8 * 512)

        def bank(n, cols=512, count=1):
            return ps[:, n * 512:(n - 1 + count) * 512 + cols]

        ident = sb("ident", [P, P])
        ones = sb("ones", [P, P])
        same_group = sb("same_group", [P, P])
        minus_half = sb("minus_half", [P, 8])
        minus_one = sb("minus_one", [P, 8])
        logits = sb("logits", [P, TILES, E])

        batch_scope = ExitStack()

        def bs(name, shape, dt=F32):
            return sb(name, shape, dt, batch_scope)

        wh = bs("wh", [P, 12, KC, C], F32R)
        wl = bs("wl", [P, 12, KC, C], F32R)
        qk_bias = bs("qk_bias", [P, 4])
        gn_aff = bs("gn_aff", [P, 4])
        o_row = bs("o_row", [P, C])
        g_row = bs("g_row", [P, C])
        b_row = bs("b_row", [P, C])
        gate_sb = bs("gate_sb", [P, KC, E])
        xn = bs("xn", [P, KC, T])
        xs = [bs(f"xs{i}", [P, KC, T], F32R) for i in range(2)]
        qs = [bs(f"qs{i}", [P, KC, T], F32R) for i in range(2)]
        ks = [bs(f"ks{i}", [P, KC, T], F32R) for i in range(2)]
        tok = bs("tok", [P, NT, C])
        prob = bs("prob", [P, 2, T])
        pr = [bs(f"pr{i}", [P, 2, T], F32R) for i in range(2)]
        gn_bn = bs("gn_bn", [P, KC, 2, 6])
        gn_mv = bs("gn_mv", [P, KC, 2])
        gn_avg = bs("gn_avg", [P, KC, 2])
        gn_d = bs("gn_d", [P, KC])
        gn_d2 = bs("gn_d2", [P, KC])
        gn_r = bs("gn_r", [P, KC])
        gn_var = bs("gn_var", [P, KC])
        gn_s = bs("gn_s", [P, KC])
        gn_t = bs("gn_t", [P, KC])
        neg_max = bs("neg_max", [P, NT])
        row_sum = bs("row_sum", [P, NT])
        row_inv = bs("row_inv", [P, NT])
        ln_bn = bs("ln_bn", [P, NT, 6])
        ln_mv = bs("ln_mv", [P, NT, 2])
        ln_eps = bs("ln_eps", [P, NT])
        ln_r = bs("ln_r", [P, NT])
        tl_bn = bs("tl_bn", [P, 2, NT, 6])
        tl_mv = bs("tl_mv", [P, 2, NT, 2])
        tl_eps = bs("tl_eps", [P, 2, NT])
        tl_r = bs("tl_r", [P, 2, NT])
        tl_mr = bs("tl_mr", [P, 2, NT])
        tl_nb = bs("tl_nb", [P, 2, NT])
        xf = bs("xf", [P, NT, C])
        xfT = bs("xfT", [P, KC, T])
        spare = bs("spare", [P, 1])
        here = ExitStack()
        raw = sb("raw", [P, 14, KC * C], F32, here)
        raw_vo = sb("raw_vo", [P, KC * C], F32, here)
        vb_wide = sb("vb_wide", [P, KC, P], F32, here)
        vb_col = sb("vb_col", [P, KC], F32, here)
        here.close()
        us = [[sb(f"us{n}{i}", [P, KC, T], F32R, here) for i in range(2)] for n in range(2)]
        here.close()
        x2 = sb("x2", [P, NT, C], F32, here)
        between = sb("between", [P, 2 * NT * C], F32, here)
        tn = sb("tn", [P, NT, C], F32, here)
        here.close()
        hold_r1 = sb("hold_r1", [P, 8192], F32, batch_scope)
        vs = [sb(f"vs{i}", [P, NT, C], F32R, here) for i in range(2)]
        here.close()
        v32 = sb("v32", [P, NT, C], F32, here)
        vk = [sb(f"vk{i}", [P, 2, C], F32R, here) for i in range(2)]
        here.close()
        hold_r2 = sb("hold_r2", [P, 4096], F32, batch_scope)
        batch_scope.close()

        route_scope = ExitStack()

        def rs(name, shape, dt=F32):
            return sb(name, shape, dt, route_scope)

        expert_of = ctx.enter_context(nc.sbuf_tensor("expert_of", [P, STEPS], I32))
        fresh = ctx.enter_context(nc.sbuf_tensor("fresh", [P, STEPS], I32))
        gather_at = sb("gather_at", [P, COLS], I32)
        scatter_at = sb("scatter_at", [P, COLS], I32)
        slot_w = sb("slot_w", [P, COLS])
        before = rs("before", [P, P])
        iota_i = rs("iota_i", [P, P], I32)
        iota = rs("iota", [P, P])
        top8 = rs("top8", [P, TILES, 8])
        top_i = rs("top_i", [P, TILES, 8], mybir.dt.uint32)
        top_f = rs("top_f", [P, TILES, 8])
        exps = rs("exps", [P, TILES, E])
        zsum = rs("zsum", [P, TILES])
        zinv = rs("zinv", [P, TILES])
        is_top = [rs(f"is_top{k}", [P, TILES, E]) for k in range(2)]
        either = rs("either", [P, TILES, E])
        scratch = rs("scratch", [P, TILES, E])
        top_w = [rs(f"top_w{k}", [P, TILES]) for k in range(2)]
        prefix = [rs(f"prefix{i}", [P, TILES, E]) for i in range(2)]
        slot_all = rs("slot_all", [P, TILES, E])
        cnt_f = rs("cnt_f", [P, E])
        cnt_i = rs("cnt_i", [P, E], I32)
        cnt_s = rs("cnt_s", [P, E], I32)
        need = rs("need", [P, E])
        ends_t = [rs(f"ends{i}", [P, E]) for i in range(2)]
        base = rs("base", [P, E])
        past = rs("past", [P, STEPS, E])
        expert_f = rs("expert_f", [P, STEPS])
        slot_f = [rs(f"slot_f{k}", [P, TILES]) for k in range(2)]
        slot_i = [rs(f"slot_i{k}", [P, TILES], I32) for k in range(2)]
        lo_i = [rs(f"lo_i{k}", [P, TILES], I32) for k in range(2)]
        hi_i = [rs(f"hi_i{k}", [P, TILES], I32) for k in range(2)]
        lo_f = [rs(f"lo_f{k}", [P, TILES]) for k in range(2)]
        hi_f = [rs(f"hi_f{k}", [P, TILES]) for k in range(2)]
        number_i = rs("number_i", [P, TILES], I32)
        number = rs("number", [P, TILES])
        pick_lo = rs("pick_lo", [P, 4, P])
        pick_hi = rs("pick_hi", [P, 4, 2, COLS])
        at_f = rs("at_f", [P, COLS])
        at_g = rs("at_g", [P, COLS])
        at_s = rs("at_s", [P, COLS])
        at_m = rs("at_m", [P, COLS])
        route_scope.close()

        ex_scope = ExitStack()

        def es(name, shape, dt=F32):
            return sb(name, shape, dt, ex_scope)

        w1r = es("w1r", [P, 2, KC * FF])
        w2r = es("w2r", [P, 2, FC * C])
        b1t = es("b1t", [P, 2, FC])
        b2t = es("b2t", [P, 2, C])
        w1s = [[es(f"w1s{n}{i}", [P, KC, FF], F32R) for i in range(2)] for n in range(2)]
        w2s = [[es(f"w2s{n}{i}", [P, FC, C], F32R) for i in range(2)] for n in range(2)]
        xg = es("xg", [P, 2, SUB, C])
        xt = [[es(f"xt{n}{i}", [P, KC, STEP], F32R) for i in range(2)] for n in range(2)]
        h32 = es("h32", [P, 4, STEP])
        hs = [es(f"hs{i}", [P, FC, STEP], F32R) for i in range(2)]
        y_b = es("y_b", [P, SUB, C])
        y_w = es("y_w", [P, 2, SUB, C])
        now_g = es("now_g", [P, 2, SUB], I32)
        now_s = es("now_s", [P, 2, SUB], I32)
        ex_scope.close()
        rows = sb("rows", [P, 2, 4, C], F32, ex_scope)
        cols_out = sb("cols_out", [P, 2, KC, HALF], F32, ex_scope)
        ex_scope.close()

        S = {}

        def signal(name):
            S[name] = sem(name)
            return S[name]

        pool_held = signal("pool_held")
        sp_held = signal("sp_held")
        c_made = signal("c_made")
        w_in = signal("w_in")
        w_fold = signal("w_fold")
        w_hi = signal("w_hi")
        w_lo = signal("w_lo")
        vo_ready = signal("vo_ready")
        vb_ready = signal("vb_ready")
        x_in = signal("x_in")
        gn_stat = signal("gn_stat")
        gn_mm = signal("gn_mm")
        gn_pow_in = signal("gn_pow_in")
        gn_pow_out = signal("gn_pow_out")
        xn_done = signal("xn_done")
        xn_hi = signal("xn_hi")
        xn_lo = signal("xn_lo")
        pj_mm = signal("pj_mm")
        pj_hi = signal("pj_hi")
        pj_lo = signal("pj_lo")
        s_mm = signal("s_mm")
        s_max = signal("s_max")
        p_exp = signal("p_exp")
        pt_mm = signal("pt_mm")
        pt_hi = signal("pt_hi")
        pt_lo = signal("pt_lo")
        av_mm = signal("av_mm")
        t_done = signal("t_done")
        ln_in = signal("ln_in")
        ln_out = signal("ln_out")
        tn_tok = signal("tn_tok")
        tn_mm = signal("tn_mm")
        tn_hi = signal("tn_hi")
        tn_lo = signal("tn_lo")
        r_mm = signal("r_mm")
        r_act = signal("r_act")
        r_dve = signal("r_dve")
        s2_mm = signal("s2_mm")
        s2_max = signal("s2_max")
        p2_exp = signal("p2_exp")
        p2_hi = signal("p2_hi")
        p2_lo = signal("p2_lo")
        v2_done = signal("v2_done")
        av2_mm = signal("av2_mm")
        added2 = signal("added2")
        tl_in = signal("tl_in")
        tl_out = signal("tl_out")
        tl_own = signal("tl_own")
        x2_done = signal("x2_done")
        xf_norm = signal("xf_norm")
        r_ready = signal("r_ready")
        xf_ready = signal("xf_ready")
        tok_out = signal("tok_out")
        xf_out = signal("xf_out")
        xf_mm = signal("xf_mm")
        xf_col = signal("xf_col")
        g_mm = signal("g_mm")
        u_read = signal("u_read")
        own = signal("own")
        pe_end = signal("pe_end")
        act_end = signal("act_end")
        dve_end = signal("dve_end")
        pool_end = signal("pool_end")
        sp_end = signal("sp_end")
        top_done = signal("top_done")
        exp_done = signal("exp_done")
        rank_mm = signal("rank_mm")
        pick_done = signal("pick_done")
        pick_mm = signal("pick_mm")
        num_done = signal("num_done")
        tables = signal("tables")
        own_r = signal("own_r")
        w1_in = [signal(f"w1_in{n}") for n in range(2)]
        w2_in = [signal(f"w2_in{n}") for n in range(2)]
        b_in = [signal(f"b_in{n}") for n in range(2)]
        ws_act = signal("ws_act")
        ws_dve = signal("ws_dve")
        ws_pool = signal("ws_pool")
        g_in = [signal(f"g_in{n}") for n in range(2)]
        idx_g = signal("idx_g")
        idx_s = signal("idx_s")
        xt_mm = signal("xt_mm")
        xt_hi = signal("xt_hi")
        xt_lo = signal("xt_lo")
        h_mm = signal("h_mm")
        h_act = signal("h_act")
        h_hi = signal("h_hi")
        h_lo = signal("h_lo")
        y_mm = signal("y_mm")
        y_dve = signal("y_dve")
        y_act = signal("y_act")
        added = signal("added")
        y_free = signal("y_free")
        r_in = [signal(f"r_in{n}") for n in range(2)]
        o_mm = signal("o_mm")
        o_act = signal("o_act")
        o_dve = signal("o_dve")
        o_out = [signal(f"o_out{n}") for n in range(2)]

        R = [("u", 0, 0, 0), ("u", 0, 0, 1), ("u", 1, 0, 0), ("u", 1, 0, 1),
             ("u", 0, 1, 0), ("u", 0, 1, 1), ("u", 1, 1, 0), ("u", 1, 1, 1)]
        R += [("p", 0, n, m) for n in range(NH) for m in range(KC)]
        R += [("u", 2, n, m) for n in range(NH) for m in range(KC)]
        R += [("p", 1, n, m) for n in range(NH) for m in range(KC)]
        R += [("v", 2, j, 0) for j in range(NT // 2)]
        RG = len(R)
        R_DVE = [sum(k != "v" for k, *_ in R[:g + 1]) for g in range(RG)]
        RD = R_DVE[-1]
        R_BANKS = (4, 5, 6, 7)
        TN_AT = 3
        GATE_AT = 8
        PE_GN = {12: 0, 16: 1}
        DVE_GN = {8: 0, 14: 1, 18: 2, 19: 3}
        GN_BANK = 1
        ACT_TAIL = {3: (0, 0), 5: (0, 1), 9: (1, 0), 11: (1, 1)}
        DVE_TAIL = {1: (0, 0), 3: (0, 1), 7: (1, 0), 9: (1, 1)}

        block = ctx.enter_context(nc.Block())

        PJ = 12

        def ends(eng, n, semaphores):
            for s in semaphores:
                eng.wait_ge(s, n)

        RAW_IN = 14 * 16
        ROW_IN = 9 * 16

        @block.sync
        def _(sp):
            for n, w in enumerate([qT, kT, W1[0], W1[1], W1[2], a_qk[0], a_qk[1],
                                   v_w, oT, W2T[0], W2T[1], W2T[2], a_vT, Wout]):
                sp.dma_start(raw[:, n, :].rearrange("p (k c) -> p k c", k=KC),
                             w.rearrange("(k p) c -> p k c", p=P)).then_inc(w_in, 16)
                if n == 1:
                    sp.dma_start(xn[:, :, :], x_d[0]).then_inc(x_in, 16)
            sp.dma_start(qk_bias[:, :], qk_b).then_inc(w_in, 16)
            sp.dma_start(gn_aff[:, :], gn).then_inc(w_in, 16)
            sp.dma_start(vb_col[:, :], v_b).then_inc(w_in, 16)
            with nc.allow_non_contiguous_dma(reason="rows read by every partition"):
                sp.dma_start(o_row[:, :], out_b.to_broadcast((P, C))).then_inc(w_in, 16)
                sp.dma_start(g_row[:, :], ln_g.to_broadcast((P, C))).then_inc(w_in, 16)
                sp.dma_start(b_row[:, :], ln_b.to_broadcast((P, C))).then_inc(w_in, 16)
            for k in range(KC):
                sp.dma_start(gate_sb[:, k, :], gate_w[k * P:(k + 1) * P, :]).then_inc(w_in, 16)

            def image(b, first, last):
                if not last:
                    if not first:
                        sp.wait_ge(xf_out, at(b, 16, 0))
                        sp.sem_inc(sp_held, 1)
                    sp.wait_ge(av_mm, at(b, NT, NT))
                    sp.sem_inc(sp_held, 1)
                    sp.dma_start(xn[:, :, :], x_d[b + 1] if isinstance(b, int) else
                                 x_d[bass.ds(b + 1, 1)].rearrange("b p k t -> (b p) k t")
                                 ).then_inc(x_in, 16)

            def rows_of(b):
                sp.wait_ge(r_ready, at(b, 2, 2))
                sp.sem_inc(sp_held, 1)
                sp.dma_start(acc_t[:, bass.ds(b * NT, NT), :], tok[:, :, :]).then_inc(tok_out, 16)
                sp.wait_ge(xf_ready, at(b, 2, 2))
                sp.sem_inc(sp_held, 1)
                sp.dma_start(xf_t[:, bass.ds(b * NT, NT), :], xf[:, :, :]).then_inc(xf_out, 16)

            image(0, True, False)
            with sp.Fori(1, B - 1) as b:
                rows_of(b - 1)
                image(b, False, False)
            rows_of(B - 2)
            rows_of(B - 1)
            sp.wait_ge(tok_out, B * 16)
            sp.wait_ge(xf_out, B * 16)
            sp.sem_inc(sp_end, 1)

            sp.wait_ge(tables, 4)
            ends(sp, 1, (pe_end, act_end, dve_end, pool_end))

            def expert_load(s, n, u, first):
                if not first:
                    sp.wait_ge(ws_act, at(s, 8, -8))
                    sp.sem_inc(sp_held, 1)
                    sp.wait_ge(ws_dve, at(s, 4, -4))
                    sp.sem_inc(sp_held, 1)
                    sp.wait_ge(ws_pool, at(s, 4, -4))
                    sp.sem_inc(sp_held, 1)
                e = sp.value_load(expert_of[0:1, bass.ds(s, 1)], min_val=0, max_val=E - 1)

                def weights():
                    sp.dma_start(w1r[:, n, :].rearrange("p (k f) -> p k f", k=KC),
                                 w1_d[bass.ds(e, 1)].rearrange("e p k f -> (e p) k f")).then_inc(w1_in[n], 16)
                    sp.dma_start(w2r[:, n, :].rearrange("p (f c) -> p f c", f=FC),
                                 w2_d[bass.ds(e, 1)].rearrange("e p f c -> (e p) f c")).then_inc(w2_in[n], 16)

                if first:
                    weights()
                else:
                    with sp.If(sp.value_load(fresh[0:1, bass.ds(s, 1)], min_val=0, max_val=1) == 1):
                        weights()
                    with sp.Else():
                        sp.wait_ge(w1_in[n], at(u, 16, 0))
                        sp.sem_inc(w1_in[n], 16)
                        sp.wait_ge(w2_in[n], at(u, 16, 0))
                        sp.sem_inc(w2_in[n], 16)
                if not first:
                    sp.wait_ge(h_act, at(s, FC, -FC))
                    sp.sem_inc(sp_held, 1)
                    sp.wait_ge(y_dve, at(s, 1, -1))
                    sp.sem_inc(sp_held, 1)
                sp.dma_start(b1t[:, n, :], b1[bass.ds(e, 1)].rearrange("e p f -> (e p) f")
                             ).then_inc(b_in[n], 16)
                sp.dma_start(b2t[:, n, :], b2[bass.ds(e, 1), :].to_broadcast((P, C))).then_inc(b_in[n], 16)

            expert_load(0, 0, 0, True)
            expert_load(1, 1, 0, True)
            with sp.Fori(1, STEPS // 2) as i:
                for n in range(2):
                    expert_load(i * 2 + n, n, i, False)

            sp.wait_ge(added, STEPS * SUB * 16)
            ends(sp, 2, (pe_end, act_end, dve_end))
            G = TILES // 4
            for g in range(2):
                sp.dma_start(rows[:, g % 2, :, :], acc_t[:, 4 * g:4 * g + 4, :]).then_inc(r_in[g % 2], 16)

            def piece(g, n, more):
                sp.wait_ge(o_act, at(g, 1, 1))
                sp.wait_ge(o_dve, at(g, 1, 1))
                b = g // NH
                sp.dma_start(out_d[b, :, :, n * HALF:(n + 1) * HALF],
                             cols_out[:, n, :, :]).then_inc(o_out[n], 16)
                if more:
                    sp.dma_start(rows[:, n, :, :], acc_t[:, bass.ds((g + 2) * 4, 4), :]).then_inc(r_in[n], 16)

            for g in range(G):
                piece(g, g % 2, g + 2 < G)
            for n in range(2):
                sp.wait_ge(o_out[n], G // 2 * 16)

        @block.gpsimd
        def _(pool):
            g = nc.gpsimd
            made = [0]

            def make(ins):
                made[0] += 1
                ins.then_inc(c_made, 1)

            make(g.memset(ident[:, :], 0.0))
            make(g.memset(ones[:, :], 1.0))
            make(g.memset(same_group[:, :], 1.0 / GROUP))
            make(g.memset(minus_half[:, :], -0.5))
            make(g.memset(minus_one[:, :], -1.0))
            pool.wait_ge(c_made, made[0])
            make(g.affine_select(out=ident[:, :], in_=ident[:, :], compare_op=ALU.not_equal, fill=1.0,
                                 base=0, pattern=[[-1, P]], channel_multiplier=1))
            wide = same_group[:, :].rearrange("p (g c) -> p g c", c=GROUP)
            make(g.affine_select(out=wide, in_=wide, compare_op=ALU.is_ge, fill=0.0,
                                 base=0, pattern=[[-GROUP, P // GROUP], [0, GROUP]], channel_multiplier=1))
            pool.wait_ge(c_made, made[0])
            make(g.affine_select(out=wide, in_=wide, compare_op=ALU.is_ge, fill=0.0, base=GROUP - 1,
                                 pattern=[[GROUP, P // GROUP], [0, GROUP]], channel_multiplier=-1))
            assert made[0] == CONSTANTS

            def rsqrt(dst, src):
                return g.tensor_tensor(dst, src, minus_half[:, 0:src.shape[1]], ALU.pow)

            def group_norm(b):
                pool.wait_ge(gn_pow_in, at(b, 1, 1))
                rsqrt(gn_r[:, :], gn_var[:, :]).then_inc(gn_pow_out, 1)

            def first_norm(b):
                for i in range(NT):
                    pool.wait_ge(ln_in, at(b, NT, i + 1))
                    rsqrt(ln_r[:, i:i + 1], ln_eps[:, i:i + 1]).then_inc(ln_out, 1)

            TL_OWN = 8 + 2

            def last_norms(b):
                n = [0]

                def own_step(ins):
                    n[0] += 1
                    ins.then_inc(tl_own, 1)
                    pool.wait_ge(tl_own, at(b, TL_OWN, n[0]))

                def scale(which, h):
                    c = slice(4 * h, 4 * h + 4)
                    pool.wait_ge(tl_in, at(b, 4, 2 * which + h + 1))
                    own_step(rsqrt(tl_r[:, which, c], tl_eps[:, which, c]))
                    own_step(g.tensor_tensor(tl_mr[:, which, c], tl_mv[:, which, c, 0], tl_r[:, which, c], ALU.mult))
                    g.tensor_tensor(tl_nb[:, which, c], tl_mr[:, which, c], minus_one[:, 0:4],
                                    ALU.mult).then_inc(tl_out, 1)

                def stream(h):
                    c = slice(4 * h, 4 * h + 4)
                    pool.wait_ge(x2_done, at(b, 2, h + 1))
                    g.tensor_tensor(tok[:, c, :], tok[:, c, :], x2[:, c, :], ALU.add).then_inc(r_ready, 1)

                def affine(h):
                    c = slice(4 * h, 4 * h + 4)
                    pool.wait_ge(xf_norm, at(b, 2, h + 1))
                    own_step(g.tensor_tensor(xf[:, c, :], xf[:, c, :],
                                             g_row[:, :].unsqueeze(1).to_broadcast((P, 4, C)), ALU.mult))
                    g.tensor_tensor(xf[:, c, :], xf[:, c, :],
                                    b_row[:, :].unsqueeze(1).to_broadcast((P, 4, C)), ALU.add).then_inc(xf_ready, 1)

                scale(0, 0)
                scale(0, 1)
                stream(0)
                scale(1, 0)
                stream(1)
                scale(1, 1)
                affine(0)
                affine(1)
                assert n[0] == TL_OWN

            def image(b, first, last):
                if not first:
                    last_norms(b - 1)
                first_norm(b)
                if not last:
                    group_norm(b + 1)

            group_norm(0)
            image(0, True, False)
            with pool.Fori(1, B - 1) as b:
                image(b, False, False)
            image(B - 1, False, True)
            last_norms(B - 1)
            pool.wait_ge(xf_ready, 2 * B)
            pool.sem_inc(pool_end, 1)

            ends(pool, 1, (pe_end, act_end, dve_end, sp_end))
            g.iota(iota_i[:, :], pattern=[[1, P]], base=0, channel_multiplier=0).then_inc(num_done, 1)
            g.iota(number_i[:, :], pattern=[[P, TILES]], base=1, channel_multiplier=1).then_inc(num_done, 1)
            g.affine_select(out=before[:, :], in_=ones[:, :], compare_op=ALU.is_gt, fill=0.0,
                            base=0, pattern=[[1, P]], channel_multiplier=-1).then_inc(num_done, 1)
            pool.wait_ge(num_done, 3)
            g.tensor_copy(iota[:, :], iota_i[:, :]).then_inc(num_done, 1)
            g.tensor_copy(number[:, :], number_i[:, :]).then_inc(num_done, 1)
            pool.wait_ge(tables, 4)

            def gather(s, n, first):
                if not first:
                    pool.wait_ge(xt_mm, at(s, 1, -1))
                    pool.sem_inc(pool_held, 1)
                g.tensor_copy(now_g[:, n, :], gather_at[:, bass.ds(s * SUB, SUB)]).then_inc(idx_g, 1)
                pool.wait_ge(idx_g, at(s, 1, 1))
                pool.sem_inc(pool_held, 1)
                for h in range(SUB):
                    g.indirect_dma_start(out=xg[:, n, h, :], out_offset=None, in_=xf_d,
                                         in_offset=bass.IndirectOffsetOnAxis(ap=now_g[:, n, h:h + 1], axis=0),
                                         bounds_check=TOK - 1, oob_is_err=True).then_inc(g_in[n], 16)

            def scatter(s, n, first):
                g.tensor_copy(now_s[:, n, :], scatter_at[:, bass.ds(s * SUB, SUB)]).then_inc(idx_s, 1)
                pool.wait_ge(idx_s, at(s, 1, 1))
                pool.wait_ge(y_act, at(s, 1, 1))
                if not first:
                    pool.wait_ge(added, at(s, SUB * 16, 0))
                pool.sem_inc(y_free, 1)
                for h in range(SUB):
                    g.indirect_dma_start(out=acc_d, out_offset=bass.IndirectOffsetOnAxis(
                        ap=now_s[:, n, h:h + 1], axis=0), in_=y_w[:, n, h, :], in_offset=None,
                        bounds_check=TOK - 1, oob_is_err=False, compute_op=ALU.add).then_inc(added, 16)

            def lo_pieces(s, n, u):
                if isinstance(s, int) and s < 2:
                    split_w2(s, n, u)
                    return
                with pool.If(pool.value_load(fresh[0:1, bass.ds(s, 1)], min_val=0, max_val=1) == 1):
                    split_w2(s, n, u)
                with pool.Else():
                    pool.wait_ge(ws_pool, at(s, 4, 0))
                    pool.sem_inc(ws_pool, 4)

            def split_w2(s, n, u):
                pool.wait_ge(w2_in[n], at(u, 16, 16))
                if not (isinstance(s, int) and s < 2):
                    pool.wait_ge(y_mm, at(s, FC, -FC))
                for f in range(4, 8):
                    pool.wait_ge(ws_act, at(s, 8, f + 1))
                    c = slice((2 * (f - 4)) * C, (2 * (f - 4) + 2) * C)
                    g.tensor_tensor(w2s[n][1][:, :, :].rearrange("p f c -> p (f c)")[:, c], w2r[:, n, c],
                                    w2s[n][0][:, :, :].rearrange("p f c -> p (f c)")[:, c].bitcast(F32),
                                    ALU.subtract).then_inc(ws_pool, 1)

            gather(0, 0, True)
            gather(1, 1, True)
            lo_pieces(0, 0, 0)

            def steps(i, first, last):
                for n in range(2):
                    s = i * 2 + n
                    if not last:
                        gather(s + 2, n, False)
                    if not (first and n == 0):
                        scatter(s - 1, 1 - n, first)
                    if not (last and n == 1):
                        lo_pieces(s + 1, 1 - n, (i if n == 0 else i + 1))

            steps(0, True, False)
            with pool.Fori(1, STEPS // 2 - 1) as i:
                steps(i, False, False)
            steps(STEPS // 2 - 1, False, True)
            scatter(STEPS - 1, 1, False)

        @block.scalar
        def _(act):
            a = nc.scalar
            act.wait_ge(w_in, RAW_IN + ROW_IN - 16)
            flat_h = wh[:, :, :, :].rearrange("p w k c -> p w (k c)")
            a.mul(raw[:, 0, :], raw[:, 0, :], C ** -0.5).then_inc(w_hi, 1)
            a.mul(qk_bias[:, 0:KC], qk_bias[:, 0:KC], C ** -0.5).then_inc(w_hi, 1)
            act.wait_ge(w_hi, 1)
            a.copy(flat_h[:, 0:DIRECT, :], raw[:, 0:DIRECT, :]).then_inc(w_hi, 1)
            for n, w in enumerate((VO, QA, KA, VA)):
                act.wait_ge(w_fold, n + 1)
                if w == VA:
                    a.copy(raw_vo[:, :], bank(n)).then_inc(vo_ready, 1)
                a.copy(flat_h[:, w, :], bank(n)).then_inc(w_hi, 1)
            act.wait_ge(w_fold, 5)
            a.copy(flat_h[:, VB, :], bank(4)).then_inc(w_hi, 1)

            def norm_hi(b, k):
                act.wait_ge(xn_done, at(b, KC, k + 1))
                a.copy(xs[0][:, k, :], xn[:, k, :]).then_inc(xn_hi, 1)

            def tail_norm(b, which, h):
                src, dst, ready = ((tok, x2, x2_done), (x2, xf, xf_norm))[which]
                act.wait_ge(tl_out, at(b, 4, 2 * which + h + 1))
                for j in range(4 * h, 4 * h + 4):
                    ins = a.activation(dst[:, j, :], src[:, j, :], ACT.Identity,
                                       bias=tl_nb[:, which, j:j + 1], scale=tl_r[:, which, j:j + 1])
                ins.then_inc(ready, 1)

            def gate_columns(b, h):
                act.wait_ge(xf_mm, at(b, 2, h + 1))
                a.copy(xfT[:, :, h * HALF:(h + 1) * HALF],
                       bank(2 * h, count=2).rearrange("p (k t) -> p k t", k=KC)).then_inc(xf_col, 1)

            def image(b, first, last):
                def w(s, per, n):
                    act.wait_ge(s, at(b, per, n))

                for gi in range(PJ):
                    w(pj_mm, PJ, gi + 1)
                    if gi < 8:
                        q, n, m = gi // 4, gi % 4 // 2, gi % 2
                        dst = (qs, ks)[q][0][:, m, n * HALF:(n + 1) * HALF]
                        a.activation(dst, bank(gi % 4), ACT.Identity,
                                     bias=qk_bias[:, 2 * q + m:2 * q + m + 1]).then_inc(pj_hi, 1)
                    else:
                        j = gi - 8
                        a.copy(vs[0][:, 2 * j:2 * j + 2, :].rearrange("p j c -> p (j c)"),
                               bank(gi % 4)).then_inc(pj_hi, 1)
                    if not first and gi in ACT_TAIL:
                        tail_norm(b - 1, *ACT_TAIL[gi])

                def exp1(i):
                    w(s_max, NT, i + 1)
                    if i >= 2:
                        w(pt_mm, NT, i - 1)
                    a.activation(prob[:, i % 2, :], bank(2 * (i % 2), count=2), ACT.Exp,
                                 bias=neg_max[:, i:i + 1], accum_out=row_sum[:, i:i + 1]).then_inc(p_exp, 1)

                def hi1(i):
                    w(pt_mm, NT, i + 1)
                    if i >= 2:
                        w(av_mm, NT, i - 1)
                    a.copy(pr[0][:, i % 2, :], bank(4, count=2)).then_inc(pt_hi, 1)

                def hi_tn(h):
                    w(tn_mm, 2, h + 1)
                    a.copy(xs[0][:, :, h * HALF:(h + 1) * HALF],
                           bank(2 * h, count=2).rearrange("p (k t) -> p k t", k=KC)).then_inc(tn_hi, 1)

                exp1(0)
                exp1(1)
                for i in range(NT):
                    hi1(i)
                    if i + 2 < NT:
                        exp1(i + 2)
                hi_tn(0)

                n_u = 0
                for gi, (kind, o, n, m) in enumerate(R):
                    w(r_mm, RG, gi + 1)
                    src = bank(R_BANKS[gi % 4])
                    if kind == "u":
                        if n_u >= 2:
                            prior = [j for j in range(gi) if R[j][0] == "u"][-2]
                            w(r_dve, RD, R_DVE[prior])
                        a.activation(prob[:, n_u % 2, 0:HALF], src, ACT.Silu).then_inc(r_act, 1)
                        n_u += 1
                    elif kind == "p":
                        a.copy((qs, ks)[o][0][:, m, n * HALF:(n + 1) * HALF], src).then_inc(r_act, 1)
                    else:
                        a.copy(v32[:, 2 * n:2 * n + 2, :].rearrange("p j c -> p (j c)"), src).then_inc(r_act, 1)
                    if gi == TN_AT - 1:
                        hi_tn(1)
                    if not first and gi in (GATE_AT, GATE_AT + 1):
                        gate_columns(b - 1, gi - GATE_AT)

                def exp2(i):
                    w(s2_max, NT, i + 1)
                    if i >= 2:
                        w(p2_lo, NT, i - 1)
                    a.activation(prob[:, i % 2, :], bank(2 * (i % 2), count=2), ACT.Exp,
                                 bias=neg_max[:, i:i + 1], accum_out=row_sum[:, i:i + 1]).then_inc(p2_exp, 1)

                def hi2(i):
                    w(p2_exp, NT, i + 1)
                    if i >= 2:
                        w(av2_mm, NT, i - 1)
                    a.copy(pr[0][:, i % 2, :], prob[:, i % 2, :]).then_inc(p2_hi, 1)

                for i in range(NT):
                    exp2(i)
                    hi2(i)
                    if not last and i in (3, 4):
                        norm_hi(b + 1, i - 3)

            for k in range(KC):
                norm_hi(0, k)
            image(0, True, False)
            with act.Fori(1, B - 1) as b:
                image(b, False, False)
            image(B - 1, False, True)
            act.wait_ge(xf_out, (B - 1) * 16)
            for which in range(2):
                for h in range(2):
                    tail_norm(B - 1, which, h)
            for h in range(2):
                gate_columns(B - 1, h)
            act.wait_ge(xf_col, 2 * B)
            act.sem_inc(act_end, 1)

            act.wait_ge(top_done, 2)
            a.activation(exps[:, :, :], scratch[:, :, :], ACT.Exp).then_inc(exp_done, 1)

            act.wait_ge(tables, 4)

            def w_piece(s, n, u, f):
                first = isinstance(s, int) and s < 2
                if f < 4:
                    if f == 0:
                        act.wait_ge(w1_in[n], at(u, 16, 16))
                        if not first:
                            act.wait_ge(h_mm, at(s, FC, -FC))
                    dst = w1s[n][0][:, :, :].rearrange("p k f -> p (k f)")
                    src = w1r
                else:
                    if f == 4:
                        act.wait_ge(w2_in[n], at(u, 16, 16))
                        if not first:
                            act.wait_ge(y_mm, at(s, FC, -FC))
                    dst = w2s[n][0][:, :, :].rearrange("p f c -> p (f c)")
                    src = w2r
                c = slice((f % 4) * 512, (f % 4 + 1) * 512)
                a.copy(dst[:, c], src[:, n, c]).then_inc(ws_act, 1)

            def x_hi(s, n):
                act.wait_ge(xt_mm, at(s, 1, 1))
                a.copy(xt[n][0][:, :, :].rearrange("p k t -> p (k t)"), bank(6)).then_inc(xt_hi, 1)

            for f in range(8):
                w_piece(0, 0, 0, f)
            x_hi(0, 0)

            def steps(i, first, last):
                for n in range(2):
                    s = i * 2 + n
                    act.wait_ge(b_in[n], at(i, 32, 32))
                    if last and n == 1:
                        chunks(i, n, first, last, False)
                    elif first and n == 0:
                        chunks(i, n, first, last, True)
                    else:
                        with act.If(act.value_load(fresh[0:1, bass.ds(s + 1, 1)], min_val=0, max_val=1) == 1):
                            chunks(i, n, first, last, True)
                        with act.Else():
                            act.wait_ge(ws_act, at(s, 8, 8))
                            act.sem_inc(ws_act, 8)
                            chunks(i, n, first, last, False)

            def chunks(i, n, first, last, split):
                if True:
                    s = i * 2 + n
                    for f in range(FC):
                        gi = n * FC + f
                        act.wait_ge(h_mm, at(i, 2 * FC, gi + 1))
                        if not (first and gi < 4):
                            act.wait_ge(h_lo, at(i, 2 * FC, gi - 3))
                        a.activation(h32[:, gi % 4, :], bank(gi % 4, STEP), ACT.Gelu,
                                     bias=b1t[:, n, f:f + 1]).then_inc(h_act, 1)
                        if split:
                            w_piece(s + 1, 1 - n, (i if n == 0 else i + 1), f)
                        if f == 4 and not (last and n == 1):
                            x_hi(s + 1, 1 - n)
                        if f == 3 and not (first and n == 0):
                            y_scale(s - 1, 1 - n, first)

            def y_scale(s, n, first):
                act.wait_ge(y_dve, at(s, 1, 1))
                if not first:
                    act.wait_ge(y_free, at(s, 1, 0))
                for h in range(SUB):
                    ins = a.activation(y_w[:, n, h, :], y_b[:, h, :], ACT.Copy,
                                       scale=slot_w[:, bass.ds(s * SUB + h, 1)])
                ins.then_inc(y_act, 1)

            steps(0, True, False)
            with act.Fori(1, STEPS // 2 - 1) as i:
                steps(i, False, False)
            steps(STEPS // 2 - 1, False, True)
            y_scale(STEPS - 1, 1, False)
            act.wait_ge(y_act, STEPS)
            act.sem_inc(act_end, 1)

            for gi in range(TILES // 4):
                act.wait_ge(o_mm, gi + 1)
                if gi >= 2:
                    act.wait_ge(o_out[gi % 2], gi // 2 * 16)
                a.copy(cols_out[:, gi % 2, 0, :], bank(2 * (gi % 2))).then_inc(o_act, 1)

        def route(dve, v):
            done = [0]

            def step(ins):
                done[0] += 1
                ins.then_inc(own_r, 1)

            def settle():
                dve.wait_ge(own_r, done[0])

            def wide(a):
                return a.unsqueeze(2).to_broadcast((P, TILES, E))

            for t in range(TILES):
                step(v.max(top8[:, t, :], logits[:, t, :]))
            settle()
            v.tensor_tensor(scratch[:, :, :], logits[:, :, :], wide(top8[:, :, 0]), ALU.subtract).then_inc(top_done, 1)
            for t in range(TILES):
                step(v.max_index(top_i[:, t, :], top8[:, t, :], logits[:, t, :]))
            settle()
            v.tensor_copy(top_f[:, :, :], top_i[:, :, :]).then_inc(top_done, 1)
            dve.wait_ge(top_done, 2)
            dve.wait_ge(num_done, 5)
            experts = iota[:, 0:E].unsqueeze(1).to_broadcast((P, TILES, E))
            for k in range(2):
                step(v.tensor_tensor(is_top[k][:, :, :], wide(top_f[:, :, k]), experts, ALU.is_equal))
            settle()
            v.tensor_tensor(either[:, :, :], is_top[0][:, :, :], is_top[1][:, :, :], ALU.add).then_inc(top_done, 1)
            dve.wait_ge(exp_done, 1)
            step(v.tensor_reduce(zsum[:, :], exps[:, :, :], AXX, ALU.add))
            settle()
            step(v.reciprocal(zinv[:, :], zsum[:, :]))
            for k in range(2):
                settle()
                step(v.tensor_tensor(scratch[:, :, :], exps[:, :, :], is_top[k][:, :, :], ALU.mult))
                settle()
                step(v.tensor_reduce(top_w[k][:, :], scratch[:, :, :], AXX, ALU.add))
                settle()
                step(v.tensor_tensor(top_w[k][:, :], top_w[k][:, :], zinv[:, :], ALU.mult))
            dve.wait_ge(rank_mm, 1)
            tile_n = bank(1, TILES * E).rearrange("p (t e) -> p t e", e=E)
            step(v.memset(prefix[0][:, 0:1, :], 0.0))
            step(v.tensor_copy(prefix[0][:, 1:TILES, :], tile_n[:, 0:TILES - 1, :]))
            src, d = 0, 1
            while d < TILES:
                settle()
                step(v.tensor_copy(prefix[1 - src][:, 0:d, :], prefix[src][:, 0:d, :]))
                step(v.tensor_tensor(prefix[1 - src][:, d:, :], prefix[src][:, d:, :],
                                     prefix[src][:, :TILES - d, :], ALU.add))
                src, d = 1 - src, 2 * d
            settle()
            step(v.tensor_tensor(cnt_f[:, :], prefix[src][:, TILES - 1, :], tile_n[:, TILES - 1, :], ALU.add))
            settle()
            step(v.tensor_scalar(cnt_i[:, :], cnt_f[:, :], float(STEP - 1), None, ALU.add))
            settle()
            shift = STEP.bit_length() - 1
            step(v.tensor_single_scalar(cnt_s[:, :], cnt_i[:, :], shift, ALU.logical_shift_right))
            settle()
            step(v.tensor_copy(need[:, :], cnt_s[:, :]))
            settle()
            step(v.tensor_copy(ends_t[0][:, :], need[:, :]))
            es_, d = 0, 1
            while d < E:
                settle()
                step(v.tensor_copy(ends_t[1 - es_][:, 0:d], ends_t[es_][:, 0:d]))
                step(v.tensor_tensor(ends_t[1 - es_][:, d:], ends_t[es_][:, d:], ends_t[es_][:, :E - d], ALU.add))
                es_, d = 1 - es_, 2 * d
            settle()
            step(v.tensor_tensor(base[:, :], ends_t[es_][:, :], need[:, :], ALU.subtract))
            settle()
            step(v.tensor_scalar(base[:, :], base[:, :], float(STEP), None, ALU.mult))
            step(v.tensor_tensor(past[:, :, :], iota[:, 0:STEPS].unsqueeze(2).to_broadcast((P, STEPS, E)),
                                 ends_t[es_][:, :].unsqueeze(1).to_broadcast((P, STEPS, E)), ALU.is_ge))
            settle()
            step(v.tensor_reduce(expert_f[:, :], past[:, :, :], AXX, ALU.add))
            settle()
            v.tensor_scalar(expert_of[:, :], expert_f[:, :], float(E - 1), None, ALU.min).then_inc(tables, 1)
            dve.wait_ge(tables, 1)
            v.tensor_tensor(fresh[:, 2:STEPS], expert_of[:, 2:STEPS], expert_of[:, 0:STEPS - 2],
                            ALU.not_equal).then_inc(tables, 1)
            rank = bank(0, TILES * E).rearrange("p (t e) -> p t e", e=E)
            step(v.tensor_tensor(slot_all[:, :, :], rank, prefix[src][:, :, :], ALU.add))
            settle()
            step(v.tensor_tensor(slot_all[:, :, :], slot_all[:, :, :],
                                 base[:, :].unsqueeze(1).to_broadcast((P, TILES, E)), ALU.add))
            for k in range(2):
                settle()
                step(v.tensor_tensor(scratch[:, :, :], slot_all[:, :, :], is_top[k][:, :, :], ALU.mult))
                settle()
                step(v.tensor_reduce(slot_f[k][:, :], scratch[:, :, :], AXX, ALU.add))
                settle()
                step(v.tensor_copy(slot_i[k][:, :], slot_f[k][:, :]))
                settle()
                step(v.tensor_single_scalar(lo_i[k][:, :], slot_i[k][:, :], P - 1, ALU.bitwise_and))
                step(v.tensor_single_scalar(hi_i[k][:, :], slot_i[k][:, :], 7, ALU.logical_shift_right))
                settle()
                step(v.tensor_copy(lo_f[k][:, :], lo_i[k][:, :]))
                step(v.tensor_copy(hi_f[k][:, :], hi_i[k][:, :]))
            settle()
            for j in range(2 * TILES):
                t, k = j // 2, j % 2
                if j >= 4:
                    dve.wait_ge(pick_mm, j - 3)
                v.tensor_scalar(pick_lo[:, j % 4, :], iota[:, :], lo_f[k][:, t:t + 1], None, ALU.is_equal)
                v.tensor_scalar(pick_hi[:, j % 4, 0, :], iota[:, 0:COLS], hi_f[k][:, t:t + 1],
                                number[:, t:t + 1], ALU.is_equal, ALU.mult)
                v.tensor_scalar(pick_hi[:, j % 4, 1, :], iota[:, 0:COLS], hi_f[k][:, t:t + 1],
                                top_w[k][:, t:t + 1], ALU.is_equal, ALU.mult).then_inc(pick_done, 1)
            dve.wait_ge(pick_mm, 2 * TILES)
            v.tensor_copy(slot_w[:, :], bank(2)[:, COLS:2 * COLS]).then_inc(tables, 1)
            step(v.tensor_scalar(at_f[:, :], bank(2)[:, 0:COLS], -1.0, None, ALU.add))
            settle()
            step(v.tensor_scalar(gather_at[:, :], at_f[:, :], 0.0, None, ALU.max))
            step(v.tensor_scalar(at_m[:, :], at_f[:, :], 0.0, float(SKIP), ALU.is_lt, ALU.mult))
            settle()
            v.tensor_tensor(scatter_at[:, :], at_f[:, :], at_m[:, :], ALU.add).then_inc(tables, 1)

        @block.vector
        def _(dve):
            v = nc.vector
            count = [0]
            before_turn = [0]

            def step(ins):
                count[0] += 1
                ins.then_inc(own, 1)

            def settle():
                dve.wait_ge(own, before_turn[0] + count[0])

            def settle_aggr():
                settle()
                v.memset(spare[:, :], 0.0)

            flat_h = wh[:, :, :, :].rearrange("p w k c -> p w (k c)")
            flat_l = wl[:, :, :, :].rearrange("p w k c -> p w (k c)")
            dve.wait_ge(w_in, RAW_IN + ROW_IN - 16)
            dve.wait_ge(c_made, CONSTANTS)
            for k in range(KC):
                v.tensor_scalar(vb_wide[:, k, :], ones[:, :], vb_col[:, k:k + 1], None,
                                ALU.mult).then_inc(vb_ready, 1)
            dve.wait_ge(w_hi, 3)
            v.tensor_tensor(flat_l[:, 0:DIRECT, :], raw[:, 0:DIRECT, :],
                            flat_h[:, 0:DIRECT, :].bitcast(F32), ALU.subtract).then_inc(w_lo, 1)
            for n, w in enumerate((VO, QA, KA, VA, VB)):
                dve.wait_ge(w_hi, 4 + n)
                v.tensor_tensor(flat_l[:, w, :], bank(n), flat_h[:, w, :].bitcast(F32),
                                ALU.subtract).then_inc(w_lo, 1)
            dve.wait_ge(w_fold, 6)
            step(v.tensor_tensor(o_row[:, :], bank(5, C), o_row[:, :], ALU.add))
            settle()

            def group_stats(b, at_bank, part):
                def w(s, per, n):
                    dve.wait_ge(s, at(b, per, n))

                if part == 0:
                    w(x_in, 16, 16)
                    for k in range(KC):
                        for h in range(2):
                            step(v.bn_stats(gn_bn[:, k, h, :], xn[:, k, h * HALF:(h + 1) * HALF]))
                    settle_aggr()
                    for k in range(KC):
                        ins = v.bn_aggr(gn_mv[:, k, :], gn_bn[:, k, :, :].rearrange("p h s -> p (h s)"))
                    ins.then_inc(gn_stat, 1)
                elif part == 1:
                    w(gn_mm, 2, 1)
                    step(v.tensor_copy(gn_avg[:, :, :],
                                       bank(at_bank)[:, 0:2 * KC].rearrange("p (k s) -> p k s", k=KC)))
                    settle()
                    step(v.tensor_tensor(gn_d[:, :], gn_mv[:, :, 0], gn_avg[:, :, 0], ALU.subtract))
                    settle()
                    v.tensor_tensor(gn_d2[:, :], gn_d[:, :], gn_d[:, :], ALU.mult).then_inc(gn_stat, 1)
                elif part == 2:
                    w(gn_mm, 2, 2)
                    v.scalar_tensor_tensor(gn_var[:, :], bank(at_bank)[:, 8:8 + KC], GN_EPS, gn_avg[:, :, 1],
                                           ALU.add, ALU.add).then_inc(gn_pow_in, 1)
                else:
                    w(gn_pow_out, 1, 1)
                    step(v.tensor_tensor(gn_s[:, :], gn_r[:, :], gn_aff[:, 0:KC], ALU.mult))
                    settle()
                    step(v.tensor_tensor(gn_t[:, :], gn_avg[:, :, 0], gn_s[:, :], ALU.mult))
                    settle()
                    step(v.tensor_tensor(gn_t[:, :], gn_aff[:, KC:2 * KC], gn_t[:, :], ALU.subtract))
                    settle()

            def group_apply(b, k):
                v.tensor_scalar(xn[:, k, :], xn[:, k, :], gn_s[:, k:k + 1], gn_t[:, k:k + 1],
                                ALU.mult, ALU.add).then_inc(xn_done, 1)

            def group_lo(b, k):
                dve.wait_ge(xn_hi, at(b, KC, k + 1))
                v.tensor_tensor(xs[1][:, k, :], xn[:, k, :], xs[0][:, k, :].bitcast(F32),
                                ALU.subtract).then_inc(xn_lo, 1)

            def tail_add(b):
                dve.wait_ge(av2_mm, at(b, NT, NT))
                for m in range(4):
                    tile = tok[:, 2 * m:2 * m + 2, :].rearrange("p j c -> p (j c)")
                    ins = v.tensor_tensor(tile, bank(4 + m), tile, ALU.add)
                ins.then_inc(added2, 1)

            def tail_stats(b, which, h):
                if which:
                    dve.wait_ge(x2_done, at(b, 2, h + 1))
                else:
                    dve.wait_ge(added2, at(b, 1, 1))
                src = (tok, x2)[which]
                c = range(4 * h, 4 * h + 4)
                for i in c:
                    step(v.bn_stats(tl_bn[:, which, i, :], src[:, i, :]))
                settle_aggr()
                for i in c:
                    step(v.bn_aggr(tl_mv[:, which, i, :], tl_bn[:, which, i, :]))
                settle()
                v.tensor_scalar(tl_eps[:, which, 4 * h:4 * h + 4], tl_mv[:, which, 4 * h:4 * h + 4, 1], LN_EPS,
                                None, ALU.add).then_inc(tl_in, 1)

            def gate_read(b):
                dve.wait_ge(g_mm, at(b, 1, 1))
                step(v.tensor_copy(logits[:, bass.ds(b * NT, NT), :].rearrange("p t e -> p (t e)"),
                                   bank(0)[:, 0:NT * E]))

            def image(b, first, last):
                def w(s, per, n):
                    dve.wait_ge(s, at(b, per, n))

                if not first:
                    tail_add(b - 1)
                for gi in range(PJ):
                    w(pj_hi, PJ, gi + 1)
                    if gi < 8:
                        q, n, m = gi // 4, gi % 4 // 2, gi % 2
                        c = slice(n * HALF, (n + 1) * HALF)
                        v.scalar_tensor_tensor((qs, ks)[q][1][:, m, c], bank(gi % 4),
                                               qk_bias[:, 2 * q + m:2 * q + m + 1],
                                               (qs, ks)[q][0][:, m, c].bitcast(F32),
                                               ALU.add, ALU.subtract).then_inc(pj_lo, 1)
                    else:
                        j = gi - 8
                        v.tensor_tensor(vs[1][:, 2 * j:2 * j + 2, :].rearrange("p j c -> p (j c)"),
                                        bank(gi % 4),
                                        vs[0][:, 2 * j:2 * j + 2, :].rearrange("p j c -> p (j c)").bitcast(F32),
                                        ALU.subtract).then_inc(pj_lo, 1)
                    if not first and gi in DVE_TAIL:
                        tail_stats(b - 1, *DVE_TAIL[gi])

                def max1(i):
                    w(s_mm, NT, i + 1)
                    v.tensor_reduce(neg_max[:, i:i + 1], bank(2 * (i % 2), count=2), AXX, ALU.max,
                                    negate=True).then_inc(s_max, 1)

                def lo1(i):
                    w(pt_hi, NT, i + 1)
                    v.tensor_tensor(pr[1][:, i % 2, :], bank(4, count=2), pr[0][:, i % 2, :].bitcast(F32),
                                    ALU.subtract).then_inc(pt_lo, 1)
                    step(v.reciprocal(row_inv[:, i:i + 1], row_sum[:, i:i + 1]))

                def out1(i):
                    w(av_mm, NT, i + 1)
                    if i == 0 and not first:
                        w(tok_out, 16, 0)
                    step(v.tensor_tensor(tok[:, i, :], bank(6 + i % 2)[:, C:2 * C], o_row[:, :], ALU.add))
                    settle()
                    v.scalar_tensor_tensor(tok[:, i, :], bank(6 + i % 2)[:, 0:C], row_inv[:, i:i + 1],
                                           tok[:, i, :], ALU.mult, ALU.add).then_inc(t_done, 1)
                    w(t_done, NT, i + 1)
                    step(v.bn_stats(ln_bn[:, i, :], tok[:, i, :]))
                    settle_aggr()
                    step(v.bn_aggr(ln_mv[:, i, :], ln_bn[:, i, :]))
                    settle()
                    v.tensor_scalar(ln_eps[:, i:i + 1], ln_mv[:, i, 1:2], LN_EPS, None,
                                    ALU.add).then_inc(ln_in, 1)

                def norm1(i):
                    w(ln_out, NT, i + 1)
                    v.tensor_scalar(tn[:, i, :], tok[:, i, :], ln_mv[:, i, 0:1], ln_r[:, i:i + 1],
                                    ALU.subtract, ALU.mult).then_inc(tn_tok, 1)

                def lo_tn(h):
                    w(tn_hi, 2, h + 1)
                    c = slice(h * HALF, (h + 1) * HALF)
                    v.tensor_tensor(xs[1][:, :, c], bank(2 * h, count=2).rearrange("p (k t) -> p k t", k=KC),
                                    xs[0][:, :, c].bitcast(F32), ALU.subtract).then_inc(tn_lo, 1)

                max1(0)
                max1(1)
                for i in range(NT):
                    lo1(i)
                    if i + 2 < NT:
                        max1(i + 2)
                    if i >= 1:
                        out1(i - 1)
                    if i >= 2:
                        norm1(i - 2)
                lo_tn(0)
                norm1(NT - 2)
                out1(NT - 1)
                norm1(NT - 1)
                if not first:
                    w(xf_ready, 2, 0)

                n_u = 0
                for gi, (kind, o, n, m) in enumerate(R):
                    if kind != "v":
                        w(r_act, RG, gi + 1)
                    c = slice(n * HALF, (n + 1) * HALF)
                    if kind == "u":
                        dst = us[o % 2]
                        step(v.tensor_copy(dst[0][:, m, c], prob[:, n_u % 2, 0:HALF]))
                        settle()
                        v.tensor_tensor(dst[1][:, m, c], prob[:, n_u % 2, 0:HALF], dst[0][:, m, c].bitcast(F32),
                                        ALU.subtract).then_inc(r_dve, 1)
                        n_u += 1
                    elif kind == "p":
                        v.tensor_tensor((qs, ks)[o][1][:, m, c], bank(R_BANKS[gi % 4]),
                                        (qs, ks)[o][0][:, m, c].bitcast(F32), ALU.subtract).then_inc(r_dve, 1)
                    if gi == TN_AT - 1:
                        lo_tn(1)
                    if not last and gi in DVE_GN:
                        group_stats(b + 1, GN_BANK, DVE_GN[gi])
                    if not first and gi == GATE_AT + 4:
                        gate_read(b - 1)
                settle()
                v.memset(spare[:, :], 0.0).then_inc(u_read, 1)

                def max2(i):
                    w(s2_mm, NT, i + 1)
                    v.tensor_reduce(neg_max[:, i:i + 1], bank(2 * (i % 2), count=2), AXX, ALU.max,
                                    negate=True).then_inc(s2_max, 1)

                def lo2(i):
                    w(p2_hi, NT, i + 1)
                    v.tensor_tensor(pr[1][:, i % 2, :], prob[:, i % 2, :], pr[0][:, i % 2, :].bitcast(F32),
                                    ALU.subtract).then_inc(p2_lo, 1)

                def values2(i):
                    w(p2_exp, NT, i + 1)
                    if i >= 2:
                        w(av2_mm, NT, i - 1)
                    step(v.reciprocal(row_inv[:, i:i + 1], row_sum[:, i:i + 1]))
                    settle()
                    step(v.tensor_scalar(vk[0][:, i % 2, :], v32[:, i, :], row_inv[:, i:i + 1], None, ALU.mult))
                    settle()
                    v.scalar_tensor_tensor(vk[1][:, i % 2, :], v32[:, i, :], row_inv[:, i:i + 1],
                                           vk[0][:, i % 2, :].bitcast(F32), ALU.mult,
                                           ALU.subtract).then_inc(v2_done, 1)

                w(r_act, RG, RG)
                max2(0)
                max2(1)
                for i in range(NT):
                    values2(i)
                    lo2(i)
                    if i + 2 < NT:
                        max2(i + 2)
                    if not last:
                        if i in (1, 2):
                            group_apply(b + 1, i - 1)
                        if i in (4, 5):
                            group_lo(b + 1, i - 4)

            for part in range(4):
                group_stats(0, 7, part)
            for k in range(KC):
                group_apply(0, k)
            for k in range(KC):
                group_lo(0, k)
            image(0, True, False)
            before_turn[0], count[0] = before_turn[0] + count[0], 0
            start = before_turn[0]
            with dve.Fori(1, B - 1) as b:
                before_turn[0] = at(b - 1, OWN_IMAGE, start)
                image(b, False, False)
                assert count[0] == OWN_IMAGE, count[0]
            before_turn[0], count[0] = start + (B - 2) * OWN_IMAGE, 0
            image(B - 1, False, True)
            tail_add(B - 1)
            for which in range(2):
                for h in range(2):
                    tail_stats(B - 1, which, h)
            gate_read(B - 1)
            settle()
            dve.sem_inc(dve_end, 1)

            ends(dve, 1, (pe_end, act_end, sp_end, pool_end))
            route(dve, v)

            def w_piece(s, n, u, f):
                first = isinstance(s, int) and s < 2
                if f == 0:
                    dve.wait_ge(w1_in[n], at(u, 16, 16))
                    if not first:
                        dve.wait_ge(h_mm, at(s, FC, -FC))
                dve.wait_ge(ws_act, at(s, 8, f + 1))
                c = slice(f * 512, (f + 1) * 512)
                v.tensor_tensor(w1s[n][1][:, :, :].rearrange("p k f -> p (k f)")[:, c], w1r[:, n, c],
                                w1s[n][0][:, :, :].rearrange("p k f -> p (k f)")[:, c].bitcast(F32),
                                ALU.subtract).then_inc(ws_dve, 1)

            def x_lo(s, n):
                dve.wait_ge(xt_hi, at(s, 1, 1))
                v.tensor_tensor(xt[n][1][:, :, :].rearrange("p k t -> p (k t)"), bank(6),
                                xt[n][0][:, :, :].rearrange("p k t -> p (k t)").bitcast(F32),
                                ALU.subtract).then_inc(xt_lo, 1)

            def y_bias(s, n, first):
                dve.wait_ge(y_mm, at(s, FC, FC))
                if not first:
                    dve.wait_ge(y_act, at(s, 1, 0))
                ins = v.tensor_tensor(y_b[:, :, :], bank(4 + n).rearrange("p (h c) -> p h c", h=SUB),
                                      b2t[:, n:n + 1, :].to_broadcast((P, SUB, C)), ALU.add)
                ins.then_inc(y_dve, 1)

            for f in range(4):
                w_piece(0, 0, 0, f)
            x_lo(0, 0)

            def steps(i, first, last):
                for n in range(2):
                    s = i * 2 + n
                    if last and n == 1:
                        chunks(i, n, first, last, False)
                    elif first and n == 0:
                        chunks(i, n, first, last, True)
                    else:
                        with dve.If(dve.value_load(fresh[0:1, bass.ds(s + 1, 1)], min_val=0, max_val=1) == 1):
                            chunks(i, n, first, last, True)
                        with dve.Else():
                            dve.wait_ge(ws_dve, at(s, 4, 4))
                            dve.sem_inc(ws_dve, 4)
                            chunks(i, n, first, last, False)

            def chunks(i, n, first, last, split):
                if True:
                    s = i * 2 + n
                    for f in range(FC):
                        gi = n * FC + f
                        dve.wait_ge(h_act, at(i, 2 * FC, gi + 1))
                        if not (first and n == 0):
                            dve.wait_ge(y_mm, at(i, 2 * FC, gi + 1 - FC))
                        v.tensor_copy(hs[0][:, f, :], h32[:, gi % 4, :]).then_inc(h_hi, 1)
                        dve.wait_ge(h_hi, at(i, 2 * FC, gi + 1))
                        v.tensor_tensor(hs[1][:, f, :], h32[:, gi % 4, :], hs[0][:, f, :].bitcast(F32),
                                        ALU.subtract).then_inc(h_lo, 1)
                        if f == 2 and not (first and n == 0):
                            y_bias(s - 1, 1 - n, first)
                        if split and f < 4:
                            w_piece(s + 1, 1 - n, (i if n == 0 else i + 1), f)
                        if f == 4 and not (last and n == 1):
                            x_lo(s + 1, 1 - n)

            steps(0, True, False)
            with dve.Fori(1, STEPS // 2 - 1) as i:
                steps(i, False, False)
            steps(STEPS // 2 - 1, False, True)
            y_bias(STEPS - 1, 1, False)
            dve.wait_ge(y_dve, STEPS)
            dve.sem_inc(dve_end, 1)

            for gi in range(TILES // 4):
                dve.wait_ge(o_mm, gi + 1)
                if gi >= 2:
                    dve.wait_ge(o_out[gi % 2], gi // 2 * 16)
                v.tensor_copy(cols_out[:, gi % 2, 1, :], bank(2 * (gi % 2) + 1)).then_inc(o_dve, 1)

        @block.tensor
        def _(pe):
            t = nc.tensor

            def three(out, left, right, first=True, last=True, **more):
                for n, (l, r) in enumerate(PASSES):
                    ins = t.matmul(out, left[l], right[r], start=first and n == 0, stop=last and n == 2, **more)
                return ins

            def weight(slot, k, m):
                return [w[:, slot, k, m * P:(m + 1) * P] for w in (wh, wl)]

            def weight_row(slot, k):
                return [w[:, slot, k, :] for w in (wh, wl)]

            def fold(n, left, right):
                for m in range(KC):
                    for k in range(KC):
                        ins = t.matmul(bank(n)[:, m * C:(m + 1) * C], left[:, k * C + m * P:k * C + (m + 1) * P],
                                       right[:, k * C:(k + 1) * C], start=(k == 0), stop=(k == KC - 1))
                ins.then_inc(w_fold, 1)

            pe.wait_ge(w_in, RAW_IN + ROW_IN - 16)
            fold(0, raw[:, 7, :], raw[:, 8, :])
            fold(1, raw[:, 9, :], raw[:, 5, :])
            fold(2, raw[:, 10, :], raw[:, 6, :])
            fold(3, raw[:, 12, :], raw[:, 13, :])
            pe.wait_ge(vo_ready, 1)
            fold(4, raw[:, 11, :], raw_vo[:, :])
            pe.wait_ge(vb_ready, KC)
            for k in range(KC):
                ins = t.matmul(bank(5, C), vb_wide[:, k, :], raw[:, 8, k * C:(k + 1) * C],
                               start=(k == 0), stop=(k == KC - 1))
            ins.then_inc(w_fold, 1)
            pe.wait_ge(c_made, CONSTANTS)

            def group_average(b, at_bank, part):
                pe.wait_ge(gn_stat, at(b, 2, part + 1))
                if part == 0:
                    t.matmul(bank(at_bank)[:, 0:2 * KC], same_group[:, :],
                             gn_mv[:, :, :].rearrange("p k s -> p (k s)"),
                             start=True, stop=True).then_inc(gn_mm, 1)
                else:
                    t.matmul(bank(at_bank)[:, 8:8 + KC], same_group[:, :], gn_d2[:, :],
                             start=True, stop=True).then_inc(gn_mm, 1)

            def gate_turn(b):
                pe.wait_ge(xf_ready, at(b, 2, 2))
                for h in range(2):
                    for k in range(KC):
                        for j in range(4):
                            ins = t.transpose(bank(2 * h + k)[:, j * P:(j + 1) * P],
                                              xf[:, 4 * h + j, k * P:(k + 1) * P], ident[:, :])
                    ins.then_inc(xf_mm, 1)

            def gate(b):
                for j in range(NT):
                    if j % 4 == 0:
                        pe.wait_ge(xf_col, at(b, 2, j // 4 + 1))
                    for k in range(KC):
                        ins = t.matmul(bank(0)[:, j * E:(j + 1) * E], xfT[:, k, j * P:(j + 1) * P],
                                       gate_sb[:, k, :], start=(k == 0), stop=(k == KC - 1))
                ins.then_inc(g_mm, 1)

            def image(b, first, last):
                def w(s, per, n):
                    pe.wait_ge(s, at(b, per, n))

                w(xn_lo, KC, KC)
                if not first:
                    pe.wait_ge(p2_exp, at(b - 1, NT, NT))
                for gi in range(PJ):
                    if gi >= 4:
                        w(pj_lo, PJ, gi - 3)
                    out = bank(gi % 4)
                    if gi < 8:
                        q, n, m = gi // 4, gi % 4 // 2, gi % 2
                        for k in range(KC):
                            ins = three(out, weight(WQ + q, k, m),
                                        [a[:, k, n * HALF:(n + 1) * HALF] for a in xs], k == 0, k == KC - 1)
                    else:
                        for h in range(2):
                            j = 2 * (gi - 8) + h
                            for k in range(KC):
                                ins = three(out[:, h * C:(h + 1) * C], [a[:, k, j * P:(j + 1) * P] for a in xs],
                                            weight_row(VO, k), k == 0, k == KC - 1)
                    ins.then_inc(pj_mm, 1)
                w(pj_lo, PJ, PJ)

                def scores(i, rows_of, cols_of, signal_):
                    for n in range(NH):
                        for k in range(KC):
                            ins = three(bank(2 * (i % 2) + n), [a[:, k, i * P:(i + 1) * P] for a in rows_of],
                                        [a[:, k, n * HALF:(n + 1) * HALF] for a in cols_of], k == 0, k == KC - 1)
                    ins.then_inc(signal_, 1)

                def turn1(i):
                    w(p_exp, NT, i + 1)
                    if i >= 1:
                        w(pt_lo, NT, i)
                    for j in range(NT):
                        ins = t.transpose(bank(4, count=2)[:, j * P:(j + 1) * P],
                                          prob[:, i % 2, j * P:(j + 1) * P], ident[:, :])
                    ins.then_inc(pt_mm, 1)

                def mix1(i):
                    if i >= 2:
                        w(t_done, NT, i - 1)
                    for k in range(KC):
                        t.transpose(bank(6 + i % 2)[:, C + k * P:C + (k + 1) * P], xn[:, k, i * P:(i + 1) * P],
                                    ident[:, :])
                    w(pt_lo, NT, i + 1)
                    for j in range(NT):
                        ins = three(bank(6 + i % 2)[:, 0:C], [a[:, i % 2, j * P:(j + 1) * P] for a in pr],
                                    [a[:, j, :] for a in vs], j == 0, j == NT - 1)
                    ins.then_inc(av_mm, 1)

                def turn_tn(h):
                    w(tn_tok, NT, 4 * h + 4)
                    for k in range(KC):
                        for j in range(4):
                            ins = t.transpose(bank(2 * h + k)[:, j * P:(j + 1) * P],
                                              tn[:, 4 * h + j, k * P:(k + 1) * P], ident[:, :])
                    ins.then_inc(tn_mm, 1)

                scores(0, qs, ks, s_mm)
                scores(1, qs, ks, s_mm)
                if not first:
                    pe.wait_ge(added2, at(b - 1, 1, 1))
                for i in range(NT):
                    turn1(i)
                    if i + 2 < NT:
                        scores(i + 2, qs, ks, s_mm)
                    if i == NT - 1:
                        turn_tn(0)
                    if i >= 1:
                        mix1(i - 1)
                mix1(NT - 1)

                for gi, (kind, o, n, m) in enumerate(R):
                    if gi == TN_AT:
                        turn_tn(1)
                    if not first and gi == GATE_AT:
                        gate_turn(b - 1)
                    if not first and gi == GATE_AT + 3:
                        gate(b - 1)
                    if not last and gi in PE_GN:
                        if not first:
                            pe.wait_ge(xf_col, at(b - 1, 2, 2))
                        group_average(b + 1, GN_BANK, PE_GN[gi])
                    if gi == 0:
                        w(tn_lo, 2, 1)
                    if gi == 2:
                        w(t_done, NT, 7)
                    if gi == 3:
                        w(t_done, NT, 8)
                    if gi == 4:
                        w(tn_lo, 2, 2)
                    if gi >= 4:
                        w(r_act, RG, gi - 3)
                        if R[gi - 4][0] == "p":
                            w(r_dve, RD, R_DVE[gi - 4])
                    if kind != "u" and R[gi - 1][:2] != R[gi][:2]:
                        w(r_dve, RD, R_DVE[max(j for j in range(gi) if R[j][:2] == ("u", o))])
                    out = bank(R_BANKS[gi % 4])
                    if kind == "u":
                        for k in range(KC):
                            ins = three(out, weight(Q1 + o, k, m),
                                        [a[:, k, n * HALF:(n + 1) * HALF] for a in xs], k == 0, k == KC - 1)
                    elif kind == "p":
                        for k in range(KC):
                            three(out, weight(AQ + o, k, m),
                                  [a[:, k, n * HALF:(n + 1) * HALF] for a in xs], k == 0, False)
                        for k in range(KC):
                            ins = three(out, weight(QA + o, k, m),
                                        [a[:, k, n * HALF:(n + 1) * HALF] for a in us[o % 2]], False, k == KC - 1)
                    else:
                        for h in range(2):
                            j = 2 * n + h
                            for k in range(KC):
                                three(out[:, h * C:(h + 1) * C], [a[:, k, j * P:(j + 1) * P] for a in xs],
                                      weight_row(VA, k), k == 0, False)
                            for k in range(KC):
                                ins = three(out[:, h * C:(h + 1) * C], [a[:, k, j * P:(j + 1) * P] for a in us[0]],
                                            weight_row(VB, k), False, k == KC - 1)
                    ins.then_inc(r_mm, 1)

                def mix2(i):
                    w(p2_lo, NT, i + 1)
                    w(v2_done, NT, i + 1)
                    if i == 0:
                        w(r_act, RG, RG)
                        w(r_dve, RD, RD)
                    for j in range(NT):
                        ins = three(bank(4 + j // 2)[:, j % 2 * C:(j % 2 + 1) * C],
                                    [a[:, i % 2, j * P:(j + 1) * P] for a in pr],
                                    [a[:, i % 2, :] for a in vk], i == 0 and j % 2 == 0, i == NT - 1,
                                    skip_group_check=True)
                    ins.then_inc(av2_mm, 1)

                w(r_dve, RD, RD)
                w(u_read, 1, 1)
                scores(0, ks, qs, s2_mm)
                scores(1, ks, qs, s2_mm)
                for i in range(NT):
                    if i + 2 < NT:
                        w(p2_exp, NT, i + 1)
                        scores(i + 2, ks, qs, s2_mm)
                    mix2(i)

            group_average(0, 7, 0)
            group_average(0, 7, 1)
            pe.wait_ge(w_lo, 6)
            image(0, True, False)
            with pe.Fori(1, B - 1) as b:
                image(b, False, False)
            image(B - 1, False, True)
            pe.wait_ge(p2_exp, B * NT)
            gate_turn(B - 1)
            gate(B - 1)
            pe.wait_ge(g_mm, B)
            pe.sem_inc(pe_end, 1)

            pe.wait_ge(top_done, 3)
            pe.wait_ge(num_done, 3)
            flat = either[:, :, :].rearrange("p t e -> p (t e)")
            t.matmul(bank(0, TILES * E), before[:, :], flat, start=True, stop=True)
            t.matmul(bank(1, TILES * E), ones[:, :], flat, start=True, stop=True).then_inc(rank_mm, 1)
            for j in range(2 * TILES):
                pe.wait_ge(pick_done, j + 1)
                t.matmul(bank(2, 2 * COLS), pick_lo[:, j % 4, :],
                         pick_hi[:, j % 4, :, :].rearrange("p a c -> p (a c)"),
                         start=(j == 0), stop=(j == 2 * TILES - 1)).then_inc(pick_mm, 1)

            pe.wait_ge(tables, 4)

            def x_turn(s, n, u):
                pe.wait_ge(g_in[n], at(u, SUB * 16, SUB * 16))
                if not (isinstance(s, int) and s == 0):
                    pe.wait_ge(xt_lo, at(s, 1, 0))
                for k in range(KC):
                    for h in range(SUB):
                        ins = t.transpose(bank(6)[:, k * STEP + h * P:k * STEP + (h + 1) * P],
                                          xg[:, n, h, k * P:(k + 1) * P], ident[:, :])
                ins.then_inc(xt_mm, 1)

            def first_product(i, s, n, f, new):
                gi = n * FC + f
                if f == 0:
                    pe.wait_ge(xt_lo, at(s, 1, 1))
                    pe.wait_ge(ws_dve, at(s, 4, 4))
                if not (new and gi < 4):
                    pe.wait_ge(h_act, at(i, 2 * FC, gi - 3))
                for k in range(KC):
                    ins = three(bank(gi % 4, STEP), [a[:, k, f * P:(f + 1) * P] for a in w1s[n % 2]],
                                [a[:, k, :] for a in xt[n % 2]], k == 0, k == KC - 1)
                ins.then_inc(h_mm, 1)

            def second_product(i, s, n, f, new):
                gi = n * FC + f
                pe.wait_ge(h_lo, at(i, 2 * FC, gi + 1))
                if f % 2 == 0:
                    pe.wait_ge(ws_act, at(s, 8, 5 + f // 2))
                    pe.wait_ge(ws_pool, at(s, 4, 1 + f // 2))
                if f == 0:
                    if not new:
                        pe.wait_ge(y_dve, at(s, 1, -1))
                for h in range(SUB):
                    ins = three(bank(4 + n)[:, h * C:(h + 1) * C], [a[:, f, h * P:(h + 1) * P] for a in hs],
                                [a[:, f, :] for a in w2s[n]], f == 0 and h == 0, f == FC - 1,
                                skip_group_check=True)
                ins.then_inc(y_mm, 1)

            AHEAD = 2
            x_turn(0, 0, 0)
            for f in range(AHEAD):
                first_product(0, 0, 0, f, True)

            def steps(i, first, last):
                for gi in range(2 * FC):
                    n, f = gi // FC, gi % FC
                    s = i * 2 + n
                    if f == 3 and not (last and n == 1):
                        x_turn(s + 1, 1 - n, (i if n == 0 else i + 1))
                    ahead = gi + AHEAD
                    if not (last and ahead >= 2 * FC):
                        na, fa = ahead // FC, ahead % FC
                        first_product(i, i * 2 + na, na, fa, first)
                    second_product(i, s, n, f, first)

            steps(0, True, False)
            with pe.Fori(1, STEPS // 2 - 1) as i:
                steps(i, False, False)
            steps(STEPS // 2 - 1, False, True)
            pe.wait_ge(y_mm, STEPS * FC)
            pe.sem_inc(pe_end, 1)

            for gi in range(TILES // 4):
                pe.wait_ge(r_in[gi % 2], (gi // 2 + 1) * 16)
                if gi == 0:
                    ends(pe, 2, (act_end, dve_end))
                if gi >= 2:
                    pe.wait_ge(o_act, gi - 1)
                    pe.wait_ge(o_dve, gi - 1)
                for k in range(KC):
                    for j in range(4):
                        ins = t.transpose(bank(2 * (gi % 2) + k)[:, j * P:(j + 1) * P],
                                          rows[:, gi % 2, j, k * P:(k + 1) * P], ident[:, :])
                ins.then_inc(o_mm, 1)


CONSTANTS = 8
OWN_IMAGE = 102


def kernel(**inputs):
    import numpy as np
    import concourse.bacc as bacc
    from concourse.bass_utils import run_bass_kernel_spmd

    a = {k: np.asarray(v) for k, v in inputs.items()}
    x = a["x"]
    B, C, H, W = x.shape

    def chunks(v):
        return v.reshape(-1, P).T

    qkv_w, qkv_b = a["L0_conv_qkv_w"], a["L0_conv_qkv_b"]
    E, F = a["L1_ffn_b1"].shape
    args = {
        "x": x.reshape(B, C, H * W),
        "qT": qkv_w[0:C].T, "kT": qkv_w[C:2 * C].T, "v_w": qkv_w[2 * C:3 * C], "oT": a["L0_conv_out_w"].T,
        "qk_b": chunks(qkv_b[0:2 * C]), "v_b": chunks(qkv_b[2 * C:3 * C]),
        "out_b": a["L0_conv_out_b"].reshape(1, C),
        "gn": np.concatenate([chunks(a["L0_conv_gn_weight"]), chunks(a["L0_conv_gn_bias"])], axis=1),
        "W1": np.stack([a[f"L1_attn_{n}W1"] for n in "qkv"]),
        "W2T": np.stack([a[f"L1_attn_{n}W2"].T for n in "qkv"]),
        "a_qk": np.stack([a["L1_attn_aWq"], a["L1_attn_aWk"]]),
        "a_vT": a["L1_attn_aWv"].T, "Wout": a["L1_attn_Wout"],
        "gate_w": a["L1_ffn_gate_w"], "w1": a["L1_ffn_w1"],
        "b1": a["L1_ffn_b1"].reshape(E, F // P, P).transpose(0, 2, 1),
        "w2": a["L1_ffn_w2"], "b2": a["L1_ffn_b2"],
        "ln_g": a["L1_ffn_ln_g"].reshape(1, C), "ln_b": a["L1_ffn_ln_b"].reshape(1, C),
    }
    nc = bacc.Bacc("TRN2", target_bir_lowering=False, num_devices=1)
    arrays, aps = {}, {}
    for name, v in args.items():
        v = np.ascontiguousarray(v)
        arrays[f"in_{name}"] = v
        aps[name] = nc.dram_tensor(f"in_{name}", v.shape, mybir.dt.from_np(v.dtype), kind="ExternalInput").ap()
    aps["out"] = nc.dram_tensor("out_tokens", (B, C, H * W), F32, kind="ExternalOutput").ap()
    hybrid_block_kernel(nc, **aps)
    r = run_bass_kernel_spmd(nc, [arrays], core_ids=[0])
    return r.results[0]["out_tokens"].reshape(B, C, H, W)
```

```python
from contextlib import ExitStack

import concourse.bass as bass
from concourse import mybir

P = 128
ALU = mybir.AluOpType
ACT = mybir.ActivationFunctionType
AXX = mybir.AxisListType.X
F32 = mybir.dt.float32
F32R = mybir.dt.float32r
I32 = mybir.dt.int32

PASSES = ((0, 0), (0, 1), (1, 0))

Q1, K1, V1, AQ, AK, SQ, VO, VA, QA, KA, VB = range(11)
DIRECT = 5


def at(turn, per_turn, n):
    return turn * per_turn + n


def hybrid_block_kernel(nc, x, q_w, k_w, v_w, oT, q_b, v_b, out_b, gn, W1, W2T, a_qk, a_vT, Wout,
                        gate_w, w1, b1, w2, b2, ln_g, ln_b, out):
    B, C, T = x.shape
    KC = C // P
    NT = T // P
    HALF = 512
    NH = T // HALF
    TOK = B * T
    TILES = TOK // P
    E = gate_w.shape[1]
    FF = w1.shape[2]
    FC = FF // P
    GROUP = C // 32
    STEP = 256
    SUB = STEP // P
    STEPS = TOK * 2 // STEP + E
    COLS = STEPS * SUB
    PAIRS = STEPS // 2
    GN_EPS = LN_EPS = 1e-5
    SKIP = 2 * TOK
    assert KC == 2 and STEPS % 2 == 0 and NT == 8 and NH == 2 and TILES * E == 256

    x_d = x.rearrange("b (k p) t -> b p k t", p=P)
    out_d = out.rearrange("b (k p) t -> b p k t", p=P)
    acc_d = nc.dram_tensor("acc_rows", (TOK, C), F32, kind="Internal").ap()
    xf_d = nc.dram_tensor("xf_rows", (TOK, C), F32, kind="Internal").ap()
    acc_t = acc_d.rearrange("(t p) c -> p t c", p=P)
    xf_t = xf_d.rearrange("(t p) c -> p t c", p=P)
    w1_d = w1.rearrange("e (k p) f -> e p k f", p=P)
    w2_d = w2.rearrange("e (f p) d -> e p f d", p=P)

    ctx = ExitStack()
    with ctx:
        def psum(name, cols):
            return ctx.enter_context(nc.psum_tensor(name, [P, cols], F32))

        def sem(name):
            return ctx.enter_context(nc.semaphore(name))

        def sb(name, shape, dt=F32, scope=ctx):
            return scope.enter_context(nc.sbuf_tensor(name, shape, dt))

        ps = psum("ps", 8 * 512)

        def bank(n, cols=512, count=1):
            return ps[:, n * 512:(n - 1 + count) * 512 + cols]

        ident = sb("ident", [P, P])
        ones = sb("ones", [P, P])
        same_group = sb("same_group", [P, P])
        minus_half = sb("minus_half", [P, 8])
        minus_one = sb("minus_one", [P, 8])
        logits = sb("logits", [P, TILES, E])
        top8 = sb("top8", [P, TILES, 8])
        top_i = sb("top_i", [P, TILES, 8], mybir.dt.uint32)

        batch_scope = ExitStack()

        def bs(name, shape, dt=F32):
            return sb(name, shape, dt, batch_scope)

        wh = bs("wh", [P, VB + 1, KC, C], F32R)
        wl = bs("wl", [P, VB + 1, KC, C], F32R)
        q_bias = bs("q_bias", [P, KC])
        s_bias = bs("s_bias", [P, KC])
        gn_aff = bs("gn_aff", [P, 4])
        o_row = bs("o_row", [P, C])
        g_row = bs("g_row", [P, C])
        b_row = bs("b_row", [P, C])
        gate_sb = bs("gate_sb", [P, KC, E])
        xn = bs("xn", [P, KC, T])
        xs = [bs(f"xs{i}", [P, KC, T], F32R) for i in range(2)]
        qs = [bs(f"qs{i}", [P, KC, T], F32R) for i in range(2)]
        ks = [bs(f"ks{i}", [P, KC, T], F32R) for i in range(2)]
        tok = bs("tok", [P, NT, C])
        prob = bs("prob", [P, 2, T])
        pr = [bs(f"pr{i}", [P, 2, T], F32R) for i in range(2)]
        gn_bn = bs("gn_bn", [P, KC, 2, 6])
        gn_mv = bs("gn_mv", [P, KC, 2])
        gn_avg = bs("gn_avg", [P, KC, 2])
        gn_d = bs("gn_d", [P, KC])
        gn_d2 = bs("gn_d2", [P, KC])
        gn_r = bs("gn_r", [P, KC])
        gn_var = bs("gn_var", [P, KC])
        gn_s = bs("gn_s", [P, KC])
        gn_t = bs("gn_t", [P, KC])
        neg_max = bs("neg_max", [P, NT])
        row_sum = bs("row_sum", [P, NT])
        row_inv = bs("row_inv", [P, NT])
        ln_bn = bs("ln_bn", [P, NT, 6])
        ln_mv = bs("ln_mv", [P, NT, 2])
        ln_eps = bs("ln_eps", [P, NT])
        ln_r = bs("ln_r", [P, NT])
        tl_bn = bs("tl_bn", [P, 2, NT, 6])
        tl_mv = bs("tl_mv", [P, 2, NT, 2])
        tl_eps = bs("tl_eps", [P, 2, NT])
        tl_r = bs("tl_r", [P, 2, NT])
        tl_mr = bs("tl_mr", [P, 2, NT])
        tl_nb = bs("tl_nb", [P, 2, NT])
        xf = bs("xf", [P, NT, C])
        here = ExitStack()
        tn = sb("tn", [P, NT, C], F32, here)
        here.close()
        xfT = sb("xfT", [P, KC, T], F32, here)
        here.close()
        hold_tn = bs("hold_tn", [P, NT * C])
        spare = bs("spare", [P, 1])
        here = ExitStack()
        raw = sb("raw", [P, 14, KC * C], F32, here)
        raw_vo = sb("raw_vo", [P, KC * C], F32, here)
        vb_wide = sb("vb_wide", [P, KC, P], F32, here)
        vb_col = sb("vb_col", [P, KC], F32, here)
        here.close()
        us = [[sb(f"us{n}{i}", [P, KC, T], F32R, here) for i in range(2)] for n in range(2)]
        here.close()
        x2 = sb("x2", [P, NT, C], F32, here)
        r_out = sb("r_out", [P, NT, C], F32, here)
        here.close()
        hold_r1 = sb("hold_r1", [P, 8192], F32, batch_scope)
        vs = [sb(f"vs{i}", [P, NT, C], F32R, here) for i in range(2)]
        here.close()
        v32 = sb("v32", [P, NT, C], F32, here)
        vk = [sb(f"vk{i}", [P, 2, C], F32R, here) for i in range(2)]
        here.close()
        hold_r2 = sb("hold_r2", [P, 4096], F32, batch_scope)
        batch_scope.close()

        route_scope = ExitStack()

        def rs(name, shape, dt=F32):
            return sb(name, shape, dt, route_scope)

        expert_of = ctx.enter_context(nc.sbuf_tensor("expert_of", [P, STEPS], I32))
        fresh = ctx.enter_context(nc.sbuf_tensor("fresh", [P, STEPS + 2], I32))
        live = sb("live", [P, PAIRS], I32)
        last_step = sb("last_step", [P, 1], I32)
        gather_at = sb("gather_at", [P, COLS + 2 * SUB], I32)
        scatter_at = sb("scatter_at", [P, COLS], I32)
        slot_w = sb("slot_w", [P, COLS])
        before = rs("before", [P, P])
        iota_i = rs("iota_i", [P, P], I32)
        iota = rs("iota", [P, P])
        top_f = rs("top_f", [P, 2, TILES])
        exps = rs("exps", [P, TILES, E])
        zsum = rs("zsum", [P, TILES])
        zinv = rs("zinv", [P, TILES])
        is_top = rs("is_top", [P, 2, TILES, E])
        either = rs("either", [P, TILES, E])
        scratch = rs("scratch", [P, 2, TILES, E])
        top_w = rs("top_w", [P, 2, TILES])
        prefix = [rs(f"prefix{i}", [P, TILES, E]) for i in range(2)]
        slot_all = rs("slot_all", [P, TILES, E])
        cnt_f = rs("cnt_f", [P, E])
        cnt_i = rs("cnt_i", [P, E], I32)
        cnt_s = rs("cnt_s", [P, E], I32)
        need = rs("need", [P, E])
        ends_t = [rs(f"ends{i}", [P, E]) for i in range(2)]
        base = rs("base", [P, E])
        past = rs("past", [P, STEPS, E])
        expert_f = rs("expert_f", [P, STEPS])
        other = rs("other", [P, STEPS])
        end_i = rs("end_i", [P, 1], I32)
        slot_f = rs("slot_f", [P, 2, TILES])
        slot_i = rs("slot_i", [P, 2, TILES], I32)
        lo_i = rs("lo_i", [P, 2, TILES], I32)
        hi_i = rs("hi_i", [P, 2, TILES], I32)
        lo_f = rs("lo_f", [P, 2, TILES])
        hi_f = rs("hi_f", [P, 2, TILES])
        number_i = rs("number_i", [P, TILES], I32)
        number = rs("number", [P, TILES])
        PICK = 8
        pick_lo = rs("pick_lo", [P, 2 * TILES, P])
        pick_hi = rs("pick_hi", [P, 2 * TILES, 2, COLS])
        one_hot = rs("one_hot", [P, 2 * TILES, COLS])
        at_f = rs("at_f", [P, COLS])
        at_m = rs("at_m", [P, COLS])
        route_scope.close()

        ex_scope = ExitStack()

        def es(name, shape, dt=F32):
            return sb(name, shape, dt, ex_scope)

        xg = es("xg", [P, 2, SUB, C])
        xt = [[es(f"xt{n}{i}", [P, KC, STEP], F32R) for i in range(2)] for n in range(2)]
        h32 = es("h32", [P, 4, STEP])
        hs = [es(f"hs{i}", [P, FC, STEP], F32R) for i in range(2)]
        y_b = es("y_b", [P, SUB, C])
        y_w = es("y_w", [P, 2, SUB, C])
        now_g = es("now_g", [P, 2, SUB], I32)
        now_s = es("now_s", [P, 2, SUB], I32)
        w1s1 = [es(f"w1s1{i}", [P, KC, FF], F32R) for i in range(2)]
        w2s1 = [es(f"w2s1{i}", [P, FC, C], F32R) for i in range(2)]
        es("past_route", [P, 10240])
        w1r = es("w1r", [P, 2, KC * FF])
        w2r = es("w2r", [P, 2, FC * C])
        b1t = es("b1t", [P, 2, FC])
        b2t = es("b2t", [P, 2, C])
        w1s = ([es(f"w1s0{i}", [P, KC, FF], F32R) for i in range(2)], w1s1)
        w2s = ([es(f"w2s0{i}", [P, FC, C], F32R) for i in range(2)], w2s1)
        ex_scope.close()
        G = TILES // 4
        rows = sb("rows", [P, G, 4, C], F32, ex_scope)
        cols_out = sb("cols_out", [P, G, KC, HALF], F32, ex_scope)
        ex_scope.close()

        S = {}

        def signal(name):
            S[name] = sem(name)
            return S[name]

        pool_held = signal("pool_held")
        sp_held = signal("sp_held")
        c_made = signal("c_made")
        wa_in = signal("wa_in")
        wb_in = signal("wb_in")
        w_fold = signal("w_fold")
        w_hi = signal("w_hi")
        w_lo = signal("w_lo")
        vo_ready = signal("vo_ready")
        vb_ready = signal("vb_ready")
        x_in = signal("x_in")
        gn_stat = signal("gn_stat")
        gn_mm = signal("gn_mm")
        gn_pow_in = signal("gn_pow_in")
        gn_pow_out = signal("gn_pow_out")
        xn_done = signal("xn_done")
        xn_hi = signal("xn_hi")
        xn_lo = signal("xn_lo")
        pj_mm = signal("pj_mm")
        pj_hi = signal("pj_hi")
        pj_lo = signal("pj_lo")
        s_mm = signal("s_mm")
        s_max = signal("s_max")
        p_exp = signal("p_exp")
        pt_mm = signal("pt_mm")
        pt_hi = signal("pt_hi")
        pt_lo = signal("pt_lo")
        av_mm = signal("av_mm")
        t_done = signal("t_done")
        ln_in = signal("ln_in")
        ln_out = signal("ln_out")
        tn_tok = signal("tn_tok")
        tn_mm = signal("tn_mm")
        tn_hi = signal("tn_hi")
        tn_lo = signal("tn_lo")
        r_mm = signal("r_mm")
        r_act = signal("r_act")
        r_dve = signal("r_dve")
        s2_mm = signal("s2_mm")
        s2_max = signal("s2_max")
        p2_exp = signal("p2_exp")
        p2_hi = signal("p2_hi")
        p2_lo = signal("p2_lo")
        v2_done = signal("v2_done")
        av2_mm = signal("av2_mm")
        added2 = signal("added2")
        tl_in = signal("tl_in")
        tl_out = signal("tl_out")
        tl_own = signal("tl_own")
        x2_done = signal("x2_done")
        xf_norm = signal("xf_norm")
        r_ready = signal("r_ready")
        xf_ready = signal("xf_ready")
        tok_out = signal("tok_out")
        xf_out = signal("xf_out")
        xf_mm = signal("xf_mm")
        xf_col = signal("xf_col")
        g_mm = signal("g_mm")
        u_read = signal("u_read")
        own = signal("own")
        pe_end = signal("pe_end")
        act_end = signal("act_end")
        dve_end = signal("dve_end")
        pool_end = signal("pool_end")
        sp_end = signal("sp_end")
        top_done = signal("top_done")
        exp_done = signal("exp_done")
        rank_mm = signal("rank_mm")
        one_hots = signal("one_hots")
        pick_rows = signal("pick_rows")
        pick_w = signal("pick_w")
        pick_w_act = signal("pick_w_act")
        pick_n = signal("pick_n")
        pick_mm = signal("pick_mm")
        num_done = signal("num_done")
        tables = signal("tables")
        own_r = signal("own_r")
        w1_in = [signal(f"w1_in{n}") for n in range(2)]
        w2_in = [signal(f"w2_in{n}") for n in range(2)]
        b_in = [signal(f"b_in{n}") for n in range(2)]
        ws_act = signal("ws_act")
        ws_dve = signal("ws_dve")
        ws_pool = signal("ws_pool")
        g_in = [signal(f"g_in{n}") for n in range(2)]
        idx_g = signal("idx_g")
        idx_s = signal("idx_s")
        xt_mm = signal("xt_mm")
        xt_hi = signal("xt_hi")
        xt_lo = signal("xt_lo")
        h_mm = signal("h_mm")
        h_act = signal("h_act")
        h_hi = signal("h_hi")
        h_lo = signal("h_lo")
        y_mm = signal("y_mm")
        y_dve = signal("y_dve")
        y_act = signal("y_act")
        added = signal("added")
        y_free = signal("y_free")
        r_in = [signal(f"r_in{n}") for n in range(G)]
        o_mm = signal("o_mm")
        o_act = signal("o_act")
        o_dve = signal("o_dve")
        o_out = signal("o_out")

        def parts(kind, operand, half):
            return [(kind, operand, half, m) for m in range(KC)]

        R = (parts("u", 0, 0) + parts("u", 1, 0) + parts("p", 0, 0) + parts("p", 1, 0)
             + parts("u", 0, 1) + parts("u", 1, 1) + parts("u", 2, 0) + parts("p", 0, 1)
             + parts("u", 2, 1) + parts("p", 1, 1))
        R += [("v", 2, j, 0) for j in range(NT // 2)]
        RG = len(R)
        R_DVE = [sum(k != "v" for k, *_ in R[:g + 1]) for g in range(RG)]
        RD = R_DVE[-1]
        R_BANKS = (4, 5, 6, 7)
        TN_AT = 5
        H1_AT = 8
        GATE_AT = 10
        GATE_MM = {13 + n: range(2 * n, 2 * n + 2) for n in range(NT // 2)}
        GATE_READ = 17
        PE_GN = {14: 0, 18: 1}
        DVE_GN = {10: 0, 15: 1, 18: 2, 19: 3}
        GN_BANK = 1
        ACT_TAIL = {1: (0, 1), 3: (1, 0), 4: (1, 1)}
        DVE_TAIL = {2: (1, 0), 3: (1, 1)}

        FOLDS = (SQ, VO, VA, QA, KA, VB)
        FOLD_BANK = (4, 5, 4, 5, 6, 7)
        FOLD_AT = (1, 2, 5, 6, 7, 8)
        HI_AT = (3, 4, 6, 7, 8, 9)

        block = ctx.enter_context(nc.Block())

        PJ = 8

        def is_live(eng, i):
            return eng.If(eng.value_load(live[0:1, bass.ds(i, 1)], min_val=0, max_val=1) == 1)

        def final_step(eng):
            return eng.value_load(last_step[0:1, 0:1], min_val=STEPS - E - 1, max_val=STEPS - 1)

        def ends(eng, n, semaphores):
            for s in semaphores:
                eng.wait_ge(s, n)

        A_IN = 8 * 16
        B_IN = 14 * 16

        @block.sync
        def _(sp):
            def raw_in(n, w, done):
                sp.dma_start(raw[:, n, :].rearrange("p (k c) -> p k c", k=KC),
                             w.rearrange("(k p) c -> p k c", p=P)).then_inc(done, 16)

            sp.dma_start(xn[:, :, :], x_d[0]).then_inc(x_in, 16)
            raw_in(0, q_w, wa_in)
            raw_in(1, k_w, wa_in)
            sp.dma_start(q_bias[:, :], q_b).then_inc(wa_in, 16)
            sp.dma_start(gn_aff[:, :], gn).then_inc(wa_in, 16)
            raw_in(2, v_w, wa_in)
            raw_in(3, oT, wa_in)
            sp.dma_start(vb_col[:, :], v_b).then_inc(wa_in, 16)
            with nc.allow_non_contiguous_dma(reason="rows read by every partition"):
                sp.dma_start(o_row[:, :], out_b.to_broadcast((P, C))).then_inc(wa_in, 16)
            for n, w in enumerate([W1[0], W1[1], W1[2], a_qk[0], a_qk[1],
                                   W2T[0], W2T[1], W2T[2], a_vT, Wout]):
                raw_in(4 + n, w, wb_in)
            with nc.allow_non_contiguous_dma(reason="rows read by every partition"):
                sp.dma_start(g_row[:, :], ln_g.to_broadcast((P, C))).then_inc(wb_in, 16)
                sp.dma_start(b_row[:, :], ln_b.to_broadcast((P, C))).then_inc(wb_in, 16)
            for k in range(KC):
                sp.dma_start(gate_sb[:, k, :], gate_w[k * P:(k + 1) * P, :]).then_inc(wb_in, 16)

            def image(b, first, last):
                if not last:
                    if not first:
                        sp.wait_ge(xf_out, at(b, 16, 0))
                        sp.sem_inc(sp_held, 1)
                    sp.wait_ge(av_mm, at(b, NT, NT))
                    sp.sem_inc(sp_held, 1)
                    sp.dma_start(xn[:, :, :], x_d[b + 1] if isinstance(b, int) else
                                 x_d[bass.ds(b + 1, 1)].rearrange("b p k t -> (b p) k t")
                                 ).then_inc(x_in, 16)

            def rows_of(b):
                sp.wait_ge(r_ready, at(b, 2, 2))
                sp.sem_inc(sp_held, 1)
                sp.dma_start(acc_t[:, bass.ds(b * NT, NT), :], r_out[:, :, :]).then_inc(tok_out, 16)
                sp.wait_ge(xf_ready, at(b, 2, 2))
                sp.sem_inc(sp_held, 1)
                sp.dma_start(xf_t[:, bass.ds(b * NT, NT), :], xf[:, :, :]).then_inc(xf_out, 16)

            image(0, True, False)
            with sp.Fori(1, B - 1) as b:
                rows_of(b - 1)
                image(b, False, False)
            rows_of(B - 2)
            rows_of(B - 1)
            sp.wait_ge(tok_out, B * 16)
            sp.wait_ge(xf_out, B * 16)
            sp.sem_inc(sp_end, 1)

            sp.wait_ge(tables, 2)
            ends(sp, 1, (pe_end, act_end, dve_end, pool_end))

            def expert_load(s, n, u, first):
                if not first:
                    sp.wait_ge(ws_act, at(s, 8, -8))
                    sp.sem_inc(sp_held, 1)
                    sp.wait_ge(ws_dve, at(s, 4, -4))
                    sp.sem_inc(sp_held, 1)
                    sp.wait_ge(ws_pool, at(s, 4, -4))
                    sp.sem_inc(sp_held, 1)
                e = sp.value_load(expert_of[0:1, bass.ds(s, 1)], min_val=0, max_val=E - 1)

                def weights():
                    sp.dma_start(w1r[:, n, :].rearrange("p (k f) -> p k f", k=KC),
                                 w1_d[bass.ds(e, 1)].rearrange("e p k f -> (e p) k f")).then_inc(w1_in[n], 16)
                    sp.dma_start(w2r[:, n, :].rearrange("p (f c) -> p f c", f=FC),
                                 w2_d[bass.ds(e, 1)].rearrange("e p f c -> (e p) f c")).then_inc(w2_in[n], 16)

                if first:
                    weights()
                else:
                    with sp.If(sp.value_load(fresh[0:1, bass.ds(s, 1)], min_val=0, max_val=1) == 1):
                        weights()
                    with sp.Else():
                        sp.wait_ge(w1_in[n], at(u, 16, 0))
                        sp.sem_inc(w1_in[n], 16)
                        sp.wait_ge(w2_in[n], at(u, 16, 0))
                        sp.sem_inc(w2_in[n], 16)
                if not first:
                    sp.wait_ge(h_act, at(s, FC, -FC))
                    sp.sem_inc(sp_held, 1)
                    sp.wait_ge(y_dve, at(s, 1, -1))
                    sp.sem_inc(sp_held, 1)
                sp.dma_start(b1t[:, n, :], b1[bass.ds(e, 1)].rearrange("e p f -> (e p) f")
                             ).then_inc(b_in[n], 16)
                sp.dma_start(b2t[:, n, :], b2[bass.ds(e, 1), :].to_broadcast((P, C))).then_inc(b_in[n], 16)

            expert_load(0, 0, 0, True)
            expert_load(1, 1, 0, True)
            with sp.Fori(1, PAIRS) as i:
                with is_live(sp, i):
                    for n in range(2):
                        expert_load(i * 2 + n, n, i, False)

            s_end = final_step(sp)
            sp.wait_ge(added, at(s_end, SUB * 16, SUB * 16))
            sp.sem_inc(sp_held, 1)
            for n in range(2):
                sp.wait_ge(g_in[n], at(s_end, SUB * 8, SUB * 24))
                sp.sem_inc(sp_held, 1)
            ends(sp, 2, (pe_end, act_end, dve_end))
            for g in range(G):
                sp.dma_start(rows[:, g, :, :], acc_t[:, 4 * g:4 * g + 4, :]).then_inc(r_in[g], 16)
            for g in range(G):
                sp.wait_ge(o_act, g + 1)
                sp.wait_ge(o_dve, g + 1)
                n = g % NH
                sp.dma_start(out_d[g // NH, :, :, n * HALF:(n + 1) * HALF],
                             cols_out[:, g, :, :]).then_inc(o_out, 16)
            sp.wait_ge(o_out, G * 16)

        @block.gpsimd
        def _(pool):
            g = nc.gpsimd
            made = [0]

            def make(ins):
                made[0] += 1
                ins.then_inc(c_made, 1)

            make(g.memset(ident[:, :], 0.0))
            make(g.memset(ones[:, :], 1.0))
            make(g.memset(same_group[:, :], 1.0 / GROUP))
            make(g.memset(minus_half[:, :], -0.5))
            make(g.memset(minus_one[:, :], -1.0))
            pool.wait_ge(c_made, made[0])
            make(g.affine_select(out=ident[:, :], in_=ident[:, :], compare_op=ALU.not_equal, fill=1.0,
                                 base=0, pattern=[[-1, P]], channel_multiplier=1))
            wide = same_group[:, :].rearrange("p (g c) -> p g c", c=GROUP)
            make(g.affine_select(out=wide, in_=wide, compare_op=ALU.is_ge, fill=0.0,
                                 base=0, pattern=[[-GROUP, P // GROUP], [0, GROUP]], channel_multiplier=1))
            pool.wait_ge(c_made, made[0])
            make(g.affine_select(out=wide, in_=wide, compare_op=ALU.is_ge, fill=0.0, base=GROUP - 1,
                                 pattern=[[GROUP, P // GROUP], [0, GROUP]], channel_multiplier=-1))
            assert made[0] == CONSTANTS

            def rsqrt(dst, src):
                return g.tensor_tensor(dst, src, minus_half[:, 0:src.shape[1]], ALU.pow)

            def group_norm(b):
                pool.wait_ge(gn_pow_in, at(b, 1, 1))
                rsqrt(gn_r[:, :], gn_var[:, :]).then_inc(gn_pow_out, 1)

            def first_norm(b, i):
                pool.wait_ge(ln_in, at(b, NT, i + 1))
                rsqrt(ln_r[:, i:i + 1], ln_eps[:, i:i + 1]).then_inc(ln_out, 1)

            TL_OWN = 8 + 2

            def last_norms(b, between_norms, affines=True):
                n = [0]

                def own_step(ins):
                    n[0] += 1
                    ins.then_inc(tl_own, 1)
                    pool.wait_ge(tl_own, at(b, TL_OWN, n[0]))

                def scale(which, h):
                    c = slice(4 * h, 4 * h + 4)
                    pool.wait_ge(tl_in, at(b, 4, 2 * which + h + 1))
                    own_step(rsqrt(tl_r[:, which, c], tl_eps[:, which, c]))
                    own_step(g.tensor_tensor(tl_mr[:, which, c], tl_mv[:, which, c, 0], tl_r[:, which, c], ALU.mult))
                    g.tensor_tensor(tl_nb[:, which, c], tl_mr[:, which, c], minus_one[:, 0:4],
                                    ALU.mult).then_inc(tl_out, 1)

                def stream(h):
                    c = slice(4 * h, 4 * h + 4)
                    pool.wait_ge(x2_done, at(b, 2, h + 1))
                    g.tensor_tensor(r_out[:, c, :], tok[:, c, :], x2[:, c, :], ALU.add).then_inc(r_ready, 1)

                def affine(h):
                    c = slice(4 * h, 4 * h + 4)
                    pool.wait_ge(xf_norm, at(b, 2, h + 1))
                    own_step(g.tensor_tensor(xf[:, c, :], xf[:, c, :],
                                             g_row[:, :].unsqueeze(1).to_broadcast((P, 4, C)), ALU.mult))
                    g.tensor_tensor(xf[:, c, :], xf[:, c, :],
                                    b_row[:, :].unsqueeze(1).to_broadcast((P, 4, C)), ALU.add).then_inc(xf_ready, 1)

                scale(0, 0)
                scale(0, 1)
                if affines:
                    stream(0)
                    stream(1)
                between_norms(0)
                between_norms(1)
                scale(1, 0)
                between_norms(2)
                scale(1, 1)
                if not affines:
                    stream(0)
                    stream(1)
                else:
                    affine(0)
                    between_norms(3)
                    affine(1)
                assert n[0] == TL_OWN or not affines

            def image(b, first, last):
                if not first:
                    last_norms(b - 1, lambda i: first_norm(b, i))
                for i in range(0 if first else 4, NT):
                    first_norm(b, i)
                if not last:
                    group_norm(b + 1)

            group_norm(0)
            image(0, True, False)
            with pool.Fori(1, B - 1) as b:
                image(b, False, False)
            image(B - 1, False, True)
            last_norms(B - 1, lambda i: None, affines=False)
            pool.wait_ge(tl_out, 4 * B)
            pool.sem_inc(pool_end, 1)

            ends(pool, 1, (pe_end, act_end, dve_end, sp_end))
            g.iota(iota_i[:, :], pattern=[[1, P]], base=0, channel_multiplier=0).then_inc(num_done, 1)
            g.iota(number_i[:, :], pattern=[[P, TILES]], base=1, channel_multiplier=1).then_inc(num_done, 1)
            g.affine_select(out=before[:, :], in_=ones[:, :], compare_op=ALU.is_gt, fill=0.0,
                            base=0, pattern=[[1, P]], channel_multiplier=-1).then_inc(num_done, 1)
            pool.wait_ge(num_done, 3)
            g.tensor_copy(iota[:, :], iota_i[:, :]).then_inc(num_done, 1)
            g.tensor_copy(number[:, :], number_i[:, :]).then_inc(num_done, 1)
            for c in range(2 * TILES // PICK):
                first = c * PICK % TILES
                pool.wait_ge(one_hots, c + 1)
                g.tensor_tensor(pick_hi[:, c * PICK:(c + 1) * PICK, 0, :], one_hot[:, c * PICK:(c + 1) * PICK, :],
                                number[:, first:first + PICK].unsqueeze(2).to_broadcast((P, PICK, COLS)),
                                ALU.mult).then_inc(pick_n, 1)
            pool.wait_ge(tables, 4)

            def gather(s, n, first):
                if not first:
                    pool.wait_ge(xt_mm, at(s, 1, -1))
                    pool.sem_inc(pool_held, 1)
                g.tensor_copy(now_g[:, n, :], gather_at[:, bass.ds(s * SUB, SUB)]).then_inc(idx_g, 1)
                pool.wait_ge(idx_g, at(s, 1, 1))
                pool.sem_inc(pool_held, 1)
                for h in range(SUB):
                    g.indirect_dma_start(out=xg[:, n, h, :], out_offset=None, in_=xf_d,
                                         in_offset=bass.IndirectOffsetOnAxis(ap=now_g[:, n, h:h + 1], axis=0),
                                         bounds_check=TOK - 1, oob_is_err=True).then_inc(g_in[n], 16)

            def scatter(s, n, first):
                g.tensor_copy(now_s[:, n, :], scatter_at[:, bass.ds(s * SUB, SUB)]).then_inc(idx_s, 1)
                pool.wait_ge(idx_s, at(s, 1, 1))
                pool.wait_ge(y_act, at(s, 1, 1))
                if not first:
                    pool.wait_ge(added, at(s, SUB * 16, 0))
                pool.sem_inc(y_free, 1)
                for h in range(SUB):
                    g.indirect_dma_start(out=acc_d, out_offset=bass.IndirectOffsetOnAxis(
                        ap=now_s[:, n, h:h + 1], axis=0), in_=y_w[:, n, h, :], in_offset=None,
                        bounds_check=TOK - 1, oob_is_err=False, compute_op=ALU.add).then_inc(added, 16)

            def lo_pieces(s, n, u):
                if isinstance(s, int) and s < 2:
                    split_w2(s, n, u)
                    return
                with pool.If(pool.value_load(fresh[0:1, bass.ds(s, 1)], min_val=0, max_val=1) == 1):
                    split_w2(s, n, u)
                with pool.Else():
                    pool.wait_ge(ws_pool, at(s, 4, 0))
                    pool.sem_inc(ws_pool, 4)

            def split_w2(s, n, u):
                pool.wait_ge(w2_in[n], at(u, 16, 16))
                if not (isinstance(s, int) and s < 2):
                    pool.wait_ge(y_mm, at(s, FC, -FC))
                for f in range(4, 8):
                    pool.wait_ge(ws_act, at(s, 8, f + 1))
                    c = slice((2 * (f - 4)) * C, (2 * (f - 4) + 2) * C)
                    g.tensor_tensor(w2s[n][1][:, :, :].rearrange("p f c -> p (f c)")[:, c], w2r[:, n, c],
                                    w2s[n][0][:, :, :].rearrange("p f c -> p (f c)")[:, c].bitcast(F32),
                                    ALU.subtract).then_inc(ws_pool, 1)

            gather(0, 0, True)
            gather(1, 1, True)
            lo_pieces(0, 0, 0)

            def steps(i, first):
                for n in range(2):
                    s = i * 2 + n
                    gather(s + 2, n, False)
                    if not (first and n == 0):
                        scatter(s - 1, 1 - n, first)
                    lo_pieces(s + 1, 1 - n, (i if n == 0 else i + 1))

            steps(0, True)
            with pool.Fori(1, PAIRS) as i:
                with is_live(pool, i):
                    steps(i, False)
            scatter(final_step(pool), 1, False)

        @block.scalar
        def _(act):
            a = nc.scalar
            act.wait_ge(wa_in, A_IN)
            flat_h = wh[:, :, :, :].rearrange("p w k c -> p w (k c)")
            a.mul(raw[:, 0, :], raw[:, 0, :], C ** -0.5).then_inc(w_hi, 1)
            a.mul(q_bias[:, :], q_bias[:, :], C ** -0.5).then_inc(w_hi, 1)

            def folded_hi(n):
                act.wait_ge(w_fold, FOLD_AT[n])
                if FOLDS[n] == VA:
                    a.copy(raw_vo[:, :], bank(FOLD_BANK[n])).then_inc(vo_ready, 1)
                a.copy(flat_h[:, FOLDS[n], :], bank(FOLD_BANK[n])).then_inc(w_hi, 1)

            def norm_hi(b, k):
                act.wait_ge(xn_done, at(b, KC, k + 1))
                a.copy(xs[0][:, k, :], xn[:, k, :]).then_inc(xn_hi, 1)

            def tail_norm(b, which, h):
                src, dst, ready = ((tok, x2, x2_done), (x2, xf, xf_norm))[which]
                act.wait_ge(tl_out, at(b, 4, 2 * which + h + 1))
                for j in range(4 * h, 4 * h + 4):
                    ins = a.activation(dst[:, j, :], src[:, j, :], ACT.Identity,
                                       bias=tl_nb[:, which, j:j + 1], scale=tl_r[:, which, j:j + 1])
                ins.then_inc(ready, 1)

            def gate_columns(b, h):
                act.wait_ge(xf_mm, at(b, 2, h + 1))
                a.copy(xfT[:, :, h * HALF:(h + 1) * HALF],
                       bank(2 * h, count=2).rearrange("p (k t) -> p k t", k=KC)).then_inc(xf_col, 1)

            def image(b, first, last):
                def w(s, per, n):
                    act.wait_ge(s, at(b, per, n))

                def project_hi(gi):
                    w(pj_mm, PJ, gi + 1)
                    if gi < 4:
                        n, m = gi // 2, gi % 2
                        a.activation(qs[0][:, m, n * HALF:(n + 1) * HALF], bank(gi), ACT.Identity,
                                     bias=s_bias[:, m:m + 1]).then_inc(pj_hi, 1)
                    else:
                        j = gi - 4
                        a.copy(vs[0][:, 2 * j:2 * j + 2, :].rearrange("p j c -> p (j c)"),
                               bank(gi)).then_inc(pj_hi, 1)

                def exp1(i):
                    w(s_max, NT, i + 1)
                    if i >= 2:
                        w(pt_mm, NT, i - 1)
                    a.activation(prob[:, i % 2, :], bank(2 * (i % 2), count=2), ACT.Exp,
                                 bias=neg_max[:, i:i + 1], accum_out=row_sum[:, i:i + 1]).then_inc(p_exp, 1)

                def hi1(i):
                    w(pt_mm, NT, i + 1)
                    if i >= 2:
                        w(av_mm, NT, i - 1)
                    a.copy(pr[0][:, i % 2, :], bank(4, count=2)).then_inc(pt_hi, 1)

                def hi_tn(h):
                    w(tn_mm, 2, h + 1)
                    a.copy(xs[0][:, :, h * HALF:(h + 1) * HALF],
                           bank(2 * h, count=2).rearrange("p (k t) -> p k t", k=KC)).then_inc(tn_hi, 1)

                if first:
                    act.wait_ge(w_lo, 2)
                for gi in range(6):
                    project_hi(gi)
                exp1(0)
                for gi in range(6, PJ):
                    project_hi(gi)
                if first:
                    act.wait_ge(wb_in, B_IN)
                    a.copy(flat_h[:, 0:DIRECT, :], raw[:, 4:4 + DIRECT, :]).then_inc(w_hi, 1)
                else:
                    tail_norm(b - 1, 0, 0)
                    hi1(0)
                exp1(1)
                if first:
                    for n in range(2, len(FOLDS)):
                        folded_hi(n)
                for i in range(NT):
                    if first or i > 0:
                        hi1(i)
                    if not first and i in ACT_TAIL:
                        tail_norm(b - 1, *ACT_TAIL[i])
                    if i + 2 < NT:
                        exp1(i + 2)
                    if i == 6:
                        hi_tn(0)

                def exp2(i):
                    w(s2_max, NT, i + 1)
                    if i >= 2:
                        w(p2_lo, NT, i - 1)
                    a.activation(prob[:, i % 2, :], bank(2 * (i % 2), count=2), ACT.Exp,
                                 bias=neg_max[:, i:i + 1], accum_out=row_sum[:, i:i + 1]).then_inc(p2_exp, 1)

                def hi2(i):
                    w(p2_exp, NT, i + 1)
                    if i >= 2:
                        w(av2_mm, NT, i - 1)
                    a.copy(pr[0][:, i % 2, :], prob[:, i % 2, :]).then_inc(p2_hi, 1)

                n_u = 0
                for gi, (kind, o, n, m) in enumerate(R):
                    w(r_mm, RG, gi + 1)
                    src = bank(R_BANKS[gi % 4])
                    if kind == "u":
                        if n_u >= 2:
                            prior = [j for j in range(gi) if R[j][0] == "u"][-2]
                            w(r_dve, RD, R_DVE[prior])
                        a.activation(prob[:, n_u % 2, 0:HALF], src, ACT.Silu).then_inc(r_act, 1)
                        n_u += 1
                    elif kind == "p":
                        a.copy((qs, ks)[o][0][:, m, n * HALF:(n + 1) * HALF], src).then_inc(r_act, 1)
                    else:
                        a.copy(v32[:, 2 * n:2 * n + 2, :].rearrange("p j c -> p (j c)"), src).then_inc(r_act, 1)
                    if gi == RG - 3:
                        exp2(0)
                        hi2(0)
                    if gi == TN_AT - 1:
                        hi_tn(1)
                    if not first and gi in (GATE_AT, GATE_AT + 1):
                        gate_columns(b - 1, gi - GATE_AT)

                for i in range(NT):
                    if i > 0:
                        exp2(i)
                        hi2(i)
                    if not last and i in (2, 3):
                        norm_hi(b + 1, i - 2)

            for k in range(KC):
                norm_hi(0, k)
            folded_hi(0)
            folded_hi(1)
            image(0, True, False)
            with act.Fori(1, B - 1) as b:
                image(b, False, False)
            image(B - 1, False, True)
            act.wait_ge(xf_out, (B - 1) * 16)
            for which in range(2):
                for h in range(2):
                    tail_norm(B - 1, which, h)
            for h in range(2):
                gate_columns(B - 1, h)
            act.wait_ge(xf_col, 2 * B)
            act.sem_inc(act_end, 1)

            act.wait_ge(top_done, 2)
            a.activation(exps[:, :, :], scratch[:, 0, :, :], ACT.Exp).then_inc(exp_done, 1)


            def w_piece(s, n, u, f):
                first = isinstance(s, int) and s < 2
                if f < 4:
                    if f == 0:
                        act.wait_ge(w1_in[n], at(u, 16, 16))
                        if not first:
                            act.wait_ge(h_mm, at(s, FC, -FC))
                    dst = w1s[n][0][:, :, :].rearrange("p k f -> p (k f)")
                    src = w1r
                else:
                    if f == 4:
                        act.wait_ge(w2_in[n], at(u, 16, 16))
                        if not first:
                            act.wait_ge(y_mm, at(s, FC, -FC))
                    dst = w2s[n][0][:, :, :].rearrange("p f c -> p (f c)")
                    src = w2r
                c = slice((f % 4) * 512, (f % 4 + 1) * 512)
                a.copy(dst[:, c], src[:, n, c]).then_inc(ws_act, 1)

            def x_hi(s, n):
                act.wait_ge(xt_mm, at(s, 1, 1))
                a.copy(xt[n][0][:, :, :].rearrange("p k t -> p (k t)"), bank(6)).then_inc(xt_hi, 1)

            for c in range(1, 2 * TILES // PICK, 2):
                act.wait_ge(one_hots, c + 1)
                for j in range(c * PICK, (c + 1) * PICK):
                    ins = a.activation(pick_hi[:, j, 1, :], one_hot[:, j, :], ACT.Copy,
                                       scale=top_w[:, j // TILES, j % TILES:j % TILES + 1])
                ins.then_inc(pick_w_act, 1)
                w_piece(0, 0, 0, c - 1)
                w_piece(0, 0, 0, c)
            act.wait_ge(tables, 4)
            x_hi(0, 0)

            def steps(i, first):
                for n in range(2):
                    s = i * 2 + n
                    act.wait_ge(b_in[n], at(i, 32, 32))
                    if first and n == 0:
                        chunks(i, n, first, True)
                    else:
                        with act.If(act.value_load(fresh[0:1, bass.ds(s + 1, 1)], min_val=0, max_val=1) == 1):
                            chunks(i, n, first, True)
                        with act.Else():
                            act.wait_ge(ws_act, at(s, 8, 8))
                            act.sem_inc(ws_act, 8)
                            chunks(i, n, first, False)

            def chunks(i, n, first, split):
                s = i * 2 + n
                for f in range(FC):
                    gi = n * FC + f
                    act.wait_ge(h_mm, at(i, 2 * FC, gi + 1))
                    if not (first and gi < 4):
                        act.wait_ge(h_lo, at(i, 2 * FC, gi - 3))
                    a.activation(h32[:, gi % 4, :], bank(gi % 4, STEP), ACT.Gelu,
                                 bias=b1t[:, n, f:f + 1]).then_inc(h_act, 1)
                    if split:
                        w_piece(s + 1, 1 - n, (i if n == 0 else i + 1), f)
                    if f == 2:
                        x_hi(s + 1, 1 - n)
                    if f == 3 and not (first and n == 0):
                        y_scale(s - 1, 1 - n, first)

            def y_scale(s, n, first):
                act.wait_ge(y_dve, at(s, 1, 1))
                if not first:
                    act.wait_ge(y_free, at(s, 1, 0))
                for h in range(SUB):
                    ins = a.activation(y_w[:, n, h, :], y_b[:, h, :], ACT.Copy,
                                       scale=slot_w[:, bass.ds(s * SUB + h, 1)])
                ins.then_inc(y_act, 1)

            steps(0, True)
            with act.Fori(1, PAIRS) as i:
                with is_live(act, i):
                    steps(i, False)
            s_end = final_step(act)
            y_scale(s_end, 1, False)
            act.wait_ge(y_act, at(s_end, 1, 1))
            act.sem_inc(act_end, 1)

            for gi in range(G):
                act.wait_ge(o_mm, gi + 1)
                a.copy(cols_out[:, gi, 0, :], bank(2 * (gi % 2))).then_inc(o_act, 1)

        def route(dve, v, first_pieces):
            done = [0]

            def step(ins):
                done[0] += 1
                ins.then_inc(own_r, 1)

            def settle():
                dve.wait_ge(own_r, done[0])

            def pair(a):
                return a[:, :, :].rearrange("p k t -> p (k t)")

            def wide(a):
                return a.unsqueeze(2).to_broadcast((P, TILES, E))

            v.tensor_tensor(scratch[:, 0, :, :], logits[:, :, :], wide(top8[:, :, 0]),
                            ALU.subtract).then_inc(top_done, 1)
            v.tensor_copy(top_f[:, :, :], top_i[:, :, 0:2].rearrange("p t k -> p k t")).then_inc(top_done, 1)
            dve.wait_ge(top_done, 2)
            dve.wait_ge(num_done, 5)
            step(v.tensor_tensor(is_top[:, :, :, :].rearrange("p k t e -> p (k t) e"),
                                 pair(top_f).unsqueeze(2).to_broadcast((P, 2 * TILES, E)),
                                 iota[:, 0:E].unsqueeze(1).to_broadcast((P, 2 * TILES, E)), ALU.is_equal))
            settle()
            v.tensor_tensor(either[:, :, :], is_top[:, 0, :, :], is_top[:, 1, :, :], ALU.add).then_inc(top_done, 1)
            dve.wait_ge(exp_done, 1)
            step(v.tensor_reduce(zsum[:, :], exps[:, :, :], AXX, ALU.add))
            for k in range(2):
                step(v.tensor_tensor(scratch[:, k, :, :], exps[:, :, :], is_top[:, k, :, :], ALU.mult))
            settle()
            step(v.reciprocal(zinv[:, :], zsum[:, :]))
            step(v.tensor_reduce(pair(top_w), scratch[:, :, :, :].rearrange("p k t e -> p (k t) e"), AXX, ALU.add))
            settle()
            for k in range(2):
                step(v.tensor_tensor(top_w[:, k, :], top_w[:, k, :], zinv[:, :], ALU.mult))
            dve.wait_ge(rank_mm, 1)
            tile_n = bank(1, TILES * E).rearrange("p (t e) -> p t e", e=E)
            step(v.memset(prefix[0][:, 0:1, :], 0.0))
            step(v.tensor_copy(prefix[0][:, 1:TILES, :], tile_n[:, 0:TILES - 1, :]))
            src, d = 0, 1
            while d < TILES:
                settle()
                step(v.tensor_copy(prefix[1 - src][:, 0:d, :], prefix[src][:, 0:d, :]))
                step(v.tensor_tensor(prefix[1 - src][:, d:, :], prefix[src][:, d:, :],
                                     prefix[src][:, :TILES - d, :], ALU.add))
                src, d = 1 - src, 2 * d
            settle()
            step(v.tensor_tensor(cnt_f[:, :], prefix[src][:, TILES - 1, :], tile_n[:, TILES - 1, :], ALU.add))
            settle()
            step(v.tensor_scalar(cnt_i[:, :], cnt_f[:, :], float(STEP - 1), None, ALU.add))
            settle()
            shift = STEP.bit_length() - 1
            step(v.tensor_single_scalar(cnt_s[:, :], cnt_i[:, :], shift, ALU.logical_shift_right))
            settle()
            step(v.tensor_copy(need[:, :], cnt_s[:, :]))
            settle()
            step(v.tensor_copy(ends_t[0][:, :], need[:, :]))
            es_, d = 0, 1
            while d < E:
                settle()
                step(v.tensor_copy(ends_t[1 - es_][:, 0:d], ends_t[es_][:, 0:d]))
                step(v.tensor_tensor(ends_t[1 - es_][:, d:], ends_t[es_][:, d:], ends_t[es_][:, :E - d], ALU.add))
                es_, d = 1 - es_, 2 * d
            settle()
            step(v.tensor_tensor(base[:, :], ends_t[es_][:, :], need[:, :], ALU.subtract))
            settle()
            step(v.tensor_scalar(base[:, :], base[:, :], float(STEP), None, ALU.mult))
            step(v.tensor_tensor(past[:, :, :], iota[:, 0:STEPS].unsqueeze(2).to_broadcast((P, STEPS, E)),
                                 ends_t[es_][:, :].unsqueeze(1).to_broadcast((P, STEPS, E)), ALU.is_ge))
            settle()
            step(v.tensor_reduce(expert_f[:, :], past[:, :, :], AXX, ALU.add))
            settle()
            step(v.tensor_scalar(live[:, :], expert_f[:, :].rearrange("p (i n) -> p i n", n=2)[:, :, 0], float(E),
                                 None, ALU.is_lt))
            step(v.tensor_scalar(end_i[:, :], ends_t[es_][:, E - 1:E], 1.0, None, ALU.add))
            step(v.tensor_tensor(other[:, 2:STEPS], expert_f[:, 2:STEPS], expert_f[:, 0:STEPS - 2], ALU.not_equal))
            step(v.memset(fresh[:, STEPS:STEPS + 2], 0))
            step(v.memset(gather_at[:, COLS:COLS + 2 * SUB], 0))
            v.tensor_scalar(expert_of[:, :], expert_f[:, :], float(E - 1), None, ALU.min).then_inc(tables, 1)
            settle()
            step(v.tensor_single_scalar(end_i[:, :], end_i[:, :], 1, ALU.logical_shift_right))
            settle()
            step(v.tensor_scalar(last_step[:, :], end_i[:, :], 2.0, -1.0, ALU.mult, ALU.add))
            settle()
            v.scalar_tensor_tensor(fresh[:, 2:STEPS], expert_f[:, 2:STEPS], float(E), other[:, 2:STEPS],
                                   ALU.is_lt, ALU.mult).then_inc(tables, 1)
            rank = bank(0, TILES * E).rearrange("p (t e) -> p t e", e=E)
            step(v.tensor_tensor(slot_all[:, :, :], rank, prefix[src][:, :, :], ALU.add))
            settle()
            step(v.tensor_tensor(slot_all[:, :, :], slot_all[:, :, :],
                                 base[:, :].unsqueeze(1).to_broadcast((P, TILES, E)), ALU.add))
            settle()
            for k in range(2):
                step(v.tensor_tensor(scratch[:, k, :, :], slot_all[:, :, :], is_top[:, k, :, :], ALU.mult))
            settle()
            step(v.tensor_reduce(pair(slot_f), scratch[:, :, :, :].rearrange("p k t e -> p (k t) e"), AXX, ALU.add))
            settle()
            step(v.tensor_copy(pair(slot_i), pair(slot_f)))
            settle()
            step(v.tensor_single_scalar(pair(lo_i), pair(slot_i), P - 1, ALU.bitwise_and))
            step(v.tensor_single_scalar(pair(hi_i), pair(slot_i), 7, ALU.logical_shift_right))
            settle()
            step(v.tensor_copy(pair(lo_f), pair(lo_i)))
            step(v.tensor_copy(pair(hi_f), pair(hi_i)))
            settle()
            for c in range(2 * TILES // PICK):
                k, t = c * PICK // TILES, slice(c * PICK % TILES, c * PICK % TILES + PICK)
                j = slice(c * PICK, (c + 1) * PICK)
                v.tensor_tensor(one_hot[:, j, :], iota[:, 0:COLS].unsqueeze(1).to_broadcast((P, PICK, COLS)),
                                hi_f[:, k, t].unsqueeze(2).to_broadcast((P, PICK, COLS)),
                                ALU.is_equal).then_inc(one_hots, 1)
                v.tensor_tensor(pick_lo[:, j, :], iota[:, :].unsqueeze(1).to_broadcast((P, PICK, P)),
                                lo_f[:, k, t].unsqueeze(2).to_broadcast((P, PICK, P)),
                                ALU.is_equal).then_inc(pick_rows, 1)
                if c % 2 == 0:
                    dve.wait_ge(one_hots, c + 1)
                    v.tensor_tensor(pick_hi[:, j, 1, :], one_hot[:, j, :],
                                    top_w[:, k, t].unsqueeze(2).to_broadcast((P, PICK, COLS)),
                                    ALU.mult).then_inc(pick_w, 1)
            first_pieces()
            dve.wait_ge(pick_mm, 2 * TILES)
            v.tensor_copy(slot_w[:, :], bank(2)[:, COLS:2 * COLS]).then_inc(tables, 1)
            step(v.tensor_scalar(at_f[:, :], bank(2)[:, 0:COLS], -1.0, None, ALU.add))
            settle()
            step(v.tensor_scalar(gather_at[:, 0:COLS], at_f[:, :], 0.0, None, ALU.max))
            step(v.tensor_scalar(at_m[:, :], at_f[:, :], 0.0, float(SKIP), ALU.is_lt, ALU.mult))
            settle()
            v.tensor_tensor(scatter_at[:, :], at_f[:, :], at_m[:, :], ALU.add).then_inc(tables, 1)

        @block.vector
        def _(dve):
            v = nc.vector
            count = [0]
            before_turn = [0]

            def step(ins):
                count[0] += 1
                ins.then_inc(own, 1)

            def settle():
                dve.wait_ge(own, before_turn[0] + count[0])

            def settle_aggr():
                settle()
                v.memset(spare[:, :], 0.0)

            flat_h = wh[:, :, :, :].rearrange("p w k c -> p w (k c)")
            flat_l = wl[:, :, :, :].rearrange("p w k c -> p w (k c)")
            def bias_columns():
                dve.wait_ge(c_made, CONSTANTS)
                for k in range(KC):
                    v.tensor_scalar(vb_wide[:, k, :], ones[:, :], vb_col[:, k:k + 1], None,
                                    ALU.mult).then_inc(vb_ready, 1)

            def folded_lo(n):
                dve.wait_ge(w_hi, HI_AT[n])
                v.tensor_tensor(flat_l[:, FOLDS[n], :], bank(FOLD_BANK[n]), flat_h[:, FOLDS[n], :].bitcast(F32),
                                ALU.subtract).then_inc(w_lo, 1)

            def group_stats(b, at_bank, part):
                def w(s, per, n):
                    dve.wait_ge(s, at(b, per, n))

                if part == 0:
                    w(x_in, 16, 16)
                    for k in range(KC):
                        for h in range(2):
                            step(v.bn_stats(gn_bn[:, k, h, :], xn[:, k, h * HALF:(h + 1) * HALF]))
                    settle_aggr()
                    for k in range(KC):
                        ins = v.bn_aggr(gn_mv[:, k, :], gn_bn[:, k, :, :].rearrange("p h s -> p (h s)"))
                    ins.then_inc(gn_stat, 1)
                elif part == 1:
                    w(gn_mm, 2, 1)
                    step(v.tensor_copy(gn_avg[:, :, :],
                                       bank(at_bank)[:, 0:2 * KC].rearrange("p (k s) -> p k s", k=KC)))
                    settle()
                    step(v.tensor_tensor(gn_d[:, :], gn_mv[:, :, 0], gn_avg[:, :, 0], ALU.subtract))
                    settle()
                    v.tensor_tensor(gn_d2[:, :], gn_d[:, :], gn_d[:, :], ALU.mult).then_inc(gn_stat, 1)
                elif part == 2:
                    w(gn_mm, 2, 2)
                    v.scalar_tensor_tensor(gn_var[:, :], bank(at_bank)[:, 8:8 + KC], GN_EPS, gn_avg[:, :, 1],
                                           ALU.add, ALU.add).then_inc(gn_pow_in, 1)
                else:
                    w(gn_pow_out, 1, 1)
                    step(v.tensor_tensor(gn_s[:, :], gn_r[:, :], gn_aff[:, 0:KC], ALU.mult))
                    settle()
                    step(v.tensor_tensor(gn_t[:, :], gn_avg[:, :, 0], gn_s[:, :], ALU.mult))
                    settle()
                    step(v.tensor_tensor(gn_t[:, :], gn_aff[:, KC:2 * KC], gn_t[:, :], ALU.subtract))
                    settle()

            def group_apply(b, k):
                v.tensor_scalar(xn[:, k, :], xn[:, k, :], gn_s[:, k:k + 1], gn_t[:, k:k + 1],
                                ALU.mult, ALU.add).then_inc(xn_done, 1)

            def group_lo(b, k):
                dve.wait_ge(xn_hi, at(b, KC, k + 1))
                v.tensor_tensor(xs[1][:, k, :], xn[:, k, :], xs[0][:, k, :].bitcast(F32),
                                ALU.subtract).then_inc(xn_lo, 1)

            def tail_add(b, h):
                dve.wait_ge(av2_mm, at(b, NT, NT))
                for m in (2 * h, 2 * h + 1):
                    tile = tok[:, 2 * m:2 * m + 2, :].rearrange("p j c -> p (j c)")
                    ins = v.tensor_tensor(tile, bank(4 + m), tile, ALU.add)
                ins.then_inc(added2, 1)

            def tail_stats(b, which, h):
                if which:
                    dve.wait_ge(x2_done, at(b, 2, h + 1))
                else:
                    dve.wait_ge(added2, at(b, 2, h + 1))
                src = (tok, x2)[which]
                c = range(4 * h, 4 * h + 4)
                for i in c:
                    step(v.bn_stats(tl_bn[:, which, i, :], src[:, i, :]))
                settle_aggr()
                for i in c:
                    step(v.bn_aggr(tl_mv[:, which, i, :], tl_bn[:, which, i, :]))
                settle()
                v.tensor_scalar(tl_eps[:, which, 4 * h:4 * h + 4], tl_mv[:, which, 4 * h:4 * h + 4, 1], LN_EPS,
                                None, ALU.add).then_inc(tl_in, 1)

            def gate_read(b):
                dve.wait_ge(g_mm, at(b, 1, 1))
                step(v.tensor_copy(logits[:, bass.ds(b * NT, NT), :].rearrange("p t e -> p (t e)"),
                                   bank(0)[:, 0:NT * E]))

            def image(b, first, last):
                def w(s, per, n):
                    dve.wait_ge(s, at(b, per, n))

                def project_lo(gi):
                    w(pj_hi, PJ, gi + 1)
                    if gi < 4:
                        n, m = gi // 2, gi % 2
                        c = slice(n * HALF, (n + 1) * HALF)
                        v.scalar_tensor_tensor(qs[1][:, m, c], bank(gi), s_bias[:, m:m + 1],
                                               qs[0][:, m, c].bitcast(F32),
                                               ALU.add, ALU.subtract).then_inc(pj_lo, 1)
                    else:
                        j = gi - 4
                        v.tensor_tensor(vs[1][:, 2 * j:2 * j + 2, :].rearrange("p j c -> p (j c)"),
                                        bank(gi),
                                        vs[0][:, 2 * j:2 * j + 2, :].rearrange("p j c -> p (j c)").bitcast(F32),
                                        ALU.subtract).then_inc(pj_lo, 1)

                def max1(i):
                    w(s_mm, NT, i + 1)
                    v.tensor_reduce(neg_max[:, i:i + 1], bank(2 * (i % 2), count=2), AXX, ALU.max,
                                    negate=True).then_inc(s_max, 1)

                def lo1(i):
                    w(pt_hi, NT, i + 1)
                    v.tensor_tensor(pr[1][:, i % 2, :], bank(4, count=2), pr[0][:, i % 2, :].bitcast(F32),
                                    ALU.subtract).then_inc(pt_lo, 1)
                    step(v.reciprocal(row_inv[:, i:i + 1], row_sum[:, i:i + 1]))

                def out1(i):
                    w(av_mm, NT, i + 1)
                    if i == 0 and not first:
                        w(r_ready, 2, 0)
                    step(v.tensor_tensor(tok[:, i, :], bank(6 + i % 2)[:, C:2 * C], o_row[:, :], ALU.add))
                    settle()
                    v.scalar_tensor_tensor(tok[:, i, :], bank(6 + i % 2)[:, 0:C], row_inv[:, i:i + 1],
                                           tok[:, i, :], ALU.mult, ALU.add).then_inc(t_done, 1)
                    w(t_done, NT, i + 1)
                    step(v.bn_stats(ln_bn[:, i, :], tok[:, i, :]))
                    settle_aggr()
                    step(v.bn_aggr(ln_mv[:, i, :], ln_bn[:, i, :]))
                    settle()
                    v.tensor_scalar(ln_eps[:, i:i + 1], ln_mv[:, i, 1:2], LN_EPS, None,
                                    ALU.add).then_inc(ln_in, 1)

                def norm1(i):
                    w(ln_out, NT, i + 1)
                    v.tensor_scalar(tn[:, i, :], tok[:, i, :], ln_mv[:, i, 0:1], ln_r[:, i:i + 1],
                                    ALU.subtract, ALU.mult).then_inc(tn_tok, 1)

                def lo_tn(h):
                    w(tn_hi, 2, h + 1)
                    c = slice(h * HALF, (h + 1) * HALF)
                    v.tensor_tensor(xs[1][:, :, c], bank(2 * h, count=2).rearrange("p (k t) -> p k t", k=KC),
                                    xs[0][:, :, c].bitcast(F32), ALU.subtract).then_inc(tn_lo, 1)

                project_lo(0)
                project_lo(1)
                if not first:
                    tail_add(b - 1, 0)
                    tail_add(b - 1, 1)
                project_lo(2)
                project_lo(3)
                project_lo(4)
                project_lo(5)
                max1(0)
                if not first:
                    tail_stats(b - 1, 0, 0)
                project_lo(6)
                project_lo(7)
                max1(1)
                if not first:
                    lo1(0)
                    tail_stats(b - 1, 0, 1)
                if first:
                    dve.wait_ge(w_hi, 5)
                    v.tensor_tensor(flat_l[:, 0:DIRECT, :], raw[:, 4:4 + DIRECT, :],
                                    flat_h[:, 0:DIRECT, :].bitcast(F32), ALU.subtract).then_inc(w_lo, 1)
                    for n in range(2, len(FOLDS)):
                        folded_lo(n)
                for i in range(NT):
                    if first or i > 0:
                        lo1(i)
                    if i + 2 < NT:
                        max1(i + 2)
                    if i >= 1:
                        out1(i - 1)
                    if i >= 2:
                        norm1(i - 2)
                    if not first and i in DVE_TAIL:
                        tail_stats(b - 1, *DVE_TAIL[i])
                    if i == 6:
                        lo_tn(0)
                norm1(NT - 2)
                out1(NT - 1)
                norm1(NT - 1)
                if not first:
                    w(xf_ready, 2, 0)
                    w(tok_out, 16, 0)

                n_u = 0
                for gi, (kind, o, n, m) in enumerate(R):
                    if kind != "v":
                        w(r_act, RG, gi + 1)
                    c = slice(n * HALF, (n + 1) * HALF)
                    if kind == "u":
                        dst = us[o % 2]
                        step(v.tensor_copy(dst[0][:, m, c], prob[:, n_u % 2, 0:HALF]))
                        settle()
                        v.tensor_tensor(dst[1][:, m, c], prob[:, n_u % 2, 0:HALF], dst[0][:, m, c].bitcast(F32),
                                        ALU.subtract).then_inc(r_dve, 1)
                        n_u += 1
                    elif kind == "p":
                        v.tensor_tensor((qs, ks)[o][1][:, m, c], bank(R_BANKS[gi % 4]),
                                        (qs, ks)[o][0][:, m, c].bitcast(F32), ALU.subtract).then_inc(r_dve, 1)
                    if gi == TN_AT - 1:
                        lo_tn(1)
                    if not last and gi in DVE_GN:
                        group_stats(b + 1, GN_BANK, DVE_GN[gi])
                    if not first and gi == GATE_READ:
                        gate_read(b - 1)
                settle()
                v.memset(spare[:, :], 0.0).then_inc(u_read, 1)

                def max2(i):
                    w(s2_mm, NT, i + 1)
                    v.tensor_reduce(neg_max[:, i:i + 1], bank(2 * (i % 2), count=2), AXX, ALU.max,
                                    negate=True).then_inc(s2_max, 1)

                def lo2(i):
                    w(p2_hi, NT, i + 1)
                    v.tensor_tensor(pr[1][:, i % 2, :], prob[:, i % 2, :], pr[0][:, i % 2, :].bitcast(F32),
                                    ALU.subtract).then_inc(p2_lo, 1)

                def values2(i):
                    w(p2_exp, NT, i + 1)
                    if i >= 2:
                        w(av2_mm, NT, i - 1)
                    step(v.reciprocal(row_inv[:, i:i + 1], row_sum[:, i:i + 1]))
                    settle()
                    step(v.tensor_scalar(vk[0][:, i % 2, :], v32[:, i, :], row_inv[:, i:i + 1], None, ALU.mult))
                    settle()
                    v.scalar_tensor_tensor(vk[1][:, i % 2, :], v32[:, i, :], row_inv[:, i:i + 1],
                                           vk[0][:, i % 2, :].bitcast(F32), ALU.mult,
                                           ALU.subtract).then_inc(v2_done, 1)

                max2(0)
                w(r_act, RG, RG - 3)
                values2(0)
                lo2(0)
                max2(1)
                for i in range(NT):
                    if i > 0:
                        w(r_act, RG, RG - 3 + i // 2)
                        values2(i)
                        lo2(i)
                    if i + 2 < NT:
                        max2(i + 2)
                    if not last:
                        if i in (1, 2):
                            group_apply(b + 1, i - 1)
                        if i in (3, 4):
                            group_lo(b + 1, i - 3)

            for part in range(3):
                group_stats(0, 3, part)
            dve.wait_ge(wa_in, A_IN)
            group_stats(0, 3, 3)
            for k in range(KC):
                group_apply(0, k)
            bias_columns()
            for k in range(KC):
                group_lo(0, k)
            folded_lo(0)
            dve.wait_ge(w_fold, 3)
            v.tensor_copy(s_bias[:, :], bank(6)[:, 0:KC]).then_inc(w_lo, 1)
            folded_lo(1)
            dve.wait_ge(w_fold, 4)
            v.tensor_tensor(o_row[:, :], bank(7, C), o_row[:, :], ALU.add).then_inc(w_lo, 1)
            image(0, True, False)
            before_turn[0], count[0] = before_turn[0] + count[0], 0
            start = before_turn[0]
            with dve.Fori(1, B - 1) as b:
                before_turn[0] = at(b - 1, OWN_IMAGE, start)
                image(b, False, False)
                assert count[0] == OWN_IMAGE, count[0]
            before_turn[0], count[0] = start + (B - 2) * OWN_IMAGE, 0
            image(B - 1, False, True)
            settle()

            def tops(tiles):
                for t in tiles:
                    step(v.max(top8[:, t, :], logits[:, t, :]))
                settle()
                for t in tiles:
                    step(v.max_index(top_i[:, t, :], top8[:, t, :], logits[:, t, :]))

            tail_add(B - 1, 0)
            tail_stats(B - 1, 0, 0)
            tail_add(B - 1, 1)
            tail_stats(B - 1, 0, 1)
            tail_stats(B - 1, 1, 0)
            tops(range(0, NT))
            tail_stats(B - 1, 1, 1)
            tops(range(NT, 2 * NT))
            for h in range(2):
                c = slice(4 * h, 4 * h + 4)
                dve.wait_ge(xf_norm, 2 * (B - 1) + h + 1)
                step(v.tensor_tensor(xf[:, c, :], xf[:, c, :],
                                     g_row[:, :].unsqueeze(1).to_broadcast((P, 4, C)), ALU.mult))
                settle()
                v.tensor_tensor(xf[:, c, :], xf[:, c, :],
                                b_row[:, :].unsqueeze(1).to_broadcast((P, 4, C)), ALU.add).then_inc(xf_ready, 1)
            tops(range(2 * NT, 3 * NT))
            gate_read(B - 1)
            settle()
            tops(range(3 * NT, 4 * NT))
            settle()
            dve.sem_inc(dve_end, 1)

            ends(dve, 1, (pe_end, act_end, sp_end, pool_end))
            W_AT = (0, 1, 3, 4)

            def w_piece(s, n, u, f):
                first = isinstance(s, int) and s < 2
                if f == 0:
                    dve.wait_ge(w1_in[n], at(u, 16, 16))
                    if not first:
                        dve.wait_ge(h_mm, at(s, FC, -FC))
                dve.wait_ge(ws_act, at(s, 8, f + 1))
                c = slice(f * 512, (f + 1) * 512)
                v.tensor_tensor(w1s[n][1][:, :, :].rearrange("p k f -> p (k f)")[:, c], w1r[:, n, c],
                                w1s[n][0][:, :, :].rearrange("p k f -> p (k f)")[:, c].bitcast(F32),
                                ALU.subtract).then_inc(ws_dve, 1)

            def first_pieces():
                for f in range(4):
                    w_piece(0, 0, 0, f)

            route(dve, v, first_pieces)

            def x_lo(s, n):
                dve.wait_ge(xt_hi, at(s, 1, 1))
                v.tensor_tensor(xt[n][1][:, :, :].rearrange("p k t -> p (k t)"), bank(6),
                                xt[n][0][:, :, :].rearrange("p k t -> p (k t)").bitcast(F32),
                                ALU.subtract).then_inc(xt_lo, 1)

            def y_bias(s, n, first):
                dve.wait_ge(y_mm, at(s, FC, FC))
                if not first:
                    dve.wait_ge(y_act, at(s, 1, 0))
                ins = v.tensor_tensor(y_b[:, :, :], bank(4 + n).rearrange("p (h c) -> p h c", h=SUB),
                                      b2t[:, n:n + 1, :].to_broadcast((P, SUB, C)), ALU.add)
                ins.then_inc(y_dve, 1)

            x_lo(0, 0)

            def steps(i, first):
                for n in range(2):
                    s = i * 2 + n
                    if first and n == 0:
                        chunks(i, n, first, True)
                    else:
                        with dve.If(dve.value_load(fresh[0:1, bass.ds(s + 1, 1)], min_val=0, max_val=1) == 1):
                            chunks(i, n, first, True)
                        with dve.Else():
                            dve.wait_ge(ws_dve, at(s, 4, 4))
                            dve.sem_inc(ws_dve, 4)
                            chunks(i, n, first, False)

            def chunks(i, n, first, split):
                s = i * 2 + n
                for f in range(FC):
                    gi = n * FC + f
                    dve.wait_ge(h_act, at(i, 2 * FC, gi + 1))
                    if not (first and n == 0):
                        dve.wait_ge(y_mm, at(i, 2 * FC, gi + 1 - FC))
                    v.tensor_copy(hs[0][:, f, :], h32[:, gi % 4, :]).then_inc(h_hi, 1)
                    dve.wait_ge(h_hi, at(i, 2 * FC, gi + 1))
                    v.tensor_tensor(hs[1][:, f, :], h32[:, gi % 4, :], hs[0][:, f, :].bitcast(F32),
                                    ALU.subtract).then_inc(h_lo, 1)
                    if f == 1 and not (first and n == 0):
                        y_bias(s - 1, 1 - n, first)
                    if split and f in W_AT:
                        w_piece(s + 1, 1 - n, (i if n == 0 else i + 1), W_AT.index(f))
                    if f == 2:
                        x_lo(s + 1, 1 - n)

            steps(0, True)
            with dve.Fori(1, PAIRS) as i:
                with is_live(dve, i):
                    steps(i, False)
            s_end = final_step(dve)
            y_bias(s_end, 1, False)
            dve.wait_ge(y_dve, at(s_end, 1, 1))
            dve.sem_inc(dve_end, 1)

            for gi in range(G):
                dve.wait_ge(o_mm, gi + 1)
                v.tensor_copy(cols_out[:, gi, 1, :], bank(2 * (gi % 2) + 1)).then_inc(o_dve, 1)

        @block.tensor
        def _(pe):
            t = nc.tensor

            def three(out, left, right, first=True, last=True, **more):
                for n, (l, r) in enumerate(PASSES):
                    ins = t.matmul(out, left[l], right[r], start=first and n == 0, stop=last and n == 2, **more)
                return ins

            def weight(slot, k, m):
                return [w[:, slot, k, m * P:(m + 1) * P] for w in (wh, wl)]

            def weight_row(slot, k):
                return [w[:, slot, k, :] for w in (wh, wl)]

            def fold(n, left, right):
                for m in range(KC):
                    for k in range(KC):
                        ins = t.matmul(bank(n)[:, m * C:(m + 1) * C], left[:, k * C + m * P:k * C + (m + 1) * P],
                                       right[:, k * C:(k + 1) * C], start=(k == 0), stop=(k == KC - 1))
                ins.then_inc(w_fold, 1)

            def group_average(b, at_bank, part):
                pe.wait_ge(gn_stat, at(b, 2, part + 1))
                if part == 0:
                    t.matmul(bank(at_bank)[:, 0:2 * KC], same_group[:, :],
                             gn_mv[:, :, :].rearrange("p k s -> p (k s)"),
                             start=True, stop=True).then_inc(gn_mm, 1)
                else:
                    t.matmul(bank(at_bank)[:, 8:8 + KC], same_group[:, :], gn_d2[:, :],
                             start=True, stop=True).then_inc(gn_mm, 1)

            def gate_turn(b):
                for h in range(2):
                    pe.wait_ge(xf_ready, at(b, 2, h + 1))
                    for k in range(KC):
                        for j in range(4):
                            ins = t.transpose(bank(2 * h + k)[:, j * P:(j + 1) * P],
                                              xf[:, 4 * h + j, k * P:(k + 1) * P], ident[:, :])
                    ins.then_inc(xf_mm, 1)

            def gate(b, tiles):
                for j in tiles:
                    if j % 4 == 0:
                        pe.wait_ge(xf_col, at(b, 2, j // 4 + 1))
                    for k in range(KC):
                        ins = t.matmul(bank(0)[:, j * E:(j + 1) * E], xfT[:, k, j * P:(j + 1) * P],
                                       gate_sb[:, k, :], start=(k == 0), stop=(k == KC - 1))
                if j == NT - 1:
                    ins.then_inc(g_mm, 1)

            def project(b, gi):
                out = bank(gi)
                if gi < 4:
                    n, m = gi // 2, gi % 2
                    for k in range(KC):
                        ins = three(out, weight(SQ, k, m),
                                    [a[:, k, n * HALF:(n + 1) * HALF] for a in xs], k == 0, k == KC - 1)
                else:
                    for h in range(2):
                        j = 2 * (gi - 4) + h
                        for k in range(KC):
                            ins = three(out[:, h * C:(h + 1) * C], [a[:, k, j * P:(j + 1) * P] for a in xs],
                                        weight_row(VO, k), k == 0, k == KC - 1)
                ins.then_inc(pj_mm, 1)

            def image(b, first, last):
                def w(s, per, n):
                    pe.wait_ge(s, at(b, per, n))

                def scores(i, rows_of, cols_of, signal_):
                    for n in range(NH):
                        for k in range(KC):
                            ins = three(bank(2 * (i % 2) + n), [a[:, k, i * P:(i + 1) * P] for a in rows_of],
                                        [a[:, k, n * HALF:(n + 1) * HALF] for a in cols_of], k == 0, k == KC - 1)
                    ins.then_inc(signal_, 1)

                def turn1(i):
                    w(p_exp, NT, i + 1)
                    if i >= 1:
                        w(pt_lo, NT, i)
                    for j in range(NT):
                        ins = t.transpose(bank(4, count=2)[:, j * P:(j + 1) * P],
                                          prob[:, i % 2, j * P:(j + 1) * P], ident[:, :])
                    ins.then_inc(pt_mm, 1)

                def mix1(i):
                    if i >= 2:
                        w(t_done, NT, i - 1)
                    for k in range(KC):
                        t.transpose(bank(6 + i % 2)[:, C + k * P:C + (k + 1) * P], xn[:, k, i * P:(i + 1) * P],
                                    ident[:, :])
                    w(pt_lo, NT, i + 1)
                    for j in range(NT):
                        ins = three(bank(6 + i % 2)[:, 0:C], [a[:, i % 2, j * P:(j + 1) * P] for a in pr],
                                    [a[:, j, :] for a in vs], j == 0, j == NT - 1)
                    ins.then_inc(av_mm, 1)

                def turn_tn(h):
                    w(tn_tok, NT, 4 * h + 4)
                    for k in range(KC):
                        for j in range(4):
                            ins = t.transpose(bank(2 * h + k)[:, j * P:(j + 1) * P],
                                              tn[:, 4 * h + j, k * P:(k + 1) * P], ident[:, :])
                    ins.then_inc(tn_mm, 1)

                if first:
                    w(xn_lo, KC, KC)
                    project(b, 0)
                    project(b, 1)
                else:
                    pe.wait_ge(p2_exp, at(b - 1, NT, NT))
                project(b, 2)
                project(b, 3)
                if first:
                    pe.wait_ge(w_lo, 4)
                else:
                    pe.wait_ge(added2, at(b - 1, 2, 2))
                project(b, 4)
                project(b, 5)
                w(pj_lo, PJ, 4)
                scores(0, qs, xs, s_mm)
                project(b, 6)
                project(b, 7)
                scores(1, qs, xs, s_mm)
                w(pj_lo, PJ, 6)
                if first:
                    pe.wait_ge(wb_in, B_IN)
                    fold(4, raw[:, 12, :], raw[:, 13, :])
                    fold(5, raw[:, 9, :], raw[:, 7, :])
                    w(pj_lo, PJ, 8)
                    fold(6, raw[:, 10, :], raw[:, 8, :])
                    pe.wait_ge(vo_ready, 1)
                    fold(7, raw[:, 11, :], raw_vo[:, :])
                    pe.wait_ge(w_lo, 7)
                for i in range(NT):
                    turn1(i)
                    if i + 2 < NT:
                        scores(i + 2, qs, xs, s_mm)
                    if i == 1:
                        w(pj_lo, PJ, PJ)
                        if first:
                            pe.wait_ge(w_lo, 9)
                    if i >= 1:
                        mix1(i - 1)
                    if i == NT - 2:
                        turn_tn(0)
                mix1(NT - 1)

                for gi, (kind, o, n, m) in enumerate(R):
                    if gi == TN_AT:
                        turn_tn(1)
                    if not first and gi == GATE_AT:
                        gate_turn(b - 1)
                    if not first and gi in GATE_MM:
                        gate(b - 1, GATE_MM[gi])
                    if not last and gi in PE_GN:
                        if not first:
                            pe.wait_ge(xf_col, at(b - 1, 2, 2))
                        group_average(b + 1, GN_BANK, PE_GN[gi])
                    if gi == 0:
                        w(tn_lo, 2, 1)
                    if gi in (2, 3):
                        w(t_done, NT, NT - 3 + gi)
                    if gi == H1_AT:
                        w(tn_lo, 2, 2)
                    if gi >= 4:
                        w(r_act, RG, gi - 3)
                        if R[gi - 4][0] == "p":
                            w(r_dve, RD, R_DVE[gi - 4])
                    if kind != "u" and R[gi - 1][:2] != R[gi][:2]:
                        w(r_dve, RD, R_DVE[max(j for j in range(gi) if R[j][:2] == ("u", o))])
                    if gi == RG - 2:
                        w(r_dve, RD, RD)
                        w(u_read, 1, 1)
                        scores(0, ks, qs, s2_mm)
                    out = bank(R_BANKS[gi % 4])
                    if kind == "u":
                        for k in range(KC):
                            ins = three(out, weight(Q1 + o, k, m),
                                        [a[:, k, n * HALF:(n + 1) * HALF] for a in xs], k == 0, k == KC - 1)
                    elif kind == "p":
                        for k in range(KC):
                            three(out, weight(AQ + o, k, m),
                                  [a[:, k, n * HALF:(n + 1) * HALF] for a in xs], k == 0, False)
                        for k in range(KC):
                            ins = three(out, weight(QA + o, k, m),
                                        [a[:, k, n * HALF:(n + 1) * HALF] for a in us[o % 2]], False, k == KC - 1)
                    else:
                        for h in range(2):
                            j = 2 * n + h
                            for k in range(KC):
                                three(out[:, h * C:(h + 1) * C], [a[:, k, j * P:(j + 1) * P] for a in xs],
                                      weight_row(VA, k), k == 0, False)
                            for k in range(KC):
                                ins = three(out[:, h * C:(h + 1) * C], [a[:, k, j * P:(j + 1) * P] for a in us[0]],
                                            weight_row(VB, k), False, k == KC - 1)
                    ins.then_inc(r_mm, 1)

                def mix2(i):
                    w(p2_lo, NT, i + 1)
                    w(v2_done, NT, i + 1)
                    if i == 0:
                        w(r_act, RG, RG)
                        w(r_dve, RD, RD)
                    for j in range(NT):
                        ins = three(bank(4 + j // 2)[:, j % 2 * C:(j % 2 + 1) * C],
                                    [a[:, i % 2, j * P:(j + 1) * P] for a in pr],
                                    [a[:, i % 2, :] for a in vk], i == 0 and j % 2 == 0, i == NT - 1,
                                    skip_group_check=True)
                    ins.then_inc(av2_mm, 1)

                scores(1, ks, qs, s2_mm)
                for i in range(NT):
                    if i + 2 < NT:
                        w(p2_exp, NT, i + 1)
                        scores(i + 2, ks, qs, s2_mm)
                    if i >= NT - 2 and not last:
                        if i == NT - 2:
                            w(p2_exp, NT, NT - 1)
                            pe.wait_ge(xn_lo, at(b + 1, KC, KC))
                        project(b + 1, i - (NT - 2))
                    mix2(i)

            pe.wait_ge(c_made, CONSTANTS)
            group_average(0, 3, 0)
            group_average(0, 3, 1)
            pe.wait_ge(w_hi, 1)
            fold(4, raw[:, 0, :], raw[:, 1, :])
            fold(5, raw[:, 2, :], raw[:, 3, :])
            pe.wait_ge(w_hi, 2)
            for m in range(KC):
                for k in range(KC):
                    ins = t.matmul(bank(6)[:, m:m + 1], raw[:, 1, k * C + m * P:k * C + (m + 1) * P],
                                   q_bias[:, k:k + 1], start=(k == 0), stop=(k == KC - 1))
            ins.then_inc(w_fold, 1)
            pe.wait_ge(vb_ready, KC)
            for k in range(KC):
                ins = t.matmul(bank(7, C), vb_wide[:, k, :], raw[:, 3, k * C:(k + 1) * C],
                               start=(k == 0), stop=(k == KC - 1))
            ins.then_inc(w_fold, 1)
            pe.wait_ge(w_lo, 1)
            image(0, True, False)
            with pe.Fori(1, B - 1) as b:
                image(b, False, False)
            image(B - 1, False, True)
            pe.wait_ge(p2_exp, B * NT)
            gate_turn(B - 1)
            gate(B - 1, range(NT))
            pe.wait_ge(g_mm, B)
            pe.sem_inc(pe_end, 1)

            pe.wait_ge(top_done, 3)
            pe.wait_ge(num_done, 3)
            flat = either[:, :, :].rearrange("p t e -> p (t e)")
            t.matmul(bank(0, TILES * E), before[:, :], flat, start=True, stop=True)
            t.matmul(bank(1, TILES * E), ones[:, :], flat, start=True, stop=True).then_inc(rank_mm, 1)
            for j in range(2 * TILES):
                if j % PICK == 0:
                    c = j // PICK
                    pe.wait_ge(pick_rows, c + 1)
                    pe.wait_ge(pick_n, c + 1)
                    pe.wait_ge((pick_w, pick_w_act)[c % 2], c // 2 + 1)
                t.matmul(bank(2, 2 * COLS), pick_lo[:, j, :],
                         pick_hi[:, j, :, :].rearrange("p a c -> p (a c)"),
                         start=(j == 0), stop=(j == 2 * TILES - 1)).then_inc(pick_mm, 1)

            pe.wait_ge(tables, 4)

            def x_turn(s, n, u):
                pe.wait_ge(g_in[n], at(u, SUB * 16, SUB * 16))
                if not (isinstance(s, int) and s == 0):
                    pe.wait_ge(xt_lo, at(s, 1, 0))
                for k in range(KC):
                    for h in range(SUB):
                        ins = t.transpose(bank(6)[:, k * STEP + h * P:k * STEP + (h + 1) * P],
                                          xg[:, n, h, k * P:(k + 1) * P], ident[:, :])
                ins.then_inc(xt_mm, 1)

            def first_product(i, s, n, f, new):
                gi = n * FC + f
                if f == 0:
                    pe.wait_ge(xt_lo, at(s, 1, 1))
                    pe.wait_ge(ws_dve, at(s, 4, 4))
                if not (new and gi < 4):
                    pe.wait_ge(h_act, at(i, 2 * FC, gi - 3))
                for k in range(KC):
                    ins = three(bank(gi % 4, STEP), [a[:, k, f * P:(f + 1) * P] for a in w1s[n % 2]],
                                [a[:, k, :] for a in xt[n % 2]], k == 0, k == KC - 1)
                ins.then_inc(h_mm, 1)

            def second_product(i, s, n, f, new):
                gi = n * FC + f
                pe.wait_ge(h_lo, at(i, 2 * FC, gi + 1))
                if f % 2 == 0:
                    pe.wait_ge(ws_act, at(s, 8, 5 + f // 2))
                    pe.wait_ge(ws_pool, at(s, 4, 1 + f // 2))
                if f == 0:
                    if not new:
                        pe.wait_ge(y_dve, at(s, 1, -1))
                for h in range(SUB):
                    ins = three(bank(4 + n)[:, h * C:(h + 1) * C], [a[:, f, h * P:(h + 1) * P] for a in hs],
                                [a[:, f, :] for a in w2s[n]], f == 0 and h == 0, f == FC - 1,
                                skip_group_check=True)
                ins.then_inc(y_mm, 1)

            AHEAD = 3
            x_turn(0, 0, 0)
            for f in range(AHEAD):
                first_product(0, 0, 0, f, True)

            def steps(i, first):
                for gi in range(2 * FC):
                    n, f = gi // FC, gi % FC
                    s = i * 2 + n
                    if f == 1:
                        x_turn(s + 1, 1 - n, (i if n == 0 else i + 1))
                    ahead = gi + AHEAD
                    na, fa = ahead // FC, ahead % FC
                    first_product(i, i * 2 + na, na, fa, first)
                    second_product(i, s, n, f, first)

            steps(0, True)
            with pe.Fori(1, PAIRS) as i:
                with is_live(pe, i):
                    steps(i, False)
            pe.wait_ge(y_mm, at(final_step(pe), FC, FC))
            pe.sem_inc(pe_end, 1)

            for gi in range(G):
                pe.wait_ge(r_in[gi], 16)
                if gi == 0:
                    ends(pe, 2, (act_end, dve_end))
                if gi >= 2:
                    pe.wait_ge(o_act, gi - 1)
                    pe.wait_ge(o_dve, gi - 1)
                for k in range(KC):
                    for j in range(4):
                        ins = t.transpose(bank(2 * (gi % 2) + k)[:, j * P:(j + 1) * P],
                                          rows[:, gi, j, k * P:(k + 1) * P], ident[:, :])
                ins.then_inc(o_mm, 1)


CONSTANTS = 8
OWN_IMAGE = 102


def kernel(**inputs):
    import numpy as np
    import concourse.bacc as bacc
    from concourse.bass_utils import run_bass_kernel_spmd

    a = {k: np.asarray(v) for k, v in inputs.items()}
    x = a["x"]
    B, C, H, W = x.shape

    def chunks(v):
        return v.reshape(-1, P).T

    qkv_w, qkv_b = a["L0_conv_qkv_w"], a["L0_conv_qkv_b"]
    E, F = a["L1_ffn_b1"].shape
    args = {
        "x": x.reshape(B, C, H * W),
        "q_w": qkv_w[0:C], "k_w": qkv_w[C:2 * C], "v_w": qkv_w[2 * C:3 * C], "oT": a["L0_conv_out_w"].T,
        "q_b": chunks(qkv_b[0:C]), "v_b": chunks(qkv_b[2 * C:3 * C]),
        "out_b": a["L0_conv_out_b"].reshape(1, C),
        "gn": np.concatenate([chunks(a["L0_conv_gn_weight"]), chunks(a["L0_conv_gn_bias"])], axis=1),
        "W1": np.stack([a[f"L1_attn_{n}W1"] for n in "qkv"]),
        "W2T": np.stack([a[f"L1_attn_{n}W2"].T for n in "qkv"]),
        "a_qk": np.stack([a["L1_attn_aWq"], a["L1_attn_aWk"]]),
        "a_vT": a["L1_attn_aWv"].T, "Wout": a["L1_attn_Wout"],
        "gate_w": a["L1_ffn_gate_w"], "w1": a["L1_ffn_w1"],
        "b1": a["L1_ffn_b1"].reshape(E, F // P, P).transpose(0, 2, 1),
        "w2": a["L1_ffn_w2"], "b2": a["L1_ffn_b2"],
        "ln_g": a["L1_ffn_ln_g"].reshape(1, C), "ln_b": a["L1_ffn_ln_b"].reshape(1, C),
    }
    nc = bacc.Bacc("TRN2", target_bir_lowering=False, num_devices=1)
    arrays, aps = {}, {}
    for name, v in args.items():
        v = np.ascontiguousarray(v)
        arrays[f"in_{name}"] = v
        aps[name] = nc.dram_tensor(f"in_{name}", v.shape, mybir.dt.from_np(v.dtype), kind="ExternalInput").ap()
    aps["out"] = nc.dram_tensor("out_tokens", (B, C, H * W), F32, kind="ExternalOutput").ap()
    hybrid_block_kernel(nc, **aps)
    r = run_bass_kernel_spmd(nc, [arrays], core_ids=[0])
    return r.results[0]["out_tokens"].reshape(B, C, H, W)
```
